# Optimizing a Trainium2 kernel written in Bass

```python
import numpy as np
import jax
import jax.numpy as jnp

def _softmax(x, axis=-1):
    return jax.nn.softmax(x, axis=axis)

def _gelu(x):
    return jax.nn.gelu(x, approximate=True)

def _silu(x):
    return jax.nn.silu(x)

def _sigmoid(x):
    return jax.nn.sigmoid(x)

def _layernorm(x, axis=-1, eps=1e-05):
    m = jnp.mean(x, axis=axis, keepdims=True)
    v = jnp.var(x, axis=axis, keepdims=True)
    return (x - m) / jnp.sqrt(v + eps)

def _scatter_add(tgt, idx, src, axis=0):
    return tgt.at[idx].add(src)

def _segment_sum(src, seg, n):
    return jax.ops.segment_sum(src, seg, n)
kernel_name = 'mk_seq_preln_d1_jaxref_r4_b359d8'

def setup_inputs(seed: int=0):
    np.random.seed(seed)
    _w = jnp.asarray

    def _L0_attn_setup():
        import jax, jax.numpy as jnp
        import numpy as np
        import math
        N_HEAD = 16
        ROPE_BASE = 10000.0

        def _rope_as_in_source(x):
            B, H, T, hd = x.shape
            theta = 1.0 / ROPE_BASE ** (jnp.arange(0, hd, 2, dtype=jnp.float32) / hd)
            ang = jnp.arange(H, dtype=jnp.float32)[:, None] * theta[None, :]
            cos = jnp.cos(ang)[None, :, None, :]
            sin = jnp.sin(ang)[None, :, None, :]
            xr = x.reshape(B, H, T, hd // 2, 2)
            out = jnp.stack([xr[..., 0] * cos - xr[..., 1] * sin, xr[..., 1] * cos + xr[..., 0] * sin], axis=-1)
            return out.reshape(B, H, T, hd)
        key = jax.random.key(seed)
        ks = jax.random.split(key, 5)
        B, T, C = (2, 512, 256)
        s = 0.02
        return {'x': jax.random.normal(ks[0], (B, T, C), dtype=jnp.float32), 'W_attn': jax.random.normal(ks[1], (C, 3 * C), dtype=jnp.float32) * s, 'b_attn': jnp.zeros((3 * C,), dtype=jnp.float32), 'W_proj': jax.random.normal(ks[2], (C, C), dtype=jnp.float32) * s, 'b_proj': jnp.zeros((C,), dtype=jnp.float32)}
    _L0_attn_in = _L0_attn_setup()

    def _L0_ffn_setup():
        import jax, jax.numpy as jnp
        import numpy as np
        EPS = 1e-05
        LN_EPS = 1e-05
        NUM_EXPERTS = 8
        TOP_K = 2
        HIDDEN = 256
        INTER = 512

        def _swiglu(x, wg, wu, wd):
            return jax.nn.silu(x @ wg) * (x @ wu) @ wd
        key = jax.random.key(seed)
        ks = jax.random.split(key, 10)
        B, S, H, I, E = (8, 1024, HIDDEN, INTER, NUM_EXPERTS)
        std_h = 1.0 / np.sqrt(H)
        std_i = 1.0 / np.sqrt(I)
        return {'x': jax.random.normal(ks[0], (B, S, H), dtype=jnp.float32), 'ln_scale': jnp.ones((H,), dtype=jnp.float32), 'ln_bias': jnp.zeros((H,), dtype=jnp.float32), 'gate_w': jax.random.normal(ks[1], (E, H), dtype=jnp.float32) * 0.01, 'Wg': jax.random.normal(ks[2], (E, H, I), dtype=jnp.float32) * std_h, 'Wu': jax.random.normal(ks[3], (E, H, I), dtype=jnp.float32) * std_h, 'Wd': jax.random.normal(ks[4], (E, I, H), dtype=jnp.float32) * std_i, 'sWg': jax.random.normal(ks[5], (H, I), dtype=jnp.float32) * std_h, 'sWu': jax.random.normal(ks[6], (H, I), dtype=jnp.float32) * std_h, 'sWd': jax.random.normal(ks[7], (I, H), dtype=jnp.float32) * std_i}
    _L0_ffn_in = _L0_ffn_setup()
    _d = {'L0_attn_x': _L0_attn_in['x'], 'L0_attn_W_attn': _L0_attn_in['W_attn'], 'L0_attn_b_attn': _L0_attn_in['b_attn'], 'L0_attn_W_proj': _L0_attn_in['W_proj'], 'L0_attn_b_proj': _L0_attn_in['b_proj'], 'L0_ffn_ln_scale': _L0_ffn_in['ln_scale'], 'L0_ffn_ln_bias': _L0_ffn_in['ln_bias'], 'L0_ffn_gate_w': _L0_ffn_in['gate_w'], 'L0_ffn_Wg': _L0_ffn_in['Wg'], 'L0_ffn_Wu': _L0_ffn_in['Wu'], 'L0_ffn_Wd': _L0_ffn_in['Wd'], 'L0_ffn_sWg': _L0_ffn_in['sWg'], 'L0_ffn_sWu': _L0_ffn_in['sWu'], 'L0_ffn_sWd': _L0_ffn_in['sWd']}
    _x0 = _d['L0_attn_x']
    _d['L0_attn_x'] = jax.random.normal(jax.random.fold_in(jax.random.key(seed), 1), (16, 512, 256), dtype=_x0.dtype)
    del _x0
    return _d

def reference(L0_attn_x, L0_attn_W_attn, L0_attn_b_attn, L0_attn_W_proj, L0_attn_b_proj, L0_ffn_ln_scale, L0_ffn_ln_bias, L0_ffn_gate_w, L0_ffn_Wg, L0_ffn_Wu, L0_ffn_Wd, L0_ffn_sWg, L0_ffn_sWu, L0_ffn_sWd):

    def _L0_attn_ref(x, W_attn, b_attn, W_proj, b_proj):
        import jax, jax.numpy as jnp
        import numpy as np
        import math
        N_HEAD = 16
        ROPE_BASE = 10000.0

        def _rope_as_in_source(x):
            B, H, T, hd = x.shape
            theta = 1.0 / ROPE_BASE ** (jnp.arange(0, hd, 2, dtype=jnp.float32) / hd)
            ang = jnp.arange(H, dtype=jnp.float32)[:, None] * theta[None, :]
            cos = jnp.cos(ang)[None, :, None, :]
            sin = jnp.sin(ang)[None, :, None, :]
            xr = x.reshape(B, H, T, hd // 2, 2)
            out = jnp.stack([xr[..., 0] * cos - xr[..., 1] * sin, xr[..., 1] * cos + xr[..., 0] * sin], axis=-1)
            return out.reshape(B, H, T, hd)
        B, T, C = x.shape
        H = N_HEAD
        hd = C // H
        qkv = x @ W_attn + b_attn
        q, k, v = jnp.split(qkv, 3, axis=2)
        q = q.reshape(B, T, H, hd).transpose(0, 2, 1, 3)
        k = k.reshape(B, T, H, hd).transpose(0, 2, 1, 3)
        v = v.reshape(B, T, H, hd).transpose(0, 2, 1, 3)
        q = _rope_as_in_source(q)
        k = _rope_as_in_source(k)
        att = jnp.einsum('bhqd,bhkd->bhqk', q, k) * (1.0 / math.sqrt(hd))
        causal = jnp.tril(jnp.ones((T, T), dtype=bool))
        att = jnp.where(causal[None, None, :, :], att, -jnp.inf)
        att = jax.nn.softmax(att, axis=-1)
        y = jnp.einsum('bhqk,bhkd->bhqd', att, v)
        y = y.transpose(0, 2, 1, 3).reshape(B, T, C)
        return y @ W_proj + b_proj

    def _L0_ffn_ref(x, ln_scale, ln_bias, gate_w, Wg, Wu, Wd, sWg, sWu, sWd):
        import jax, jax.numpy as jnp
        import numpy as np
        EPS = 1e-05
        LN_EPS = 1e-05
        NUM_EXPERTS = 8
        TOP_K = 2
        HIDDEN = 256
        INTER = 512

        def _swiglu(x, wg, wu, wd):
            return jax.nn.silu(x @ wg) * (x @ wu) @ wd
        B, S, H = x.shape
        xf = x.reshape(-1, H)
        mu = jnp.mean(xf, axis=-1, keepdims=True)
        var = jnp.var(xf, axis=-1, keepdims=True)
        xn = (xf - mu) * jax.lax.rsqrt(var + LN_EPS) * ln_scale + ln_bias
        logits = xn @ gate_w.T
        probs = jax.nn.softmax(logits, axis=-1)
        tk_probs, tk_idx = jax.lax.top_k(probs, TOP_K)
        tk_probs = tk_probs / (jnp.sum(tk_probs, axis=-1, keepdims=True) + EPS)
        onehot = tk_idx[..., None] == jnp.arange(NUM_EXPERTS)[None, None, :]
        w = jnp.sum(tk_probs[..., None] * onehot.astype(tk_probs.dtype), axis=1)
        out = _swiglu(xf, sWg, sWu, sWd)
        for e in range(NUM_EXPERTS):
            out = out + w[:, e:e + 1] * _swiglu(xf, Wg[e], Wu[e], Wd[e])
        return out.reshape(B, S, H)
    x = L0_attn_x
    x = x + _L0_attn_ref(_layernorm(x, axis=-1), L0_attn_W_attn, L0_attn_b_attn, L0_attn_W_proj, L0_attn_b_proj)
    x = x + _L0_ffn_ref(_layernorm(x, axis=-1), L0_ffn_ln_scale, L0_ffn_ln_bias, L0_ffn_gate_w, L0_ffn_Wg, L0_ffn_Wu, L0_ffn_Wd, L0_ffn_sWg, L0_ffn_sWu, L0_ffn_sWd)
    return x

_drawn_inputs = setup_inputs


def setup_inputs(seed=0):
    import zlib

    import numpy as np

    out = dict(_drawn_inputs(seed))
    spreads = {'L0_attn_b_attn': (0.0, 0.1),
     'L0_attn_b_proj': (0.0, 0.1),
     'L0_ffn_ln_scale': (1.0, 0.2),
     'L0_ffn_ln_bias': (0.0, 0.1)}
    factors = {}
    for name, (base, spread) in spreads.items():
        noise = np.random.default_rng([zlib.crc32(name.encode()), seed]).standard_normal(out[name].shape)
        drawn = base * np.exp(spread * noise) if base else spread * noise
        out[name] = jnp.asarray(drawn.astype(out[name].dtype))
    for name, factor in factors.items():
        out[name] = (out[name] * factor).astype(out[name].dtype)
    return out
```

```python
from contextlib import ExitStack

import numpy as np
import concourse.bass as bass
from concourse import mybir

F32 = mybir.dt.float32
F32R = mybir.dt.float32r
F16 = mybir.dt.float16
BF16 = mybir.dt.bfloat16
I32 = mybir.dt.int32
ALU = mybir.AluOpType
ACT = mybir.ActivationFunctionType
AX_X = mybir.AxisListType.X
RMAX = bass.bass_isa.ReduceOp.max

P = 128
EPS = 1e-5
X_SCALE = 2048.0
SHIFT_UNIT = 32768.0
MASKED = -1e30
DVE_LINKS = 22


class Count:

    def __init__(self, sem):
        self.sem, self.base, self.n = sem, 0, 0

    def link(self, engine, instruction):
        instruction.then_inc(self.sem, 1)
        self.n += 1
        engine.wait_ge(self.sem, self.base + self.n)


def some(value):
    return not isinstance(value, int) or value > 0


def build(nc, x, w_attn, b_attn, w_proj, b_proj, ln_scale, ln_bias, gate_w, Wg, Wu, Wd, sWg, sWu, sWd, rope, out):
    NTOK, C = x.shape
    T = 512
    NB = NTOK // T
    NT = T // P
    H = 16
    HD = C // H
    GH = 4
    NG = H // GH
    UN = 10
    LOADS = 18 * 16

    E = Wg.shape[0]
    HID = Wg.shape[2]
    TILES = NTOK // P
    BLOCKS = (2 * NTOK + E * (P - 1)) // P
    BLOCKS += BLOCKS % 2
    CC, HC = C // P, HID // P
    WG, WU, WD = 0, 2 * CC * HID, 4 * CC * HID
    SLOT = 4 * CC * HID + 2 * HC * C

    def scratch(name, shape, dt):
        return nc.dram_tensor(name, shape, dt, kind="Internal").ap()

    x1_d = scratch("x1_d", (NTOK, C), F32)
    xhl_d = scratch("xhl_d", (NTOK, 2 * C), F16)
    sh_d = scratch("sh_d", (NTOK, C), F32)
    y_d = scratch("y_d", (BLOCKS * P, C), F32)
    tok_d = scratch("tok_d", (P * BLOCKS, 1), I32)

    xv = x.rearrange("(b t p) c -> b p t c", t=NT, p=P)
    x1v = x1_d.rearrange("(b j t p) c -> b j p t c", j=2, t=2, p=P)
    xhlv = xhl_d.rearrange("(b j t p) c -> b j p t c", j=2, t=2, p=P)

    with ExitStack() as ctx:
        def sb(name, shape, dt):
            return ctx.enter_context(nc.sbuf_tensor(name, shape, dt))

        ctx_a = ctx.enter_context(ExitStack())

        def sb_a(name, shape, dt):
            return ctx_a.enter_context(nc.sbuf_tensor(name, shape, dt))

        def sem(name):
            return ctx.enter_context(nc.semaphore(name))

        bank = [ctx.enter_context(nc.psum_tensor(f"bank{i}", [P, 512], F32)) for i in range(8)]
        ps_s, ps_t, ps_o, ps_q, ps_m, ps_y = bank[0:2], bank[2:4], bank[4], bank[5], bank[6], bank[7]

        ident_h = sb("ident_h", [P, P], F16)
        wsh = sb("wsh", [P, SLOT], F16)
        var_all = sb("var_all", [P, TILES], F32)
        early = sb("early", [P, SLOT // 2 + 3 * 256], F32)
        ident = sb("ident", [P, P], F32)
        ident_b = sb("ident_b", [P, P], BF16)
        mask = sb("mask", [P, P], BF16)
        one = sb("one", [P, 1], F32)
        neghalf = sb("neghalf", [P, 4], F32)
        cs = sb_a("cs", [P, 2, 256], F32)
        bvb = sb_a("bvb", [P, C], F32)
        bpb = sb_a("bpb", [P, C], F32)
        wa = early[:, 0:9 * C].rearrange("p (k n) -> p k n", k=3)
        shared_raw = early[:, 0:SLOT // 2]
        wah = sb_a("wah", [P, 2, 3 * C], F32R)
        wal = sb_a("wal", [P, 2, 3 * C], F32R)
        wp = sb_a("wp", [P, 2, C], F32)
        bcol = sb_a("bcol", [P, 4], F32)
        qk_max = sb_a("qk_max", [P, 2], F32)
        qk_top = sb_a("qk_top", [P, 2], F32)
        qk_inv = sb_a("qk_inv", [P, 2], F32)
        qk_scale = sb_a("qk_scale", [P, 2], F32)
        exp_scale = sb_a("exp_scale", [P, 1], F32)
        rope_t = early[:, 9 * C:15 * C].rearrange("p (a k n) -> p a k n", a=2, k=3)
        x_in = sb_a("x_in", [P, 2, NT, C], F32)
        xn = sb_a("xn", [P, NT, C], F32)
        st6 = sb_a("st6", [P, NT, 6], F32)
        mv = sb_a("mv", [P, NT, 2], F32)
        rstd = sb_a("rstd", [P, NT], F32)
        xh = sb_a("xh", [P, 2, T], F32R)
        xl = sb_a("xl", [P, 2, T], F32R)
        qkh = sb_a("qkh", [P, 4, T], F16)
        qkl = sb_a("qkl", [P, 4, T], F16)
        q_op = sb_a("q_op", [P, H // 2, T], F16)
        k_op = sb_a("k_op", [P, H, T], F16)
        v_op = sb_a("v_op", [P, 2, NT, H, 32], F32)
        mx = sb_a("mx", [P, 2, NT, GH], F32)
        prob = sb_a("prob", [P, 2, UN, 512], F32)
        o_t = sb_a("o_t", [P, 2, NG, T], F32)
        rec = sb_a("rec", [P, 2, H], F32)
        y = sb_a("y", [P, 2, C], F32)
        y_t = sb_a("y_t", [P, 2, 2, P], F32)
        xres = sb_a("xres", [P, NT, C], F32)
        x1 = sb_a("x1", [P, 2, 2, C], F32)
        st6b = sb_a("st6b", [P, 2, 6], F32)
        mvb = sb_a("mvb", [P, 2, 2], F32)
        rstdb = sb_a("rstdb", [P, 2], F32)
        xf = sb_a("xf", [P, 2, C], F32)
        xhl = sb_a("xhl", [P, 2, 2, 2, C], F16)

        ctx_a.close()
        wbuf = sb("wbuf", [P, (E + 1) * SLOT], F16)
        wraw = wbuf[:].bitcast(F32).rearrange("p (s n) -> p s n", s=E + 1)
        xrow = sb("xrow", [P, 2, 2 * C], F16)
        xt = sb("xt", [P, 2, 2 * CC, P], F16)
        sg = sb("sg", [P, 2, HID], F32)
        hb = sb("hb", [P, HID], F32)
        hth = sb("hth", [P, HC, P], F16)
        htl = sb("htl", [P, HC, P], F16)
        ysb = sb("ysb", [P, 2, C], F32)
        x1t = sb("x1t", [P, 2, C], F32)
        shc = sb("shc", [P, 2, C], F32)
        y1 = sb("y1", [P, 2, C], F32)
        y2 = sb("y2", [P, 2, C], F32)
        acc = sb("acc", [P, 2, C], F32)
        fin = sb("fin", [P, 2, C], F32)
        top = sb("top", [P, 3, 4], F32)
        inv = sb("inv", [P, 3, 4], F32)
        wsc = sb("wsc", [P, 3, 4], F32)
        run3 = sb("run3", [P, 3], F32)
        silu_s = sb("silu_s", [P, 2], F32)
        h_s = sb("h_s", [P, 2], F32)
        y_s = sb("y_s", [P, 2], F32)
        lg_s = sb("lg_s", [P, 1], F32)
        gate_t = sb("gate_t", [P, CC, E], F32)
        gs_t = sb("gs_t", [P, 2 * CC, E], F32)
        gate_hl = sb("gate_hl", [P, 2, CC, E], F16)
        lns = sb("lns", [P, 2, CC], F32)
        ones_f = sb("ones_f", [P, P], F32)
        ones_b = sb("ones_b", [P, P], BF16)
        before_b = sb("before_b", [P, P], BF16)
        sgb = sb("sgb", [P, 2, E], F32)
        rvar = sb("rvar", [P, 2, TILES], F32)
        rhalf = sb("rhalf", [P, TILES], F32)
        lg = sb("lg", [P, TILES, E], F32)
        lg2 = sb("lg2", [P, TILES, E], F32)
        tmp = sb("tmp", [P, TILES, E], F32)
        oh = sb("oh", [P, 2, TILES, E], F32)
        sel = sb("sel", [P, TILES, E], BF16)
        m12 = sb("m12", [P, 4, TILES], F32)
        rw = sb("rw", [P, 6, TILES], F32)
        iota_e = sb("iota_e", [P, E], F32)
        iota_j = sb("iota_j", [P, TILES], F32)
        iota_b = sb("iota_b", [1, BLOCKS], F32)
        incl = sb("incl", [P, E, TILES], F32)
        zeros = sb("zeros", [P, TILES], F32)
        nblk = sb("nblk", [P, 4, E], F32)
        slot_f = sb("slot_f", [P, 2, TILES], F32)
        slot_i = sb("slot_i", [P, 2, TILES], I32)
        row_i = sb("row_i", [P, 3, 2, TILES], I32)
        dest_i = sb("dest_i", [P, 2, TILES], I32)
        tok_i = sb("tok_i", [P, TILES], I32)
        tok_rows = sb("tok_rows", [P, BLOCKS], I32)
        zero_i = sb("zero_i", [P, BLOCKS], I32)
        blk_cmp = sb("blk_cmp", [1, BLOCKS, E - 1], F32)
        blk_f = sb("blk_f", [1, BLOCKS], F32)
        blk_off = sb("blk_off", [1, BLOCKS], I32)
        sc_col = sb("sc_col", [P, 2, 3], I32)
        ga_col = sb("ga_col", [P, 2, 1], I32)
        co_col = sb("co_col", [P, 2, 2], I32)
        ps_g, ps_u, ps_h, ps_x, ps_z, ps_l = bank[0], bank[1], bank[2], bank[3], bank[4], bank[5]
        ps_x16 = ps_x[:].bitcast(F16)
        ps_r = bank[6:8]

        names = ("const_in w_in x_in0 x_in1 res_in ops0 ops1 ops2 ops3 "
                 "pool_const attn_w qk_topped biascols scales_done "
                 "xn_done xnT_in xh_done xl_done qk_in qkh_done qkl_done v_in v_done "
                 "s_in max_done m_in m_done t_in exp_done sel_done pv_in o_done "
                 "ot_in y_done yT_in yT_done pr_in x1_done xb_done "
                 "var_done rstd_done varb_done rstdb_done xf_done hi_done lo_done "
                 "x1_out0 x1_out1 xhl_out0 xhl_out1 dve_link pool_link "
                 "shw_in shsplit_done misc_in bconst row_in0 row_in1 rowg0 rowg1 x1t_in0 x1t_in1 w_exp "
                 "xT_in xt_done g_in sg_done u_in h_done hT_in hh_done hl_done yp_in y_out "
                 "y_st0 y_st1 lg_in top_in topped wmax_done whi_done wlo_done gprep gsum "
                 "stats_taken scol route_var route_rstd exp_in exp_out sel_ready ranks_in slots_done zero_st "
                 "scat0 scat1 rows_in cols_done blk_done gcol sh_in0 sh_in1 gy0 gy1 ccol comb fin_st0 fin_st1 "
                 "y1_added pool_passed sp_passed dve_passed").split()
        S = {n: sem(n) for n in names}
        ops_in = [S[f"ops{g}"] for g in range(4)]
        x_loaded = [S["x_in0"], S["x_in1"]]
        x1_stored = [S["x1_out0"], S["x1_out1"]]
        xhl_stored = [S["xhl_out0"], S["xhl_out1"]]

        LOOPS = (NB - 6) // 2

        def batches(engine, body, link=None, links=0):
            full = dict(cur=True, prev=True, nxt=True, nxt2=True)
            body(0, 0, **{**full, "prev": False})
            body(1, 1, **full)
            body(2, 0, **full)
            before = link.n if link else 0
            with engine.Fori(0, LOOPS) as i:
                if link:
                    link.base = i * links
                body(2 * i + 3, 1, **full)
                body(2 * i + 4, 0, **full)
            if link:
                assert link.n - before == links, link.n - before
                link.base, link.n = 0, before + LOOPS * links
            body(NB - 3, 1, **full)
            body(NB - 2, 0, **{**full, "nxt2": False})
            body(NB - 1, 1, **{**full, "nxt2": False, "nxt": False})
            body(NB, 0, cur=False, prev=True, nxt=False, nxt2=False)

        row_loaded = [S["row_in0"], S["row_in1"]]
        row_gathered = [S["rowg0"], S["rowg1"]]
        y_stored = [S["y_st0"], S["y_st1"]]
        x1_loaded = [S["x1t_in0"], S["x1t_in1"]]
        scattered = [S["scat0"], S["scat1"]]
        sh_loaded = [S["sh_in0"], S["sh_in1"]]
        y_gathered = [S["gy0"], S["gy1"]]
        fin_stored = [S["fin_st0"], S["fin_st1"]]
        GROUPS = TILES // (2 * E)
        N_SH = TILES
        N_ALL = TILES + BLOCKS

        def shared_blocks(engine, body, first=None, second=None, middle=None, link=None, links=(0, 0)):
            for k in range(GROUPS):
                body(k, k % 2, k // 2, k > 0, True)
            if first:
                first(0)
            before = link.n if link else 0
            with engine.Fori(0, E - 1) as i:
                if link:
                    link.base = i * links[0]
                for k in range(GROUPS):
                    body(GROUPS * i + (GROUPS + k), k % 2, (GROUPS // 2) * i + (GROUPS + k) // 2, True, True)
                if first:
                    first(i + 1)
            if link:
                assert link.n - before == links[0], link.n - before
                link.base, link.n = 0, before + (E - 1) * links[0]
            if middle:
                middle()
            before = link.n if link else 0
            with engine.Fori(0, E - 1) as i:
                if link:
                    link.base = i * links[1]
                for k in range(GROUPS):
                    body(GROUPS * i + (E * GROUPS + k), k % 2, (GROUPS // 2) * i + (E * GROUPS + k) // 2,
                         True, True)
                if second:
                    second(i)
            if link:
                assert link.n - before == links[1], link.n - before
                link.base, link.n = 0, before + (E - 1) * links[1]
            for k in range(GROUPS):
                n = TILES - GROUPS + k
                body(n, n % 2, n // 2, True, n < TILES - 1)
            if second:
                second(E - 1)

        def routed_blocks(engine, body):
            for k in range(2):
                body(N_SH + k, k % 2, N_SH // 2, k > 0, True)
            with engine.Fori(0, BLOCKS // 2 - 2) as i:
                for k in range(2):
                    body(2 * i + (N_SH + 2 + k), k, i + (N_SH // 2 + 1), True, True)
            for k in range(2):
                body(N_ALL - 2 + k, k, N_ALL // 2 - 1, True, k == 0)

        def power_scale(dve, link, r):
            link.link(dve, nc.vector.tensor_scalar(top[:, r], top[:, r], 1e-9, None, ALU.max))
            link.link(dve, nc.vector.tensor_scalar(top[:, r].bitcast(I32), top[:, r].bitcast(I32), 0x7F800000,
                                                   None, ALU.bitwise_and))
            link.link(dve, nc.vector.reciprocal(inv[:, r], top[:, r]))
            link.link(dve, nc.vector.tensor_scalar(wsc[:, r], inv[:, r], 2.0 ** 14, None, ALU.mult))

        def scale_columns(dve, link, r):
            power_scale(dve, link, r)
            nc.vector.tensor_scalar(silu_s[:, r:r + 1], top[:, r, 0:1], 2.0 ** -25, None, ALU.mult)
            nc.vector.tensor_scalar(h_s[:, r:r + 1], inv[:, r, 0:1], 2.0 ** -28, None, ALU.mult)
            link.link(dve, nc.vector.scalar_tensor_tensor(out=y_s[:, r:r + 1], in0=top[:, r, 0:1],
                                                          scalar=2.0 ** -11, in1=top[:, r, 1:2],
                                                          op0=ALU.mult, op1=ALU.mult))
            link.link(dve, nc.vector.tensor_tensor(y_s[:, r:r + 1], y_s[:, r:r + 1], top[:, r, 2:3], ALU.mult))
            nc.vector.tensor_copy(wsc[:, r, 3:4], wsc[:, r, 0:1]).then_inc(S["wlo_done" if r == 0 else "top_in"], 1)

        MATS = ((WG, CC * HID), (WU, CC * HID), (WD, HC * C))

        block = ctx.enter_context(nc.Block())

        @block.sync
        def _(sp):
            def load_x(b, par):
                sp.dma_start(x_in[:, par], xv[b]).then_inc(x_loaded[par], 16)

            def load_group(n, g):
                j = g // 2
                sp.wait_ge(S["qkl_done"], 4 * n + 2 * j + 2)
                sp.sem_inc(S["sp_passed"], 1)
                if some(4 * UN * n + UN * (g + 1) - 4 * UN):
                    sp.wait_ge(S["t_in"], 4 * UN * n + UN * (g + 1) - 4 * UN)
                    sp.sem_inc(S["sp_passed"], 1)
                r0 = 64 * (g % 2)
                for quad, (qs, ks) in enumerate(((qkh, qkh), (qkh, qkl), (qkl, qkh))):
                    for t in range(2):
                        sp.dma_start(q_op[32 * quad:32 * quad + 32, 2 * g + t, :],
                                     qs[r0 + 32 * t:r0 + 32 * t + 32, 2 * j, :]).then_inc(ops_in[g], 16)
                    for h in range(GH):
                        row = 32 * quad + HD * (h % 2)
                        sp.dma_start(k_op[row:row + HD, GH * g + h, :],
                                     ks[r0 + HD * h:r0 + HD * (h + 1), 2 * j + 1, :]).then_inc(ops_in[g], 16)

            sp.dma_start(wa[:, 0:2, :], w_attn.rearrange("(k p) n -> p k n", p=P)).then_inc(S["w_in"], 16)
            sp.wait_ge(S["pool_const"], 1)
            sp.dma_start(wa[0:1, 2, :], b_attn.unsqueeze(0)).then_inc(S["w_in"], 16)
            sp.dma_start(cs[:], rope.unsqueeze(0).broadcast_to([P, 2, 256])).then_inc(S["w_in"], 16)
            load_x(0, 0)
            load_x(1, 1)
            sp.dma_start(bvb[:], b_attn[2 * C:].unsqueeze(0).broadcast_to([P, C])).then_inc(S["const_in"], 16)
            sp.dma_start(bpb[:], b_proj.unsqueeze(0).broadcast_to([P, C])).then_inc(S["const_in"], 16)
            sp.dma_start(wp[:], w_proj.rearrange("(k p) n -> p k n", p=P)).then_inc(S["const_in"], 16)
            sp.wait_ge(S["pool_const"], 5)
            for g in range(3):
                load_group(0, g)
            sp.wait_ge(S["scales_done"], 1)
            for k, (src, n) in enumerate(((sWg, HID), (sWu, HID), (sWd, C))):
                sp.dma_start(shared_raw[:, k * CC * HID:(k + 1) * CC * HID].rearrange("p (c n) -> p c n", n=n),
                             src.rearrange("(c p) n -> p c n", p=P)).then_inc(S["shw_in"], 16)

            def body(b, par, cur, prev, nxt, nxt2):
                if cur:
                    load_group(b, 3)
                if nxt2:
                    sp.wait_ge(S["xn_done"], b + 1)
                    sp.sem_inc(S["sp_passed"], 1)
                    load_x(b + 2, par)
                if prev:
                    if some(2 * (b - 1)):
                        sp.wait_ge(S["x1_done"], 2 * (b - 1))
                        sp.sem_inc(S["sp_passed"], 1)
                    sp.dma_start(xres[:], xv[b - 1]).then_inc(S["res_in"], 16)
                if nxt:
                    load_group(b + 1, 0)
                    load_group(b + 1, 1)
                for j in range(2):
                    if j and nxt:
                        load_group(b + 1, 2)
                    if prev:
                        sp.wait_ge(S["lo_done"], 2 * (b - 1) + j + 1)
                        sp.sem_inc(S["sp_passed"], 1)
                        sp.dma_start(x1v[b - 1, j], x1[:, j]).then_inc(x1_stored[j], 16)
                        sp.dma_start(xhlv[b - 1, j], xhl[:, j].rearrange("p t s c -> p t (s c)")
                                     ).then_inc(xhl_stored[j], 16)

            batches(sp, body)

            sp.wait_ge(S["lo_done"], 2 * NB)
            for stored in (*x1_stored, *xhl_stored):
                sp.wait_ge(stored, 16 * NB)
            sp.dma_start(gate_t[:], gate_w).then_inc(S["misc_in"], 16)
            sp.dma_start(lns[:, 0], ln_scale).then_inc(S["misc_in"], 16)
            sp.dma_start(lns[:, 1], ln_bias).then_inc(S["misc_in"], 16)

            def rows(n, par):
                if some(n - 1):
                    sp.wait_ge(S["xT_in"], n - 1)
                    sp.sem_inc(S["sp_passed"], 1)
                sp.dma_start(xrow[:, par], xhl_d[bass.ds(n * P, P), :]).then_inc(row_loaded[par], 16)

            def residual_rows(n, par):
                if some(n - 1):
                    sp.wait_ge(S["y_out"], n - 1)
                    sp.sem_inc(S["sp_passed"], 1)
                sp.dma_start(x1t[:, par], x1_d[bass.ds(n * P, P), :]).then_inc(x1_loaded[par], 16)

            rows(0, 0)
            rows(1, 1)
            residual_rows(0, 0)
            sp.wait_ge(S["bconst"], 1)
            sp.dma_start(tok_d.rearrange("(p n) o -> p (n o)", p=P), zero_i[:]).then_inc(S["zero_st"], 16)

            def body(n, par, half, prev, nxt):
                if isinstance(n, int) and n >= TILES - 2:
                    pass
                else:
                    rows(n + 2, par)
                if nxt:
                    residual_rows(n + 1, 1 - par)
                if prev:
                    sp.wait_ge(S["y_out"], n)
                    sp.sem_inc(S["sp_passed"], 1)
                    sp.dma_start(sh_d[bass.ds((n - 1) * P, P), :], ysb[:, 1 - par]).then_inc(y_stored[1 - par], 16)

            def load_expert(e):
                if some(48 * e):
                    sp.wait_ge(S["w_exp"], 48 * e)
                    sp.sem_inc(S["sp_passed"], 1)
                for (off, n), src in zip(MATS, (Wg, Wu, Wd)):
                    dst = wraw[:, bass.ds(e + 1, 1), off // 2:off // 2 + n]
                    w = src[bass.ds(e, 1)].rearrange("o (c p) n -> p (o c) n", p=P)
                    sp.dma_start(dst.rearrange("p o (c n) -> p (o c) n", n=w.shape[2]), w).then_inc(S["w_exp"], 16)

            load_expert(0)
            for k in range(GROUPS):
                body(k, k % 2, k // 2, k > 0, True)
            load_expert(1)
            with sp.Fori(0, E - 2) as i:
                for k in range(GROUPS):
                    body(GROUPS * i + (GROUPS + k), k % 2, 0, True, True)
                load_expert(i + 2)
            with sp.Fori(E - 1, 2 * E - 1) as i:
                for k in range(GROUPS):
                    body(GROUPS * i + k, k % 2, 0, True, True)
            for k in range(GROUPS):
                n = TILES - GROUPS + k
                body(n, n % 2, n // 2, True, n < TILES - 1)
            n = TILES - 1
            sp.wait_ge(S["y_out"], n + 1)
            sp.dma_start(sh_d[n * P:(n + 1) * P, :], ysb[:, n % 2]).then_inc(y_stored[n % 2], 16)

            sp.wait_ge(scattered[0], 16 * TILES)
            sp.wait_ge(scattered[1], 16 * TILES)
            sp.dma_start(tok_rows[:], tok_d.rearrange("(p n) o -> p (n o)", p=P)).then_inc(S["rows_in"], 16)

            def store(n, par, half, prev, nxt):
                if prev:
                    sp.wait_ge(S["y_out"], n)
                    sp.sem_inc(S["sp_passed"], 1)
                    sp.dma_start(y_d[bass.ds((n - (N_SH + 1)) * P, P), :],
                                 ysb[:, 1 - par]).then_inc(y_stored[1 - par], 16)

            routed_blocks(sp, store)
            n = N_ALL - 1
            sp.wait_ge(S["y_out"], n + 1)
            sp.dma_start(y_d[(n - N_SH) * P:, :], ysb[:, n % 2]).then_inc(y_stored[n % 2], 16)

            for par in range(2):
                sp.wait_ge(y_stored[par], 16 * (N_ALL // 2))

            def load_sh(t, par):
                sp.dma_start(shc[:, par], sh_d[bass.ds(t * P, P), :]).then_inc(sh_loaded[par], 16)

            def store_sum(t, par):
                sp.wait_ge(S["comb"], t + 1)
                sp.sem_inc(S["sp_passed"], 1)
                sp.dma_start(out[bass.ds(t * P, P), :], fin[:, par]).then_inc(fin_stored[par], 16)

            load_sh(0, 0)
            load_sh(1, 1)
            with sp.Fori(0, TILES // 2 - 1) as i:
                for par in range(2):
                    store_sum(2 * i + par, par)
                    load_sh(2 * i + (par + 2), par)
            for par in range(2):
                store_sum(TILES - 2 + par, par)
            for par in range(2):
                sp.wait_ge(fin_stored[par], 16 * (TILES // 2))

        @block.gpsimd
        def _(pool):
            link = Count(S["pool_link"])
            nc.gpsimd.memset(wa[:, 2, :], 0.0).then_inc(S["pool_const"], 1)
            link.link(pool, nc.gpsimd.memset(ident[:], 0.0))
            link.link(pool, nc.gpsimd.affine_select(
                out=ident[:], in_=ident[:], compare_op=ALU.not_equal, fill=1.0, base=0,
                pattern=[[-1, P]], channel_multiplier=1))
            nc.gpsimd.tensor_copy(ident_b[:], ident[:])
            nc.gpsimd.tensor_copy(ident_h[:], ident[:])
            nc.gpsimd.memset(one[:], 1.0)
            nc.gpsimd.memset(neghalf[:], -0.5).then_inc(S["pool_const"], 1)
            link.link(pool, nc.gpsimd.memset(mask[:], 0.0))
            nc.gpsimd.affine_select(out=mask[:], in_=mask[:], compare_op=ALU.is_ge, fill=MASKED, base=0,
                                    pattern=[[-1, P]], channel_multiplier=1).then_inc(S["pool_const"], 1)
            nc.gpsimd.memset(q_op[:], 0.0).then_inc(S["pool_const"], 1)
            link.link(pool, nc.gpsimd.memset(k_op[:], 0.0))
            k_sel = k_op[96:128].rearrange("p (g h) n -> p g h n", h=GH)
            nc.gpsimd.affine_select(out=k_sel, in_=k_sel, compare_op=ALU.not_equal, fill=-SHIFT_UNIT, base=0,
                                    pattern=[[0, NG], [-1, GH], [0, T]],
                                    channel_multiplier=1).then_inc(S["pool_const"], 1)
            pool.wait_ge(S["pool_const"], 5)
            pool.wait_ge(S["attn_w"], 1)
            nc.gpsimd.partition_all_reduce(qk_top[:], qk_max[:], P, RMAX).then_inc(S["qk_topped"], 1)

            def normalise(n, par):
                pool.wait_ge(S["var_done"], n + 1)
                pool.sem_inc(S["pool_passed"], 1)
                nc.gpsimd.tensor_tensor(rstd[:], mv[:, :, 1], neghalf[:], ALU.pow).then_inc(S["rstd_done"], 1)
                pool.wait_ge(S["rstd_done"], n + 1)
                pool.sem_inc(S["pool_passed"], 1)
                if some(2 * n):
                    pool.wait_ge(S["xnT_in"], 2 * n)
                    pool.sem_inc(S["pool_passed"], 1)
                for t in range(NT):
                    last = nc.gpsimd.tensor_scalar(xn[:, t], x_in[:, par, t], mv[:, t, 0:1], rstd[:, t:t + 1],
                                                   ALU.subtract, ALU.mult)
                last.then_inc(S["xn_done"], 1)

            normalise(0, 0)
            normalise(1, 1)

            def select(G, u, half):
                pool.wait_ge(S["exp_done"], UN * G + u + 1)
                pool.sem_inc(S["pool_passed"], 1)
                bankv = prob[:, half, u, :]
                if u < 4:
                    v, pat = bankv[:, 0:P], [[1, P]]
                elif u < 8:
                    v, pat = bankv.rearrange("p (s n) -> p s n", n=P)[:, 0:4:3, :], [[0, 2], [1, P]]
                else:
                    v, pat = bankv.rearrange("p (s n) -> p s n", n=P)[:, 0:4:2, :], [[0, 2], [1, P]]
                nc.gpsimd.affine_select(out=v, in_=v, compare_op=ALU.is_ge, fill=0.0, base=0, pattern=pat,
                                        channel_multiplier=-1).then_inc(S["sel_done"], 1)

            def body(b, par, cur, prev, nxt, nxt2):
                for g in range(NG):
                    G = 4 * b + g
                    has1 = (cur or g < 1) and (prev or g >= 1)
                    for s in range(13):
                        if has1 and 3 <= s < 13:
                            select(G - 1, s - 3, (g - 1) % 2)
                        if (g, s) == (1, 0) and prev:
                            pool.wait_ge(S["const_in"], 48)
                            pool.wait_ge(S["res_in"], 16 * b)
                            pool.sem_inc(S["pool_passed"], 1)
                            for t in range(NT):
                                last = nc.gpsimd.tensor_tensor(xres[:, t], xres[:, t], bpb[:], ALU.add)
                            last.then_inc(S["xb_done"], 1)
                        if (g, s) == (2, 12) and nxt2:
                            normalise(b + 2, par)
                        if prev and g == 3 and s in (4, 11):
                            j = (4, 11).index(s)
                            k = 2 * (b - 1) + j
                            pool.wait_ge(S["varb_done"], k + 1)
                            pool.sem_inc(S["pool_passed"], 1)
                            nc.gpsimd.tensor_tensor(rstdb[:], mvb[:, :, 1], neghalf[:, 0:2],
                                                    ALU.pow).then_inc(S["rstdb_done"], 1)
                        if prev and g == 3 and s in (6, 12):
                            j = (6, 12).index(s)
                            k = 2 * (b - 1) + j
                            pool.wait_ge(S["xf_done"], k + 1)
                            pool.sem_inc(S["pool_passed"], 1)
                            if some(16 * (b - 1)):
                                pool.wait_ge(xhl_stored[j], 16 * (b - 1))
                                pool.sem_inc(S["pool_passed"], 1)
                            nc.gpsimd.tensor_scalar(xhl[:, j, :, 0, :], xf[:], X_SCALE, None,
                                                    ALU.mult).then_inc(S["hi_done"], 1)

            batches(pool, body)

            pool.wait_ge(S["lo_done"], 2 * NB)
            for stored in (*x1_stored, *xhl_stored):
                pool.wait_ge(stored, 16 * NB)
            nc.gpsimd.memset(zero_i[:], 0).then_inc(S["bconst"], 1)
            nc.gpsimd.memset(ones_f[:], 1.0)
            nc.gpsimd.memset(ones_b[:], 1.0)
            nc.gpsimd.memset(zeros[:], 0.0)
            nc.gpsimd.memset(rhalf[:], -0.5)
            nc.gpsimd.iota(iota_e[:], [[1, E]], base=0, channel_multiplier=0, allow_small_or_imprecise_dtypes=True)
            nc.gpsimd.iota(iota_j[:], [[P, TILES]], base=0, channel_multiplier=0,
                           allow_small_or_imprecise_dtypes=True)
            nc.gpsimd.iota(tok_i[:], [[P, TILES]], base=0, channel_multiplier=1)
            link.link(pool, nc.gpsimd.memset(before_b[:], 1.0))
            link.link(pool, nc.gpsimd.affine_select(out=before_b[:], in_=before_b[:], compare_op=ALU.is_gt,
                                                    fill=0.0, base=0, pattern=[[1, P]], channel_multiplier=-1))
            nc.gpsimd.iota(iota_b[:], [[1, BLOCKS]], base=0, channel_multiplier=0,
                           allow_small_or_imprecise_dtypes=True).then_inc(S["bconst"], 1)
            pool.wait_ge(S["bconst"], 2)
            pool.wait_ge(S["gprep"], 1)
            nc.gpsimd.partition_all_reduce(top[:, 1:3, :], top[:, 1:3, :], P, RMAX).then_inc(S["topped"], 1)
            pool.wait_ge(S["wmax_done"], E)
            nc.gpsimd.partition_all_reduce(top[:, 0, 0:3], run3[:], P, RMAX).then_inc(S["topped"], 1)
            pool.wait_ge(S["route_var"], 1)
            nc.gpsimd.tensor_tensor(rvar[:, 1], rvar[:, 0], rhalf[:], ALU.pow).then_inc(S["route_rstd"], 1)
            pool.wait_ge(S["zero_st"], 16)
            pool.wait_ge(S["slots_done"], 1)
            def scatter(t, par, i):
                if some(32 * i):
                    pool.wait_ge(scattered[par], 32 * i)
                    pool.sem_inc(S["pool_passed"], 1)
                nc.gpsimd.tensor_copy(sc_col[:, par, 0:1], dest_i[:, 0, bass.ds(t, 1)])
                nc.gpsimd.tensor_copy(sc_col[:, par, 1:2], dest_i[:, 1, bass.ds(t, 1)])
                nc.gpsimd.tensor_copy(sc_col[:, par, 2:3], tok_i[:, bass.ds(t, 1)]).then_inc(S["scol"], 1)
                pool.wait_ge(S["scol"], t + 1)
                pool.sem_inc(S["pool_passed"], 1)
                for k in range(2):
                    pool.indirect_dma_start(
                        out=tok_d, out_offset=bass.IndirectOffsetOnAxis(ap=sc_col[:, par, k:k + 1], axis=0),
                        in_=sc_col[:, par, 2:3], in_offset=None).then_inc(scattered[par], 16)
            for par in range(2):
                scatter(par, par, 0)
            with pool.Fori(1, TILES // 2) as i:
                for par in range(2):
                    scatter(2 * i + par, par, i)
            pool.wait_ge(S["rows_in"], 16)

            def gather(n, par, half):
                pool.wait_ge(S["xT_in"], n - 1)
                pool.sem_inc(S["pool_passed"], 1)
                nc.gpsimd.tensor_copy(ga_col[:, par, :], tok_rows[:, bass.ds(n - N_SH, 1)]).then_inc(S["gcol"], 1)
                pool.wait_ge(S["gcol"], n - (N_SH - 1))
                pool.sem_inc(S["pool_passed"], 1)
                pool.indirect_dma_start(
                    out=xrow[:, par], out_offset=None, in_=xhl_d,
                    in_offset=bass.IndirectOffsetOnAxis(ap=ga_col[:, par, :], axis=0),
                ).then_inc(row_gathered[par], 16)

            with pool.Fori(0, BLOCKS // 2) as i:
                for par in range(2):
                    gather(2 * i + (N_SH + par), par, 0)

            for par in range(2):
                pool.wait_ge(y_stored[par], 16 * (N_ALL // 2))
            def gather_outputs(t, par):
                if some(t - 1):
                    pool.wait_ge(S["comb"], t - 1)
                    pool.sem_inc(S["pool_passed"], 1)
                nc.gpsimd.tensor_copy(co_col[:, par, 0:1], slot_i[:, 0, bass.ds(t, 1)])
                nc.gpsimd.tensor_copy(co_col[:, par, 1:2], slot_i[:, 1, bass.ds(t, 1)]).then_inc(S["ccol"], 1)
                pool.wait_ge(S["ccol"], t + 1)
                pool.sem_inc(S["pool_passed"], 1)
                for k, dst in enumerate((y1, y2)):
                    pool.indirect_dma_start(
                        out=dst[:, par], out_offset=None, in_=y_d,
                        in_offset=bass.IndirectOffsetOnAxis(ap=co_col[:, par, k:k + 1], axis=0),
                    ).then_inc(y_gathered[par], 16)

            for par in range(2):
                gather_outputs(par, par)
            with pool.Fori(1, TILES // 2) as i:
                for par in range(2):
                    gather_outputs(2 * i + par, par)

        @block.scalar
        def _(act):
            def xn_high(n, c):
                act.wait_ge(S["xnT_in"], 2 * n + c + 1)
                if some(2 * n):
                    act.wait_ge(S["v_in"], 2 * n)
                nc.scalar.copy(xh[:, c, :], ps_q[:]).then_inc(S["xh_done"], 1)

            def qk_high(n, i):
                act.wait_ge(S["qk_in"], 4 * n + i + 1)
                for g in (0, 1) if i < 2 else (2, 3):
                    if some(LOADS * n):
                        act.wait_ge(ops_in[g], LOADS * n)
                nc.scalar.activation(qkh[:, i, :], ps_q[:], ACT.Identity,
                                     bias=bcol[:, i:i + 1]).then_inc(S["qkh_done"], 1)

            def prologue():
                act.wait_ge(S["pool_const"], 5)
                act.wait_ge(S["scales_done"], 1)
                for c in range(2):
                    xn_high(0, c)
                for i in range(4):
                    qk_high(0, i)

            prologue()

            def body(b, par, cur, prev, nxt, nxt2):
                for g in range(NG):
                    G = 4 * b + g
                    has1 = (cur or g < 1) and (prev or g >= 1)
                    has2 = (cur or g < 2) and (prev or g >= 2)
                    for s in range(13):
                        if s == 2 and has1:
                            act.wait_ge(S["m_in"], G)
                            pair = 2 * ((g - 1) % 4)
                            nc.scalar.activation(
                                q_op[96:96 + GH, pair:pair + 2, :],
                                ps_m[0:GH, :].unsqueeze(1).broadcast_to([GH, 2, T]),
                                ACT.Copy, scale=1.0 / SHIFT_UNIT).then_inc(S["m_done"], 1)
                        if has1 and 3 <= s < 13:
                            u = s - 3
                            if u == 0:
                                if some(G - 2):
                                    act.wait_ge(S["pv_in"], G - 2)
                            act.wait_ge(S["t_in"], UN * (G - 1) + u + 1)
                            nc.scalar.activation(prob[:, (g - 1) % 2, u, :], ps_t[u % 2][:], ACT.Exp,
                                                 scale=exp_scale[:]).then_inc(S["exp_done"], 1)
                        if s == 10 and has2:
                            opar = par if g >= 2 else 1 - par
                            nb = b if g >= 2 else b - 1
                            act.wait_ge(S["pv_in"], G - 1)
                            if some(4 * (nb - 1)):
                                act.wait_ge(S["ot_in"], 4 * (nb - 1))
                            nc.scalar.copy(o_t[:, opar, (g - 2) % 4, :], ps_o[:]).then_inc(S["o_done"], 1)
                        if nxt:
                            for c, at in enumerate(((0, 2), (0, 6))):
                                if (g, s) == at:
                                    xn_high(b + 1, c)
                            for i, at in enumerate(((0, 11), (1, 3), (1, 8), (2, 5))):
                                if (g, s) == at:
                                    qk_high(b + 1, i)
                        if prev:
                            for j, at in enumerate(((2, 8), (3, 5))):
                                if (g, s) == at:
                                    k = 2 * (b - 1) + j
                                    act.wait_ge(S["yT_in"], k + 1)
                                    if some(k):
                                        act.wait_ge(S["pr_in"], k)
                                    nc.scalar.copy(y_t[:].rearrange("p t c n -> p (t c n)"),
                                                   ps_y[:]).then_inc(S["yT_done"], 1)

            batches(act, body)

            act.wait_ge(S["top_in"], 1)
            for m, (off, n) in enumerate(MATS):
                nc.scalar.activation(wsh[:, off:off + n], shared_raw[:, off // 2:off // 2 + n], ACT.Copy,
                                     scale=wsc[:, 1, m:m + 1]).then_inc(S["shsplit_done"], 1)

            def silu(n, par, r):
                act.wait_ge(S["g_in"], n + 1)
                if some(n - 1):
                    act.wait_ge(S["h_done"], n - 1)
                nc.scalar.activation(sg[:, par], ps_g[:], ACT.Silu, scale=silu_s[:, r:r + 1]
                                     ).then_inc(S["sg_done"], 1)

            def high(n):
                act.wait_ge(S["hT_in"], n + 1)
                if some(n):
                    act.wait_ge(S["yp_in"], n)
                nc.scalar.copy(hth[:].rearrange("p c n -> p (c n)"), ps_h[:]).then_inc(S["hh_done"], 1)

            def shared(n, par, half, prev, nxt):
                silu(n, par, 1)
                if prev:
                    high(n - 1)

            def second(e):
                act.wait_ge(S["wlo_done"], e + 1)
                for m, (off, n) in enumerate(MATS):
                    last = nc.scalar.activation(wbuf[:, bass.ds(e * SLOT + off, n)],
                                                wraw[:, bass.ds(e + 1, 1), off // 2:off // 2 + n],
                                                ACT.Copy, scale=wsc[:, 0, m:m + 1])
                last.then_inc(S["whi_done"], 1)

            shared_blocks(act, shared, second=second)
            high(N_SH - 1)
            act.wait_ge(S["exp_in"], 1)
            nc.scalar.activation(tmp[:], tmp[:], ACT.Exp)
            nc.scalar.activation(m12[:, 3], m12[:, 2], ACT.Exp).then_inc(S["exp_out"], 1)

            def result(n, par, half):
                act.wait_ge(S["yp_in"], n + 1)
                act.wait_ge(y_stored[par], 16 * half)
                nc.scalar.activation(ysb[:, par], ps_z[:, 0:C], ACT.Copy, scale=y_s[:, 0:1]
                                     ).then_inc(S["y_out"], 1)

            def routed(n, par, half, prev, nxt):
                silu(n, par, 0)
                if prev:
                    high(n - 1)
                    result(n - 1, 1 - par, half - 1 if par == 0 else half)

            routed_blocks(act, routed)
            high(N_ALL - 1)
            result(N_ALL - 1, (N_ALL - 1) % 2, (N_ALL - 1) // 2)

        @block.vector
        def _(dve):
            link = Count(S["dve_link"])

            def stats(n, par):
                dve.wait_ge(x_loaded[par], 8 * n + 16 - 8 * par)
                if some(n):
                    dve.wait_ge(S["xn_done"], n)
                for t in range(NT):
                    last = nc.vector.bn_stats(st6[:, t], x_in[:, par, t])
                last.then_inc(S["stats_taken"], 1)
                dve.wait_ge(S["stats_taken"], n + 1)
                dve.sem_inc(S["dve_passed"], 1)
                for t in range(NT):
                    last = nc.vector.bn_aggr(mv[:, t], st6[:, t])
                link.link(dve, last)
                nc.vector.tensor_scalar(mv[:, :, 1], mv[:, :, 1], EPS, None,
                                        ALU.add).then_inc(S["var_done"], 1)

            def xn_low(n, c):
                dve.wait_ge(S["xh_done"], 2 * n + c + 1)
                nc.vector.tensor_tensor(xl[:, c, :], ps_q[:], xh[:, c, :].bitcast(F32),
                                        ALU.subtract).then_inc(S["xl_done"], 1)

            def qk_low(n, i):
                dve.wait_ge(S["qkh_done"], 4 * n + i + 1)
                nc.vector.scalar_tensor_tensor(out=qkl[:, i, :], in0=ps_q[:], scalar=bcol[:, i:i + 1],
                                               in1=qkh[:, i, :], op0=ALU.add,
                                               op1=ALU.subtract).then_inc(S["qkl_done"], 1)

            def values(n, par, j):
                dve.wait_ge(S["v_in"], 2 * n + j + 1)
                if some(4 * (n - 1)):
                    dve.wait_ge(S["pv_in"], 4 * (n - 1))
                for t in range(2):
                    last = nc.vector.tensor_tensor(
                        v_op[:, par, 2 * j + t, :, 0:HD],
                        ps_q[:, 256 * t:256 * t + 256].rearrange("p (h d) -> p h d", d=HD),
                        bvb[:].rearrange("p (h d) -> p h d", d=HD), ALU.add)
                last.then_inc(S["v_done"], 1)

            def prologue():
                for par in range(2):
                    nc.vector.memset(v_op[:, par, :, :, HD:], 0.0)
                link.link(dve, nc.vector.memset(mx[:], 0.0))
                link.link(dve, nc.vector.memset(v_op[:, :, :, :, HD:HD + 1].rearrange(
                    "p a t h d -> p (a t h) d"), 1.0))
                stats(0, 0)
                dve.wait_ge(S["w_in"], 48)
                ev = wa[:, :, 0:512].rearrange("p k (i e) -> p k i e", e=2)[:, :, :, 0]
                od = wa[:, :, 0:512].rearrange("p k (i e) -> p k i e", e=2)[:, :, :, 1]
                cosv = cs[:, 0:1, :].broadcast_to([P, 3, 256])
                sinv = cs[:, 1:2, :].broadcast_to([P, 3, 256])
                nc.vector.tensor_tensor(rope_t[:, 0], ev, sinv, ALU.mult)
                link.link(dve, nc.vector.tensor_tensor(rope_t[:, 1], od, sinv, ALU.mult))
                nc.vector.tensor_tensor(ev, ev, cosv, ALU.mult)
                link.link(dve, nc.vector.tensor_tensor(od, od, cosv, ALU.mult))
                nc.vector.tensor_tensor(ev, ev, rope_t[:, 1], ALU.subtract)
                link.link(dve, nc.vector.tensor_tensor(od, od, rope_t[:, 0], ALU.add))
                for s in range(2):
                    last = nc.vector.tensor_reduce(qk_max[:, s:s + 1], wa[:, :, 256 * s:256 * s + 256],
                                                   mybir.AxisListType.XY, ALU.max, apply_absolute_value=True)
                last.then_inc(S["attn_w"], 1)
                dve.wait_ge(S["qk_topped"], 1)
                link.link(dve, nc.vector.tensor_scalar(qk_top[:], qk_top[:], 1e-30, None, ALU.max))
                link.link(dve, nc.vector.tensor_scalar(qk_top[:].bitcast(I32), qk_top[:].bitcast(I32),
                                                       0x7F800000, None, ALU.bitwise_and))
                link.link(dve, nc.vector.reciprocal(qk_inv[:], qk_top[:]))
                link.link(dve, nc.vector.tensor_scalar(qk_scale[:], qk_inv[:], 16.0, None, ALU.mult))
                nc.vector.scalar_tensor_tensor(out=exp_scale[:], in0=qk_top[:, 0:1], scalar=1.0 / 256,
                                               in1=qk_top[:, 1:2], op0=ALU.mult, op1=ALU.mult)
                for s in range(2):
                    w_s = wa[:, :, 256 * s:256 * s + 256]
                    last = nc.vector.tensor_scalar(w_s, w_s, qk_scale[:, s:s + 1], None, ALU.mult)
                last.then_inc(S["attn_w"], 1)
                dve.wait_ge(S["biascols"], 1)
                nc.vector.tensor_copy(bcol[:], ps_m[:, 0:4])
                link.link(dve, nc.vector.tensor_copy(wah[:], wa[:, 0:2, :]))
                nc.vector.tensor_tensor(wal[:], wa[:, 0:2, :], wah[:].bitcast(F32),
                                        ALU.subtract).then_inc(S["scales_done"], 1)
                stats(1, 1)

            def prologue_qkv():
                dve.wait_ge(S["const_in"], 48)
                for c in range(2):
                    xn_low(0, c)
                for i in range(4):
                    qk_low(0, i)
                for j in range(2):
                    values(0, 0, j)

            prologue()
            prologue_qkv()

            def row_max(G, g, u):
                dve.wait_ge(S["s_in"], UN * G + u + 1)
                if u == 0:
                    if some(G - 1):
                        dve.wait_ge(S["m_in"], G - 1)
                src, dst = ps_s[u % 2], mx[:, g % 2]

                def top(lo, n, out):
                    return nc.vector.tensor_reduce(out, src[:, lo:lo + n], AX_X, ALU.max)

                if u < 4:
                    last = top(0, 512, dst[:, 3, u:u + 1])
                elif u < 8:
                    top(0, 384, dst[:, 2, u - 4:u - 3])
                    last = top(384, 128, dst[:, 0, u - 4:u - 3])
                else:
                    c = 2 * (u - 8)
                    last = nc.vector.tensor_reduce(dst[:, 1, c:c + 2],
                                                   src[:].rearrange("p (h n) -> p h n", h=2), AX_X, ALU.max)
                last.then_inc(S["max_done"], 1)

            def divide(bp, q):
                k = 4 * bp + q
                dve.wait_ge(S["ot_in"], k + 1)
                ov = ps_y[:].rearrange("p (h d) -> p h d", d=32)
                link.link(dve, nc.vector.reciprocal(rec[:, q % 2], ov[:, :, HD]))
                if some(2 * bp + q // 2):
                    dve.wait_ge(S["yT_in"], 2 * bp + q // 2)
                nc.vector.tensor_tensor(y[:, q % 2].rearrange("p (h d) -> p h d", d=HD), ov[:, :, 0:HD],
                                        rec[:, q % 2].unsqueeze(2).broadcast_to([P, H, HD]),
                                        ALU.mult).then_inc(S["y_done"], 1)

            def residual(bp, j):
                k = 2 * bp + j
                dve.wait_ge(S["pr_in"], k + 1)
                dve.wait_ge(S["xb_done"], bp + 1)
                if some(16 * bp):
                    dve.wait_ge(x1_stored[j], 16 * bp)
                link.link(dve, nc.vector.tensor_tensor(
                    x1[:, j].rearrange("p t c -> p (t c)"), ps_m[:],
                    xres[:, 2 * j:2 * j + 2].rearrange("p t c -> p (t c)"), ALU.add))
                for t in range(2):
                    last = nc.vector.bn_stats(st6b[:, t], x1[:, j, t])
                last.then_inc(S["x1_done"], 1)
                dve.wait_ge(S["x1_done"], k + 1)
                dve.sem_inc(S["dve_passed"], 1)
                for t in range(2):
                    last = nc.vector.bn_aggr(mvb[:, t], st6b[:, t])
                link.link(dve, last)
                link.link(dve, nc.vector.tensor_copy(var_all[:, bass.ds(NT * bp + 2 * j, 2)], mvb[:, :, 1]))
                nc.vector.tensor_scalar(mvb[:, :, 1], mvb[:, :, 1], EPS, None,
                                        ALU.add).then_inc(S["varb_done"], 1)

            def rows(bp, j):
                k = 2 * bp + j
                dve.wait_ge(S["rstdb_done"], k + 1)
                if some(k):
                    dve.wait_ge(S["hi_done"], k)
                for t in range(2):
                    last = nc.vector.tensor_scalar(xf[:, t], x1[:, j, t], mvb[:, t, 0:1], rstdb[:, t:t + 1],
                                                   ALU.subtract, ALU.mult)
                last.then_inc(S["xf_done"], 1)

            def low(bp, j):
                k = 2 * bp + j
                dve.wait_ge(S["hi_done"], k + 1)
                nc.vector.scalar_tensor_tensor(out=xhl[:, j, :, 1, :], in0=xf[:], scalar=X_SCALE,
                                               in1=xhl[:, j, :, 0, :], op0=ALU.mult,
                                               op1=ALU.subtract).then_inc(S["lo_done"], 1)

            def body(b, par, cur, prev, nxt, nxt2):
                for g in range(NG):
                    G = 4 * b + g
                    for s in range(13):
                        if cur and s < 10:
                            row_max(G, g, s)
                        if nxt:
                            for c, at in enumerate(((0, 2), (0, 6))):
                                if (g, s) == at:
                                    xn_low(b + 1, c)
                            for i, at in enumerate(((0, 11), (1, 3), (1, 8), (2, 5))):
                                if (g, s) == at:
                                    qk_low(b + 1, i)
                            for j, at in enumerate(((3, 3), (3, 7))):
                                if (g, s) == at:
                                    values(b + 1, 1 - par, j)
                        if nxt2 and (g, s) == (2, 2):
                            stats(b + 2, par)
                        if prev:
                            for q, at in enumerate(((2, 1), (2, 4), (2, 10), (3, 1))):
                                if (g, s) == at:
                                    divide(b - 1, q)
                            if (g, s) == (3, 0):
                                residual(b - 1, 0)
                            if (g, s) == (3, 5):
                                rows(b - 1, 0)
                            if (g, s) == (3, 8):
                                low(b - 1, 0)
                            if (g, s) == (3, 10):
                                residual(b - 1, 1)
                            if (g, s) == (3, 12):
                                rows(b - 1, 1)
                                low(b - 1, 1)

            batches(dve, body, link, DVE_LINKS)

            def route():
                V = nc.vector

                def per_tile(v):
                    return v.unsqueeze(2).broadcast_to([P, TILES, E])

                def per_expert(v):
                    return v.unsqueeze(1).broadcast_to([P, TILES, E])

                def step(instruction):
                    link.link(dve, instruction)

                step(V.tensor_scalar(rvar[:, 0], var_all[:], EPS, None, ALU.add))
                step(V.reciprocal(rvar[:, 1], rvar[:, 0]))
                step(V.tensor_tensor(rvar[:, 0], rvar[:, 1], var_all[:], ALU.mult))
                V.tensor_scalar(rvar[:, 0], rvar[:, 0], EPS, None, ALU.add).then_inc(S["route_var"], 1)
                dve.wait_ge(S["route_rstd"], 1)
                dve.wait_ge(S["lg_in"], N_SH)
                pl = ps_l[:].rearrange("p (t e) -> p t e", e=E)
                step(V.scalar_tensor_tensor(out=lg[:], in0=pl, scalar=lg_s[:], in1=per_tile(rvar[:, 1]),
                                            op0=ALU.mult, op1=ALU.mult))
                step(V.tensor_tensor(lg[:], lg[:], per_expert(sgb[:, 1]), ALU.add))
                src = lg
                for k in range(2):
                    step(V.tensor_reduce(m12[:, k], src[:], AX_X, ALU.max))
                    step(V.tensor_tensor(tmp[:], src[:], per_tile(m12[:, k]), ALU.is_equal))
                    step(V.scalar_tensor_tensor(out=tmp[:], in0=tmp[:], scalar=-float(E), in1=per_expert(iota_e[:]),
                                                op0=ALU.mult, op1=ALU.add))
                    step(V.tensor_reduce(rw[:, 0], tmp[:], AX_X, ALU.min))
                    step(V.tensor_scalar(rw[:, 0], rw[:, 0], float(E), None, ALU.add))
                    step(V.tensor_tensor(oh[:, k], per_expert(iota_e[:]), per_tile(rw[:, 0]), ALU.is_equal))
                    if k == 0:
                        step(V.scalar_tensor_tensor(out=lg2[:], in0=oh[:, 0], scalar=MASKED, in1=lg[:], op0=ALU.mult,
                                                    op1=ALU.add))
                        src = lg2
                V.tensor_tensor(sel[:], oh[:, 0], oh[:, 1], ALU.add).then_inc(S["sel_ready"], 1)
                step(V.tensor_tensor(tmp[:], lg[:], per_tile(m12[:, 0]), ALU.subtract))
                V.tensor_tensor(m12[:, 2], m12[:, 1], m12[:, 0], ALU.subtract).then_inc(S["exp_in"], 1)

                dve.wait_ge(S["ranks_in"], 1)
                ranks = ps_r[0][:].rearrange("p (t e) -> p t e", e=E)
                totals = ps_r[1][:].rearrange("p (t e) -> p e t", e=E)
                for e in range(E):
                    last = V.tensor_tensor_scan(out=incl[:, e], data0=totals[:, e], data1=zeros[:], initial=0.0,
                                                op0=ALU.add, op1=ALU.add)
                step(last)
                cmp = lg2[:].rearrange("p t e -> p (t e)").rearrange("p (e t) -> p e t", e=E)
                step(V.tensor_tensor(cmp, incl[:, :, TILES - 1:TILES].broadcast_to([P, E, TILES]),
                                     iota_j[:].unsqueeze(1).broadcast_to([P, E, TILES]), ALU.is_gt))
                step(V.tensor_reduce(nblk[:, 0], cmp, AX_X, ALU.add))
                step(V.tensor_tensor_scan(out=nblk[:, 1], data0=nblk[:, 0], data1=zeros[:, 0:E], initial=0.0,
                                          op0=ALU.add, op1=ALU.add))
                step(V.tensor_tensor(nblk[:, 2], nblk[:, 1], nblk[:, 0], ALU.subtract))
                step(V.tensor_scalar(nblk[:, 3], nblk[:, 2], float(P), None, ALU.mult))
                step(V.tensor_tensor(blk_cmp[:], iota_b[:].unsqueeze(2).broadcast_to([1, BLOCKS, E - 1]),
                                     nblk[0:1, 1, 0:E - 1].unsqueeze(1).broadcast_to([1, BLOCKS, E - 1]), ALU.is_ge))
                step(V.tensor_reduce(blk_f[:], blk_cmp[:], AX_X, ALU.add))
                V.tensor_scalar(blk_off[:], blk_f[:], float(SLOT), None, ALU.mult).then_inc(S["blk_done"], 1)
                inclt = incl[:].rearrange("p e t -> p t e")
                step(V.tensor_tensor(lg[:], inclt, ps_r[1][:].rearrange("p (t e) -> p t e", e=E), ALU.subtract))
                step(V.tensor_tensor(lg[:], lg[:], ranks, ALU.add))
                step(V.tensor_tensor(lg[:], lg[:], per_expert(nblk[:, 3]), ALU.add))
                for k in range(2):
                    step(V.tensor_tensor(lg2[:], oh[:, k], lg[:], ALU.mult))
                    step(V.tensor_reduce(slot_f[:, k], lg2[:], AX_X, ALU.add))
                step(V.tensor_copy(slot_i[:], slot_f[:]))
                V.tensor_scalar(row_i[:, 0], slot_i[:], P - 1, None, ALU.bitwise_and)
                step(V.tensor_scalar(row_i[:, 1], slot_i[:], 7, None, ALU.logical_shift_right))
                V.scalar_tensor_tensor(out=dest_i[:], in0=row_i[:, 0], scalar=float(BLOCKS), in1=row_i[:, 1],
                                       op0=ALU.mult, op1=ALU.add).then_inc(S["slots_done"], 1)
                dve.wait_ge(S["exp_out"], 1)
                step(V.tensor_reduce(rw[:, 0], tmp[:], AX_X, ALU.add))
                step(V.reciprocal(rw[:, 1], rw[:, 0]))
                step(V.tensor_tensor(rw[:, 2], m12[:, 3], rw[:, 1], ALU.mult))
                step(V.scalar_tensor_tensor(out=rw[:, 3], in0=rw[:, 1], scalar=EPS, in1=rw[:, 2], op0=ALU.add,
                                            op1=ALU.add))
                step(V.reciprocal(rw[:, 0], rw[:, 3]))
                V.tensor_tensor(rw[:, 4], rw[:, 1], rw[:, 0], ALU.mult)
                step(V.tensor_tensor(rw[:, 5], rw[:, 2], rw[:, 0], ALU.mult))

            dve.wait_ge(S["lo_done"], 2 * NB)
            for stored in (*x1_stored, *xhl_stored):
                dve.wait_ge(stored, 16 * NB)
            dve.wait_ge(S["shw_in"], 48)
            dve.wait_ge(S["misc_in"], 48)
            dve.wait_ge(S["bconst"], 2)
            link.link(dve, nc.vector.memset(top[:], 0.0))
            nc.vector.memset(run3[:], 0.0)
            nc.vector.tensor_reduce(top[:, 1, 0:3], shared_raw.rearrange("p (m n) -> p m n", m=3), AX_X, ALU.max,
                                    apply_absolute_value=True)
            for k in range(2):
                for c in range(CC):
                    last = nc.vector.tensor_scalar(gs_t[:, CC * k + c], gate_t[:, c], lns[:, k, c:c + 1], None,
                                                   ALU.mult)
            link.link(dve, last)
            nc.vector.tensor_reduce(top[:, 2, 0:1], gs_t[:, 0:CC], mybir.AxisListType.XY, ALU.max,
                                    apply_absolute_value=True).then_inc(S["gprep"], 1)
            dve.wait_ge(S["topped"], 1)
            scale_columns(dve, link, 1)
            power_scale(dve, link, 2)
            nc.vector.tensor_scalar(lg_s[:], top[:, 2, 0:1], 2.0 ** -25, None, ALU.mult)
            link.link(dve, nc.vector.tensor_scalar(gate_hl[:, 0], gs_t[:, 0:CC], wsc[:, 2, 0:1], None, ALU.mult))
            nc.vector.scalar_tensor_tensor(out=gate_hl[:, 1], in0=gs_t[:, 0:CC], scalar=wsc[:, 2, 0:1],
                                           in1=gate_hl[:, 0], op0=ALU.mult, op1=ALU.subtract
                                           ).then_inc(S["top_in"], 1)
            for m, (off, n) in enumerate(MATS):
                dve.wait_ge(S["shsplit_done"], m + 1)
                nc.vector.scalar_tensor_tensor(out=wsh[:, off + n:off + 2 * n],
                                               in0=shared_raw[:, off // 2:off // 2 + n],
                                               scalar=wsc[:, 1, m:m + 1], in1=wsh[:, off:off + n],
                                               op0=ALU.mult, op1=ALU.subtract).then_inc(S["gprep"], 1)
            dve.wait_ge(S["gsum"], 1)
            link.link(dve, nc.vector.tensor_copy(sgb[:], bank[6][:, 0:2 * E].rearrange("p (k e) -> p k e", k=2)))

            def take_rows(n, par):
                dve.wait_ge(S["xT_in"], n + 1)
                if some(n - 1):
                    dve.wait_ge(S["u_in"], n - 1)
                nc.vector.tensor_copy(xt[:, par].rearrange("p c n -> p (c n)"), ps_x16[:, 0:2 * C]
                                      ).then_inc(S["xt_done"], 1)

            def low(n):
                dve.wait_ge(S["hh_done"], n + 1)
                nc.vector.tensor_tensor(htl[:].rearrange("p c n -> p (c n)"), ps_h[:],
                                        hth[:].rearrange("p c n -> p (c n)"),
                                        ALU.subtract).then_inc(S["hl_done"], 1)

            def hidden(n, par, r):
                dve.wait_ge(S["u_in"], n + 1)
                dve.wait_ge(S["sg_done"], n + 1)
                if some(n):
                    dve.wait_ge(S["hT_in"], n)
                nc.vector.scalar_tensor_tensor(out=hb[:], in0=ps_u[:], scalar=h_s[:, r:r + 1], in1=sg[:, par],
                                               op0=ALU.mult, op1=ALU.mult).then_inc(S["h_done"], 1)

            def result(n, par, half):
                dve.wait_ge(S["yp_in"], n + 1)
                if some(16 * half):
                    dve.wait_ge(y_stored[par], 16 * half)
                dve.wait_ge(x1_loaded[par], 16 * half + 16)
                nc.vector.scalar_tensor_tensor(out=ysb[:, par], in0=ps_z[:, 0:C], scalar=y_s[:, 1:2],
                                               in1=x1t[:, par], op0=ALU.mult, op1=ALU.add
                                               ).then_inc(S["y_out"], 1)

            def shared(n, par, half, prev, nxt):
                if prev:
                    low(n - 1)
                hidden(n, par, 1)
                if nxt:
                    take_rows(n + 1, 1 - par)
                if prev:
                    result(n - 1, 1 - par, half - 1 if par == 0 else half)

            def first(e):
                dve.wait_ge(S["w_exp"], 48 * (e + 1))
                link.link(dve, nc.vector.tensor_reduce(
                    top[:, 0, 0:3], wraw[:, bass.ds(e + 1, 1), :].rearrange("p o (m n) -> p (o m) n", m=3),
                    AX_X, ALU.max, apply_absolute_value=True))
                nc.vector.tensor_tensor(run3[:], run3[:], top[:, 0, 0:3], ALU.max).then_inc(S["wmax_done"], 1)
                dve.wait_ge(S["wmax_done"], e + 1)

            def second(e):
                dve.wait_ge(S["whi_done"], e + 1)
                for m, (off, n) in enumerate(MATS):
                    last = nc.vector.scalar_tensor_tensor(
                        out=wbuf[:, bass.ds(e * SLOT + (off + n), n)],
                        in0=wraw[:, bass.ds(e + 1, 1), off // 2:off // 2 + n].rearrange("p o n -> p (o n)"),
                        scalar=wsc[:, 0, m:m + 1], in1=wbuf[:, bass.ds(e * SLOT + off, n)],
                        op0=ALU.mult, op1=ALU.subtract)
                last.then_inc(S["wlo_done"], 1)

            take_rows(0, 0)
            def middle():
                dve.wait_ge(S["topped"], 2)
                scale_columns(dve, link, 0)

            shared_blocks(dve, shared, first, second, middle, link, (1, 0))
            low(N_SH - 1)
            result(N_SH - 1, (N_SH - 1) % 2, (N_SH - 1) // 2)
            route()

            def routed(n, par, half, prev, nxt):
                if prev:
                    low(n - 1)
                hidden(n, par, 0)
                if nxt:
                    take_rows(n + 1, 1 - par)

            take_rows(N_SH, 0)
            routed_blocks(dve, routed)
            low(N_ALL - 1)
            def combine(t, par, i):
                dve.wait_ge(sh_loaded[par], 16 * i + 16)
                dve.wait_ge(y_gathered[par], 32 * i + 32)
                nc.vector.scalar_tensor_tensor(out=acc[:, par], in0=y1[:, par], scalar=rw[:, 4, bass.ds(t, 1)],
                                               in1=shc[:, par], op0=ALU.mult, op1=ALU.add
                                               ).then_inc(S["y1_added"], 1)
                dve.wait_ge(S["y1_added"], t + 1)
                if some(16 * i):
                    dve.wait_ge(fin_stored[par], 16 * i)
                nc.vector.scalar_tensor_tensor(out=fin[:, par], in0=y2[:, par], scalar=rw[:, 5, bass.ds(t, 1)],
                                               in1=acc[:, par], op0=ALU.mult, op1=ALU.add
                                               ).then_inc(S["comb"], 1)

            for par in range(2):
                combine(par, par, 0)
            with dve.Fori(1, TILES // 2) as i:
                for par in range(2):
                    combine(2 * i + par, par, i)

        @block.tensor
        def _(pe):
            def transpose_xn(n, c):
                pe.wait_ge(S["xn_done"], n + 1)
                if c:
                    pe.wait_ge(S["xl_done"], 2 * n + c)
                elif some(2 * n):
                    pe.wait_ge(S["v_done"], 2 * n)
                for t in range(NT):
                    last = nc.tensor.transpose(ps_q[:, P * t:P * (t + 1)], xn[:, t, P * c:P * (c + 1)], ident[:])
                last.then_inc(S["xnT_in"], 1)

            def products(out, pairs):
                n = 3 * len(pairs)
                i = 0
                for (lh, ll), (rh, rl) in pairs:
                    for a, m in ((lh, rh), (lh, rl), (ll, rh)):
                        last = nc.tensor.matmul(out, a, m, start=(i == 0), stop=(i == n - 1))
                        i += 1
                return last

            def project_qk(n, i):
                if i == 0:
                    pe.wait_ge(S["xl_done"], 2 * n + 2)
                else:
                    pe.wait_ge(S["qkl_done"], 4 * n + i)
                col = 256 * (i % 2) + P * (i // 2)
                products(ps_q[:], [((wah[:, c, col:col + P], wal[:, c, col:col + P]),
                                    (xh[:, c, :], xl[:, c, :])) for c in range(2)]).then_inc(S["qk_in"], 1)

            def project_v(n, j):
                if j == 0:
                    pe.wait_ge(S["qkl_done"], 4 * n + 4)
                else:
                    pe.wait_ge(S["v_done"], 2 * n + 1)
                for t in range(2):
                    tok = slice(P * (2 * j + t), P * (2 * j + t + 1))
                    last = products(ps_q[:, 256 * t:256 * t + 256],
                                    [((xh[:, c, tok], xl[:, c, tok]),
                                      (wah[:, c, 2 * C:], wal[:, c, 2 * C:])) for c in range(2)])
                last.then_inc(S["v_in"], 1)

            def prologue():
                pe.wait_ge(S["attn_w"], 2)
                pe.wait_ge(S["pool_const"], 3)
                for i in range(4):
                    col = 256 * (i % 2) + P * (i // 2)
                    last = nc.tensor.matmul(ps_m[:, i:i + 1], wa[0:1, 2, col:col + P], one[0:1, :],
                                            start=True, stop=True)
                last.then_inc(S["biascols"], 1)
                transpose_xn(0, 0)
                transpose_xn(0, 1)
                pe.wait_ge(S["scales_done"], 1)
                for i in range(4):
                    project_qk(0, i)
                project_v(0, 0)
                project_v(0, 1)

            prologue()

            def scores(b, G, g, u):
                if u == 0:
                    pe.wait_ge(ops_in[g], LOADS * (b + 1))
                if some(UN * G + u - 1):
                    pe.wait_ge(S["max_done"], UN * G + u - 1)
                out = ps_s[u % 2]

                def mm(h, q, lo, start):
                    nc.tensor.matmul(out[:, lo:lo + P * (q + 1)],
                                     q_op[0:96, 2 * g + h // 2, P * q:P * (q + 1)],
                                     k_op[0:96, GH * g + h, 0:P * (q + 1)], start=start, stop=False)

                cols = out[:].rearrange("p (s n) -> p s n", n=P)
                if u < 4:
                    mm(u, 3, 0, True)
                    sel, n = cols[:, 3:4, :], 1
                elif u < 8:
                    mm(u - 4, 2, 0, True)
                    mm(u - 4, 0, 384, False)
                    sel, n = cols[:, 2:4, :], 2
                else:
                    mm(2 * (u - 8), 1, 0, True)
                    mm(2 * (u - 8) + 1, 1, 256, False)
                    sel, n = cols[:, 1:4:2, :], 2
                nc.tensor.matmul(sel, ident_b[:], mask[:].unsqueeze(1).broadcast_to([P, n, P]),
                                 start=False, stop=True).then_inc(S["s_in"], 1)

            def maxima(b, G, g):
                pe.wait_ge(S["max_done"], UN * G)
                if some(G - 1):
                    pe.wait_ge(S["m_done"], G - 1)
                if g == 0:
                    if some(2 * (b - 1)):
                        pe.wait_ge(S["x1_done"], 2 * (b - 1))
                if g == 3:
                    if some(2 * (b - 1) + 1):
                        pe.wait_ge(S["x1_done"], 2 * (b - 1) + 1)
                for q in range(NT):
                    last = nc.tensor.matmul(ps_m[0:GH, P * q:P * (q + 1)], mx[:, (g - 1) % 2, q, :], ident[:],
                                            start=True, stop=True)
                last.then_inc(S["m_in"], 1)

            def shifted(G, gg, u):
                if u == 0:
                    pe.wait_ge(S["m_done"], G + 1)
                if some(UN * G + u - 1):
                    pe.wait_ge(S["exp_done"], UN * G + u - 1)
                out = ps_t[u % 2]

                def mm(h, k, lo, start, stop):
                    n = T - P * k
                    return nc.tensor.matmul(out[:, lo:lo + n], k_op[:, GH * gg + h, P * k:P * (k + 1)],
                                            q_op[:, 2 * gg + h // 2, P * k:], start=start, stop=stop)

                if u < 4:
                    last = mm(u, 0, 0, True, True)
                elif u < 8:
                    mm(u - 4, 1, 0, True, False)
                    last = mm(u - 4, 3, 384, False, True)
                else:
                    mm(2 * (u - 8), 2, 0, True, False)
                    last = mm(2 * (u - 8) + 1, 2, 256, False, True)
                last.then_inc(S["t_in"], 1)

            def mix(G, gg, vpar, nb, piece):
                if piece == 0:
                    if some(G):
                        pe.wait_ge(S["o_done"], G)
                    pe.wait_ge(S["v_done"], 2 * (nb + 1))
                k = (0, 1, 3, 2)[piece]
                pe.wait_ge(S["sel_done"], UN * G + (4, 8, 8, 10)[piece])
                pr = prob[:, gg % 2]
                for h in range(GH):
                    unit, lo = ((h, 0), (4 + h, 0), (8 + h // 2, 256 * (h % 2)), (4 + h, 384))[k]
                    n = T - P * k
                    last = nc.tensor.matmul(ps_o[32 * h:32 * h + 32, P * k:], v_op[:, vpar, k, GH * gg + h, :],
                                            pr[:, unit, lo:lo + n], start=(piece == 0), stop=(piece == 3))
                if piece == 3:
                    last.then_inc(S["pv_in"], 1)

            def transpose_o(bp, opar, q):
                k = 4 * bp + q
                pe.wait_ge(S["o_done"], 4 * bp + 4)
                if q == 0:
                    if some(2 * bp):
                        pe.wait_ge(S["yT_done"], 2 * bp)
                elif q == 2:
                    pe.wait_ge(S["yT_done"], 2 * bp + 1)
                else:
                    pe.wait_ge(S["y_done"], k)
                for g in range(NG):
                    last = nc.tensor.transpose(ps_y[:, P * g:P * (g + 1)], o_t[:, opar, g, P * q:P * (q + 1)],
                                               ident[:])
                last.then_inc(S["ot_in"], 1)

            def transpose_y(bp, j):
                pe.wait_ge(S["y_done"], 4 * bp + 2 * j + 2)
                for t in range(2):
                    for c in range(2):
                        last = nc.tensor.transpose(ps_y[:, P * (2 * t + c):P * (2 * t + c + 1)],
                                                   y[:, t, P * c:P * (c + 1)], ident[:])
                last.then_inc(S["yT_in"], 1)

            def project_out(b, bp, j, tail):
                pe.wait_ge(S["yT_done"], 2 * bp + j + 1)
                if tail:
                    pe.wait_ge(S["x1_done"], 2 * bp + j)
                else:
                    pe.wait_ge(S["m_done"], 4 * b + 2 + j)
                for t in range(2):
                    for c in range(2):
                        last = nc.tensor.matmul(ps_m[:, 256 * t:256 * t + 256], y_t[:, t, c, :], wp[:, c, :],
                                                start=(c == 0), stop=(c == 1))
                last.then_inc(S["pr_in"], 1)

            def body(b, par, cur, prev, nxt, nxt2):
                for g in range(NG):
                    G = 4 * b + g
                    has1 = (cur or g < 1) and (prev or g >= 1)
                    has2 = (cur or g < 2) and (prev or g >= 2)
                    for s in range(13):
                        if cur and s < 10:
                            scores(b, G, g, s)
                        if s == 2 and has1:
                            maxima(b, G, g)
                        if has1 and 3 <= s < 13:
                            shifted(G - 1, (g - 1) % 4, s - 3)
                        if has2 and s in (1, 3, 5, 8):
                            mix(G - 2, (g - 2) % 4, par if g >= 2 else 1 - par, b if g >= 2 else b - 1,
                                (1, 3, 5, 8).index(s))
                        if nxt:
                            for c, at in enumerate(((0, 1), (0, 5))):
                                if (g, s) == at:
                                    transpose_xn(b + 1, c)
                            for i, at in enumerate(((0, 10), (1, 2), (1, 7), (2, 4))):
                                if (g, s) == at:
                                    project_qk(b + 1, i)
                            for j, at in enumerate(((3, 2), (3, 6))):
                                if (g, s) == at:
                                    project_v(b + 1, j)
                        if prev:
                            for q, at in enumerate(((2, 0), (2, 3), (2, 9), (3, 0))):
                                if (g, s) == at:
                                    transpose_o(b - 1, 1 - par, q)
                            for j, at in enumerate(((2, 7), (3, 4))):
                                if (g, s) == at:
                                    transpose_y(b - 1, j)
                            for j, at in enumerate(((2, 11), (3, 8))):
                                if (g, s) == at:
                                    project_out(b, b - 1, j, not cur)

            batches(pe, body)

            pe.wait_ge(S["lo_done"], 2 * NB)
            for stored in (*x1_stored, *xhl_stored):
                pe.wait_ge(stored, 16 * NB)
            pe.wait_ge(S["top_in"], 2)
            pe.wait_ge(S["bconst"], 2)
            for k in range(2):
                for c in range(CC):
                    last = nc.tensor.matmul(bank[6][:, E * k:E * (k + 1)], ones_f[:], gs_t[:, CC * k + c],
                                            start=(c == 0), stop=(c == CC - 1))
            last.then_inc(S["gsum"], 1)

            def weights(w, off, k, n, size):
                if w is None:
                    return wsh[:, off + k * n:off + (k + 1) * n], wsh[:, off + size + k * n:off + size + (k + 1) * n]
                return (wbuf[:, bass.ds(w + (off + k * n), n)], wbuf[:, bass.ds(w + (off + size + k * n), n)])

            def transpose_rows(n, par, arrived, count):
                pe.wait_ge(arrived[par], 16 * count + 16)
                if some(n):
                    pe.wait_ge(S["xt_done"], n)
                for c in range(2 * CC):
                    last = nc.tensor.transpose(ps_x16[:, P * c:P * (c + 1)], xrow[:, par, P * c:P * (c + 1)],
                                               ident_h[:])
                last.then_inc(S["xT_in"], 1)

            def x_pair(par, c):
                return xt[:, par, c, :], xt[:, par, CC + c, :]

            def gate(n, par, w):
                pe.wait_ge(S["xt_done"], n + 1)
                if some(n):
                    pe.wait_ge(S["sg_done"], n)
                products(ps_g[:], [(x_pair(par, c), weights(w, WG, c, HID, CC * HID)) for c in range(CC)]
                         ).then_inc(S["g_in"], 1)

            def up(n, par, w):
                if some(n):
                    pe.wait_ge(S["h_done"], n)
                products(ps_u[:], [(x_pair(par, c), weights(w, WU, c, HID, CC * HID)) for c in range(CC)]
                         ).then_inc(S["u_in"], 1)

            def transpose_hidden(n):
                pe.wait_ge(S["h_done"], n + 1)
                if some(n):
                    pe.wait_ge(S["hl_done"], n)
                for k in range(HC):
                    last = nc.tensor.transpose(ps_h[:, P * k:P * (k + 1)], hb[:, P * k:P * (k + 1)], ident[:])
                last.then_inc(S["hT_in"], 1)

            def down(n, w):
                pe.wait_ge(S["hl_done"], n + 1)
                if some(n):
                    pe.wait_ge(S["y_out"], n)
                products(ps_z[:, 0:C], [((hth[:, k, :], htl[:, k, :]), weights(w, WD, k, C, HC * C))
                                        for k in range(HC)]).then_inc(S["yp_in"], 1)

            def logits(n, par):
                products(ps_l[:, bass.ds(n * E, E)], [(x_pair(par, c), (gate_hl[:, 0, c, :], gate_hl[:, 1, c, :]))
                                                      for c in range(CC)]).then_inc(S["lg_in"], 1)

            def shared(n, par, half, prev, nxt):
                gate(n, par, None)
                if prev:
                    transpose_hidden(n - 1)
                logits(n, par)
                up(n, par, None)
                if nxt:
                    transpose_rows(n + 1, 1 - par, row_loaded, half + par)
                if prev:
                    down(n - 1, None)

            transpose_rows(0, 0, row_loaded, 0)
            pe.wait_ge(S["gprep"], 4)
            shared_blocks(pe, shared)
            transpose_hidden(N_SH - 1)
            down(N_SH - 1, None)

            pe.wait_ge(S["sel_ready"], 1)
            flat = sel[:].rearrange("p t e -> p (t e)")
            nc.tensor.matmul(ps_r[0][:], before_b[:], flat, start=True, stop=True)
            nc.tensor.matmul(ps_r[1][:], ones_b[:], flat, start=True, stop=True).then_inc(S["ranks_in"], 1)
            pe.wait_ge(S["wlo_done"], E + 1)
            pe.wait_ge(S["blk_done"], 1)

            def routed(n, par, half, prev, nxt):
                w = pe.value_load(blk_off[0:1, bass.ds(n - N_SH, 1)], min_val=0, max_val=(E - 1) * SLOT)
                gate(n, par, w)
                if prev:
                    transpose_hidden(n - 1)
                up(n, par, w)
                if nxt:
                    transpose_rows(n + 1, 1 - par, row_gathered, half + (par - N_SH // 2))
                if prev:
                    wp_ = pe.value_load(blk_off[0:1, bass.ds(n - (N_SH + 1), 1)], min_val=0,
                                        max_val=(E - 1) * SLOT)
                    down(n - 1, wp_)

            transpose_rows(N_SH, 0, row_gathered, 0)
            routed_blocks(pe, routed)
            transpose_hidden(N_ALL - 1)
            down(N_ALL - 1, pe.value_load(blk_off[0:1, BLOCKS - 1:BLOCKS], min_val=0, max_val=(E - 1) * SLOT))


def rope_table(heads, hd):
    theta = (1.0 / 10000.0 ** (np.arange(0, hd, 2, dtype=np.float32) / np.float32(hd))).astype(np.float32)
    ang = (np.arange(heads, dtype=np.float32)[:, None] * theta[None, :]).reshape(-1)
    k = np.stack([np.cos(ang), np.sin(ang)]).astype(np.float32)
    return np.concatenate([k * np.float32(hd ** -0.5), k], axis=1)


INPUTS = ["L0_attn_x", "L0_attn_W_attn", "L0_attn_b_attn", "L0_attn_W_proj", "L0_attn_b_proj",
          "L0_ffn_ln_scale", "L0_ffn_ln_bias", "L0_ffn_gate_w", "L0_ffn_Wg", "L0_ffn_Wu", "L0_ffn_Wd",
          "L0_ffn_sWg", "L0_ffn_sWu", "L0_ffn_sWd"]


def kernel(**inputs):
    import concourse.bacc as bacc
    from concourse.bass_utils import run_bass_kernel_spmd

    nc = bacc.Bacc("TRN2", target_bir_lowering=False, num_devices=1)
    shape = inputs["L0_attn_x"].shape
    arrays = {f"in_{name}": np.ascontiguousarray(inputs[name]) for name in INPUTS}
    arrays["in_L0_attn_x"] = arrays["in_L0_attn_x"].reshape(-1, shape[-1])
    gate = arrays["in_L0_ffn_gate_w"]
    arrays["in_L0_ffn_gate_w"] = np.ascontiguousarray(gate.reshape(gate.shape[0], -1, P).transpose(2, 1, 0))
    for name in ("in_L0_ffn_ln_scale", "in_L0_ffn_ln_bias"):
        arrays[name] = np.ascontiguousarray(arrays[name].reshape(-1, P).T)
    arrays["in_rope"] = rope_table(16, shape[-1] // 16)
    args = [nc.dram_tensor(n, a.shape, mybir.dt.from_np(a.dtype), kind="ExternalInput").ap()
            for n, a in arrays.items()]
    out = nc.dram_tensor("out_x", arrays["in_L0_attn_x"].shape, F32, kind="ExternalOutput").ap()
    build(nc, *args, out)
    r = run_bass_kernel_spmd(nc, [arrays], core_ids=[0])
    return r.results[0]["out_x"].reshape(shape)
```

```python
from contextlib import ExitStack

import numpy as np
import concourse.bass as bass
from concourse import mybir

F32 = mybir.dt.float32
F32R = mybir.dt.float32r
F16 = mybir.dt.float16
BF16 = mybir.dt.bfloat16
I32 = mybir.dt.int32
ALU = mybir.AluOpType
ACT = mybir.ActivationFunctionType
AX_X = mybir.AxisListType.X
RMAX = bass.bass_isa.ReduceOp.max

P = 128
BEFORE_MAX = 26
EPS = 1e-5
X_SCALE = 2048.0
SHIFT_UNIT = 32768.0
MASKED = -1e30
DVE_LINKS = 18


class Count:

    def __init__(self, sem):
        self.sem, self.base, self.n = sem, 0, 0

    def link(self, engine, instruction):
        instruction.then_inc(self.sem, 1)
        self.n += 1
        engine.wait_ge(self.sem, self.base + self.n)


def some(value):
    return not isinstance(value, int) or value > 0


def build(nc, x, w_attn, b_attn, w_proj, b_proj, ln_scale, ln_bias, gate_w, Wg, Wu, Wd, sWg, sWu, sWd, rope, out):
    NTOK, C = x.shape
    T = 512
    NB = NTOK // T
    NT = T // P
    H = 16
    HD = C // H
    GH = 4
    NG = H // GH
    UN = 10
    LOADS = 18 * 16

    E = Wg.shape[0]
    HID = Wg.shape[2]
    TILES = NTOK // P
    BLOCKS = (2 * NTOK + E * (P - 1)) // P
    BLOCKS += BLOCKS % 2
    CC, HC = C // P, HID // P
    WG, WU, WD = 0, 2 * CC * HID, 4 * CC * HID
    SLOT = 4 * CC * HID + 2 * HC * C

    def scratch(name, shape, dt):
        return nc.dram_tensor(name, shape, dt, kind="Internal").ap()

    x1_d = scratch("x1_d", (NTOK, C), F32)
    xhl_d = scratch("xhl_d", (NTOK + P, 2 * C), F16)
    tok_d = scratch("tok_d", (P * BLOCKS, 2), I32)

    xv = x.rearrange("(b t p) c -> b p t c", t=NT, p=P)
    x1v = x1_d.rearrange("(b j t p) c -> b j p t c", j=2, t=2, p=P)
    xhlv = xhl_d[0:NTOK].rearrange("(b j t p) c -> b j p t c", j=2, t=2, p=P)

    with ExitStack() as ctx:
        def sb(name, shape, dt):
            return ctx.enter_context(nc.sbuf_tensor(name, shape, dt))

        ctx_a = ctx.enter_context(ExitStack())

        def sb_a(name, shape, dt):
            return ctx_a.enter_context(nc.sbuf_tensor(name, shape, dt))

        def sem(name):
            return ctx.enter_context(nc.semaphore(name))

        bank = [ctx.enter_context(nc.psum_tensor(f"bank{i}", [P, 512], F32)) for i in range(8)]
        ps_s, ps_t, ps_o, ps_q, ps_m, ps_y = bank[0:2], bank[2:4], bank[4], bank[5], bank[6], bank[7]

        ident_h = sb("ident_h", [P, P], F16)
        wsh = sb("wsh", [P, SLOT], F16)
        var_all = sb("var_all", [P, TILES], F32)
        early = sb("early", [P, SLOT // 2 + 3 * 256], F32)
        ident = sb("ident", [P, P], F32)
        ident_b = sb("ident_b", [P, P], BF16)
        mask = sb("mask", [P, P], BF16)
        one = sb("one", [P, 1], F32)
        neghalf = sb("neghalf", [P, 4], F32)
        cs = sb_a("cs", [P, 2, 256], F32)
        bvb = sb_a("bvb", [P, C], F32)
        bpb = sb_a("bpb", [P, C], F32)
        wa = early[:, 0:9 * C].rearrange("p (k n) -> p k n", k=3)
        shared_raw = early[:, 0:SLOT // 2]
        wah = sb_a("wah", [P, 2, 3 * C], F32R)
        wal = sb_a("wal", [P, 2, 3 * C], F32R)
        wp = sb_a("wp", [P, 2, C], F32)
        bcol = sb_a("bcol", [P, 4], F32)
        qk_max = sb_a("qk_max", [P, 2], F32)
        qk_top = sb_a("qk_top", [P, 2], F32)
        qk_inv = sb_a("qk_inv", [P, 2], F32)
        qk_scale = sb_a("qk_scale", [P, 2], F32)
        exp_scale = sb_a("exp_scale", [P, 1], F32)
        rope_t = early[:, 9 * C:15 * C].rearrange("p (a k n) -> p a k n", a=2, k=3)
        x_in = sb_a("x_in", [P, 2, NT, C], F32)
        xn = sb_a("xn", [P, NT, C], F32)
        st6 = sb_a("st6", [P, NT, 6], F32)
        mv = sb_a("mv", [P, NT, 2], F32)
        rstd = sb_a("rstd", [P, NT], F32)
        xh = sb_a("xh", [P, 2, T], F32R)
        xl = sb_a("xl", [P, 2, T], F32R)
        qkh = sb_a("qkh", [P, 4, T], F16)
        qkl = sb_a("qkl", [P, 4, T], F16)
        q_op = sb_a("q_op", [P, H // 2, T], F16)
        k_op = sb_a("k_op", [P, H, T], F16)
        v_op = sb_a("v_op", [P, 2, NT, H, 32], F32)
        mx = sb_a("mx", [P, 2, NT, GH], F32)
        prob = sb_a("prob", [P, 2, UN, 512], F32)
        o_t = sb_a("o_t", [P, 2, NG, T], F32)
        rec = sb_a("rec", [P, 2, H], F32)
        y = sb_a("y", [P, 2, C], F32)
        y_t = sb_a("y_t", [P, 2, 2, P], F32)
        xres = sb_a("xres", [P, NT, C], F32)
        x1 = sb_a("x1", [P, 2, 2, C], F32)
        st6b = sb_a("st6b", [P, 2, 6], F32)
        mvb = sb_a("mvb", [P, 2, 2], F32)
        rstdb = sb_a("rstdb", [P, 2], F32)
        xf = sb_a("xf", [P, 2, C], F32)
        xhl = sb_a("xhl", [P, 2, 2, 2, C], F16)

        ctx_a.close()
        wbuf = sb("wbuf", [P, (E + 1) * SLOT], F16)
        wraw = wbuf[:].bitcast(F32).rearrange("p (s n) -> p s n", s=E + 1)
        xrow = sb("xrow", [P, 2, 2 * C], F16)
        xt = sb("xt", [P, 2, 2 * CC, P], F16)
        sg = sb("sg", [P, 2, HID], F32)
        hb = sb("hb", [P, HID], F32)
        hth = sb("hth", [P, HC, P], F16)
        htl = sb("htl", [P, HC, P], F16)
        ysb = sb("ysb", [P, 2, C], F32)
        x1t = sb("x1t", [P, 2, C], F32)
        spare = wbuf[:, E * SLOT:]
        lrow = spare[:, 0:2 * 4 * 2 * C].rearrange("p (a t n) -> p a t n", a=2, t=4)
        xtl = sb("xtl", [P, 2, 2, 2 * CC, P], F16)
        zero_h = sb("zero_h", [P, 2 * C], F16)
        top = sb("top", [P, 3, 4], F32)
        inv = sb("inv", [P, 3, 4], F32)
        wsc = sb("wsc", [P, 3, 4], F32)
        run3 = sb("run3", [P, 3], F32)
        silu_s = sb("silu_s", [P, 2], F32)
        h_s = sb("h_s", [P, 2], F32)
        y_s = sb("y_s", [P, 2], F32)
        lg_s = sb("lg_s", [P, 1], F32)
        gate_t = sb("gate_t", [P, CC, E], F32)
        gs_t = sb("gs_t", [P, 2 * CC, E], F32)
        gate_hl = sb("gate_hl", [P, 2, CC, E], F16)
        lns = sb("lns", [P, 2, CC], F32)
        ones_f = sb("ones_f", [P, P], F32)
        ones_b = sb("ones_b", [P, P], BF16)
        before_b = sb("before_b", [P, P], BF16)
        sgb = sb("sgb", [P, 2, E], F32)
        rvar = sb("rvar", [P, 2, TILES], F32)
        rhalf = sb("rhalf", [P, TILES], F32)
        lg = sb("lg", [P, TILES, E], F32)
        lg2 = sb("lg2", [P, TILES, E], F32)
        tmp = sb("tmp", [P, TILES, E], F32)
        oh = sb("oh", [P, 2, TILES, E], F32)
        sel = sb("sel", [P, TILES, E], BF16)
        m12 = sb("m12", [P, 4, TILES], F32)
        rw = sb("rw", [P, 6, TILES], F32)
        iota_e = sb("iota_e", [P, E], F32)
        iota_j = sb("iota_j", [P, TILES], F32)
        iota_b = sb("iota_b", [1, BLOCKS], F32)
        incl = sb("incl", [P, E, TILES], F32)
        zeros = sb("zeros", [P, TILES], F32)
        nblk = sb("nblk", [P, 4, E], F32)
        slot_f = sb("slot_f", [P, 2, TILES], F32)
        slot_i = sb("slot_i", [P, 2, TILES], I32)
        row_i = sb("row_i", [P, 3, 2, TILES], I32)
        dest_i = sb("dest_i", [P, TILES, 2], I32)
        tok_w = sb("tok_w", [P, TILES, 2, 2], I32)
        tok_rows = sb("tok_rows", [P, BLOCKS, 2], I32)
        no_tok = sb("no_tok", [P, BLOCKS, 2], I32)
        row_w = sb("row_w", [P, BLOCKS], F32)
        blk_cmp = sb("blk_cmp", [1, BLOCKS, E - 1], F32)
        blk_f = sb("blk_f", [1, BLOCKS], F32)
        blk_off = sb("blk_off", [1, BLOCKS], I32)
        to_col = sb("to_col", [P, 2, 2], I32)
        tw_col = sb("tw_col", [P, 2, 4], I32)
        ga_col = sb("ga_col", [P, 2, 1], I32)
        ad_col = sb("ad_col", [P, 2, 1], I32)
        ps_g, ps_u, ps_h, ps_x, ps_z, ps_l = bank[0], bank[1], bank[2], bank[3], bank[4], bank[5]
        ps_x16 = ps_x[:].bitcast(F16)
        ps_lx = [bank[k][:].bitcast(F16) for k in (0, 1)]
        ps_r = bank[6:8]

        names = ("const_in w_in x_in0 x_in1 res_in ops0 ops1 ops2 ops3 "
                 "pool_const attn_w qk_topped biascols scales_done "
                 "xn_done xnT_in xh_done xl_done qk_in qkh_done qkl_done v_in v_done "
                 "s_in max_done m_in m_done t_in exp_done sel_done pv_in o_done "
                 "ot_in y_done yT_in yT_done pr_in x1_done xb_done "
                 "var_done rstd_done varb_done rstdb_done xf_done hi_done lo_done "
                 "x1_out0 x1_out1 xhl_out0 xhl_out1 dve_link pool_link "
                 "shw_in shsplit_done misc_in bconst row_in0 row_in1 rowg0 rowg1 x1t_in0 x1t_in1 w_exp "
                 "xT_in xt_done g_in sg_done u_in h_done hT_in hh_done hl_done yp_in y_out "
                 "y_st0 y_st1 lg_in top_in topped wmax_done whi_done wlo_done gprep gsum "
                 "stats_taken x1_taken scol route_var route_rstd exp_in exp_out sel_ready ranks_in slots_done zero_st "
                 "scat0 scat1 rows_in blk_done gcol acol y_added spare_st lrow_in0 lrow_in1 lxT_in lxt_done0 lxt_done1 row_w_done "
                 "weights_done pool_passed sp_passed dve_passed").split()
        S = {n: sem(n) for n in names}
        ops_in = [S[f"ops{g}"] for g in range(4)]
        x_loaded = [S["x_in0"], S["x_in1"]]
        x1_stored = [S["x1_out0"], S["x1_out1"]]
        xhl_stored = [S["xhl_out0"], S["xhl_out1"]]

        LOOPS = (NB - 6) // 2
        EXP_AT, RANKS_AT = 7, 8

        LAG = 13
        MAXIMA, M_ROWS = 1, 2
        MIX, O_OUT = (2, 4, 5, 6), 7
        XN_T, XN_HIGH, XN_LOW = ((0, 0), (0, 3)), ((0, 1), (0, 4)), ((0, 2), (0, 5))
        QK, QK_HIGH, QK_LOW = (((0, 7), (1, 0), (2, 3), (2, 7)), ((0, 8), (1, 1), (2, 4), (2, 8)),
                               ((0, 9), (1, 2), (2, 5), (2, 9)))
        V_PROJ, VALUES = ((1, 7), (1, 9)), ((1, 8), (2, 0))
        STATS, VARIANCE = ((1, 4), (1, 6)), (2, 3)
        NORMALISE = ((2, 5), (2, 8), (3, 1), (3, 3))
        O_T, DIVIDE = ((1, 8), (2, 0), (2, 9), (3, 2)), ((1, 9), (2, 1), (3, 1), (3, 3))
        Y_T, Y_OUT, PROJ = ((2, 5), (3, 4)), ((2, 6), (3, 5)), ((2, 8), (3, 6))
        X_BIAS = ((0, 4), (0, 7), (1, 0), (1, 3))
        X1, X1_STATS, X1_VARIANCE = ((3, 0), (3, 7)), ((3, 2), (3, 9)), ((3, 4), (0, 0))
        RSTD_B, ROWS, HIGH, LOW = ((3, 4), (0, 1)), ((3, 5), (0, 3)), ((3, 6), (0, 5)), ((3, 8), (0, 7))

        def layernorm_of(b, prev, prev2):
            return (0, b - 1, prev), (1, b - 2, prev2)

        def batches(engine, body, link=None, links=0):
            full = dict(cur=True, prev=True, prev2=True, nxt=True, nxt2=True)
            body(0, 0, **{**full, "prev": False, "prev2": False})
            body(1, 1, **{**full, "prev2": False})
            body(2, 0, **full)
            before = link.n if link else 0
            with engine.Fori(0, LOOPS) as i:
                if link:
                    link.base = i * links
                body(2 * i + 3, 1, **full)
                body(2 * i + 4, 0, **full)
            if link:
                assert link.n - before == links, link.n - before
                link.base, link.n = 0, before + LOOPS * links
            body(NB - 3, 1, **full)
            body(NB - 2, 0, **{**full, "nxt2": False})
            body(NB - 1, 1, **{**full, "nxt2": False, "nxt": False})
            body(NB, 0, cur=False, prev=True, prev2=True, nxt=False, nxt2=False)

        row_loaded = [S["row_in0"], S["row_in1"]]
        row_gathered = [S["rowg0"], S["rowg1"]]
        y_stored = [S["y_st0"], S["y_st1"]]
        x1_loaded = [S["x1t_in0"], S["x1t_in1"]]
        scattered = [S["scat0"], S["scat1"]]
        lrow_loaded = [S["lrow_in0"], S["lrow_in1"]]
        GROUPS = TILES // (2 * E)
        ROUTE_GROUPS = 4
        LQ = TILES // 4
        N_SH = TILES
        N_ALL = TILES + BLOCKS

        def shared_blocks(engine, body, beside=None, first=None, second=None, middle=None, link=None,
                          links=(0, 0)):
            for n in range(ROUTE_GROUPS * GROUPS):
                body(n, n % 2, n // 2, n > 0, True)
                if beside:
                    beside(n)
                if first and n % GROUPS == GROUPS - 1:
                    first(n // GROUPS)
            before = link.n if link else 0
            with engine.Fori(0, E - ROUTE_GROUPS) as i:
                if link:
                    link.base = i * links[0]
                for k in range(GROUPS):
                    n = GROUPS * i + (GROUPS * ROUTE_GROUPS + k)
                    body(n, k % 2, (GROUPS // 2) * i + (GROUPS * ROUTE_GROUPS + k) // 2, True, True)
                if first:
                    first(i + ROUTE_GROUPS)
            if link:
                assert link.n - before == links[0], link.n - before
                link.base, link.n = 0, before + (E - ROUTE_GROUPS) * links[0]
            if middle:
                middle()
            before = link.n if link else 0
            with engine.Fori(0, E - 1) as i:
                if link:
                    link.base = i * links[1]
                for k in range(GROUPS):
                    body(GROUPS * i + (E * GROUPS + k), k % 2, (GROUPS // 2) * i + (E * GROUPS + k) // 2,
                         True, True)
                    if second:
                        second(i, k)
            if link:
                assert link.n - before == links[1], link.n - before
                link.base, link.n = 0, before + (E - 1) * links[1]
            for k in range(GROUPS):
                n = TILES - GROUPS + k
                body(n, n % 2, n // 2, True, n < TILES - 1)
                if second:
                    second(E - 1, k)

        def routed_blocks(engine, body):
            for k in range(4):
                body(N_SH + k, k % 2, (N_SH + k) // 2, k > 0, True)
            with engine.Fori(0, BLOCKS // 2 - 3) as i:
                for k in range(2):
                    body(2 * i + (N_SH + 4 + k), k, i + (N_SH // 2 + 2), True, True)
            for k in range(2):
                body(N_ALL - 2 + k, k, N_ALL // 2 - 1, True, k == 0)

        def power_scale(dve, link, r):
            link.link(dve, nc.vector.tensor_scalar(top[:, r], top[:, r], 1e-9, None, ALU.max))
            link.link(dve, nc.vector.tensor_scalar(top[:, r].bitcast(I32), top[:, r].bitcast(I32), 0x7F800000,
                                                   None, ALU.bitwise_and))
            link.link(dve, nc.vector.reciprocal(inv[:, r], top[:, r]))
            link.link(dve, nc.vector.tensor_scalar(wsc[:, r], inv[:, r], 2.0 ** 14, None, ALU.mult))

        def scale_columns(dve, link, r):
            power_scale(dve, link, r)
            nc.vector.tensor_scalar(silu_s[:, r:r + 1], top[:, r, 0:1], 2.0 ** -25, None, ALU.mult)
            nc.vector.tensor_scalar(h_s[:, r:r + 1], inv[:, r, 0:1], 2.0 ** -28, None, ALU.mult)
            link.link(dve, nc.vector.scalar_tensor_tensor(out=y_s[:, r:r + 1], in0=top[:, r, 0:1],
                                                          scalar=2.0 ** -11, in1=top[:, r, 1:2],
                                                          op0=ALU.mult, op1=ALU.mult))
            link.link(dve, nc.vector.tensor_tensor(y_s[:, r:r + 1], y_s[:, r:r + 1], top[:, r, 2:3], ALU.mult))
            nc.vector.tensor_copy(wsc[:, r, 3:4], wsc[:, r, 0:1]).then_inc(S["wlo_done" if r == 0 else "top_in"], 1)

        MATS = ((WG, CC * HID), (WU, CC * HID), (WD, HC * C))

        block = ctx.enter_context(nc.Block())

        @block.sync
        def _(sp):
            def load_x(b, par):
                sp.dma_start(x_in[:, par], xv[b]).then_inc(x_loaded[par], 16)

            def load_group(n, g):
                j = g // 2
                sp.wait_ge(S["qkl_done"], 4 * n + 2 * j + 2)
                sp.sem_inc(S["sp_passed"], 1)
                if some(4 * UN * n + UN * (g + 1) - 4 * UN):
                    sp.wait_ge(S["t_in"], 4 * UN * n + UN * (g + 1) - 4 * UN)
                    sp.sem_inc(S["sp_passed"], 1)
                r0 = 64 * (g % 2)
                for quad, (qs, ks) in enumerate(((qkh, qkh), (qkh, qkl), (qkl, qkh))):
                    for t in range(2):
                        sp.dma_start(q_op[32 * quad:32 * quad + 32, 2 * g + t, :],
                                     qs[r0 + 32 * t:r0 + 32 * t + 32, 2 * j, :]).then_inc(ops_in[g], 16)
                    for h in range(GH):
                        row = 32 * quad + HD * (h % 2)
                        sp.dma_start(k_op[row:row + HD, GH * g + h, :],
                                     ks[r0 + HD * h:r0 + HD * (h + 1), 2 * j + 1, :]).then_inc(ops_in[g], 16)

            sp.dma_start(wa[:, 0:2, :], w_attn.rearrange("(k p) n -> p k n", p=P)).then_inc(S["w_in"], 16)
            sp.wait_ge(S["pool_const"], 1)
            sp.dma_start(wa[0:1, 2, :], b_attn.unsqueeze(0)).then_inc(S["w_in"], 16)
            sp.dma_start(cs[:], rope.unsqueeze(0).broadcast_to([P, 2, 256])).then_inc(S["w_in"], 16)
            load_x(0, 0)
            load_x(1, 1)
            sp.dma_start(bvb[:], b_attn[2 * C:].unsqueeze(0).broadcast_to([P, C])).then_inc(S["const_in"], 16)
            sp.dma_start(bpb[:], b_proj.unsqueeze(0).broadcast_to([P, C])).then_inc(S["const_in"], 16)
            sp.dma_start(wp[:], w_proj.rearrange("(k p) n -> p k n", p=P)).then_inc(S["const_in"], 16)
            sp.wait_ge(S["pool_const"], 5)
            for g in range(2):
                load_group(0, g)
            sp.wait_ge(S["scales_done"], 1)
            for k, (src, n) in enumerate(((sWg, HID), (sWu, HID), (sWd, C))):
                sp.dma_start(shared_raw[:, k * CC * HID:(k + 1) * CC * HID].rearrange("p (c n) -> p c n", n=n),
                             src.rearrange("(c p) n -> p c n", p=P)).then_inc(S["shw_in"], 16)

            def store_half(b, j):
                sp.wait_ge(S["lo_done"], 2 * b + j + 1)
                sp.sem_inc(S["sp_passed"], 1)
                sp.dma_start(x1v[b, j], x1[:, j]).then_inc(x1_stored[j], 16)
                sp.dma_start(xhlv[b, j], xhl[:, j].rearrange("p t s c -> p t (s c)")
                             ).then_inc(xhl_stored[j], 16)

            def body(b, par, cur, prev, prev2, nxt, nxt2):
                if nxt2:
                    sp.wait_ge(S["xn_done"], b + 1)
                    sp.sem_inc(S["sp_passed"], 1)
                    load_x(b + 2, par)
                if prev:
                    if some(2 * (b - 1)):
                        sp.wait_ge(S["x1_done"], 2 * (b - 1))
                        sp.sem_inc(S["sp_passed"], 1)
                    sp.dma_start(xres[:], xv[b - 1]).then_inc(S["res_in"], 16)
                if cur:
                    load_group(b, 2)
                if prev2:
                    store_half(b - 2, 1)
                if cur:
                    load_group(b, 3)
                if nxt:
                    load_group(b + 1, 0)
                    load_group(b + 1, 1)
                if prev:
                    store_half(b - 1, 0)
                if not cur:
                    store_half(b - 1, 1)

            batches(sp, body)

            sp.wait_ge(S["lo_done"], 2 * NB)
            for stored in (*x1_stored, *xhl_stored):
                sp.wait_ge(stored, 16 * NB)
            sp.dma_start(gate_t[:], gate_w).then_inc(S["misc_in"], 16)
            sp.dma_start(lns[:, 0], ln_scale).then_inc(S["misc_in"], 16)
            sp.dma_start(lns[:, 1], ln_bias).then_inc(S["misc_in"], 16)

            def rows(n, par):
                if some(n - 1):
                    sp.wait_ge(S["xT_in"], n - 1)
                    sp.sem_inc(S["sp_passed"], 1)
                sp.dma_start(xrow[:, par], xhl_d[bass.ds(n * P, P), :]).then_inc(row_loaded[par], 16)

            def residual_rows(n, par):
                if some(n - 1):
                    sp.wait_ge(S["y_out"], n - 1)
                    sp.sem_inc(S["sp_passed"], 1)
                sp.dma_start(x1t[:, par], x1_d[bass.ds(n * P, P), :]).then_inc(x1_loaded[par], 16)

            def logit_rows(q, par):
                if some(2 * q - 2):
                    sp.wait_ge(S["lxT_in"], 2 * q - 2)
                    sp.sem_inc(S["sp_passed"], 1)
                sp.dma_start(lrow[:, par], xhl_d[bass.ds(q * 4 * P, 4 * P), :].rearrange("(t p) n -> p t n", p=P)
                             ).then_inc(lrow_loaded[par], 16)

            logit_rows(0, 0)
            logit_rows(1, 1)
            with sp.Fori(1, LQ // 2) as i:
                for par in range(2):
                    logit_rows(2 * i + par, par)
            rows(0, 0)
            rows(1, 1)
            residual_rows(0, 0)
            sp.wait_ge(S["bconst"], 1)
            sp.dma_start(tok_d.rearrange("(p n) o -> p (n o)", p=P), no_tok[:].rearrange("p n o -> p (n o)")
                         ).then_inc(S["zero_st"], 16)
            sp.dma_start(xhl_d[NTOK:, :], zero_h[:]).then_inc(S["spare_st"], 16)
            sp.dma_start(out[NTOK:, :], zero_h[:].bitcast(F32)).then_inc(S["spare_st"], 16)

            def body(n, par, half, prev, nxt):
                if isinstance(n, int) and n >= TILES - 2:
                    pass
                else:
                    rows(n + 2, par)
                if nxt:
                    residual_rows(n + 1, 1 - par)
                if prev:
                    sp.wait_ge(S["y_out"], n)
                    sp.sem_inc(S["sp_passed"], 1)
                    sp.dma_start(out[bass.ds((n - 1) * P, P), :], ysb[:, 1 - par]).then_inc(y_stored[1 - par], 16)

            def load_expert(e):
                if some(48 * e):
                    sp.wait_ge(S["w_exp"], 48 * e)
                    sp.sem_inc(S["sp_passed"], 1)
                for (off, n), src in zip(MATS, (Wg, Wu, Wd)):
                    dst = wraw[:, bass.ds(e + 1, 1), off // 2:off // 2 + n]
                    w = src[bass.ds(e, 1)].rearrange("o (c p) n -> p (o c) n", p=P)
                    sp.dma_start(dst.rearrange("p o (c n) -> p (o c) n", n=w.shape[2]), w).then_inc(S["w_exp"], 16)

            load_expert(0)
            for n in range(ROUTE_GROUPS * GROUPS):
                body(n, n % 2, n // 2, n > 0, True)
                if n % GROUPS == GROUPS - 1:
                    load_expert(n // GROUPS + 1)
            with sp.Fori(ROUTE_GROUPS, E - 1) as i:
                for k in range(GROUPS):
                    body(GROUPS * i + k, k % 2, 0, True, True)
                load_expert(i + 1)
            with sp.Fori(E - 1, 2 * E - 1) as i:
                for k in range(GROUPS):
                    body(GROUPS * i + k, k % 2, 0, True, True)
            for k in range(GROUPS):
                n = TILES - GROUPS + k
                body(n, n % 2, n // 2, True, n < TILES - 1)
            n = TILES - 1
            sp.wait_ge(S["y_out"], n + 1)
            sp.dma_start(out[n * P:(n + 1) * P, :], ysb[:, n % 2]).then_inc(y_stored[n % 2], 16)

            sp.wait_ge(scattered[0], 16 * TILES)
            sp.wait_ge(scattered[1], 16 * TILES)
            sp.dma_start(tok_rows[:].rearrange("p n o -> p (n o)"), tok_d.rearrange("(p n) o -> p (n o)", p=P)
                         ).then_inc(S["rows_in"], 16)

        @block.gpsimd
        def _(pool):
            link = Count(S["pool_link"])
            nc.gpsimd.memset(wa[:, 2, :], 0.0).then_inc(S["pool_const"], 1)
            link.link(pool, nc.gpsimd.memset(ident[:], 0.0))
            link.link(pool, nc.gpsimd.affine_select(
                out=ident[:], in_=ident[:], compare_op=ALU.not_equal, fill=1.0, base=0,
                pattern=[[-1, P]], channel_multiplier=1))
            nc.gpsimd.tensor_copy(ident_b[:], ident[:])
            nc.gpsimd.tensor_copy(ident_h[:], ident[:])
            nc.gpsimd.memset(one[:], 1.0)
            nc.gpsimd.memset(neghalf[:], -0.5).then_inc(S["pool_const"], 1)
            link.link(pool, nc.gpsimd.memset(mask[:], 0.0))
            nc.gpsimd.affine_select(out=mask[:], in_=mask[:], compare_op=ALU.is_ge, fill=MASKED, base=0,
                                    pattern=[[-1, P]], channel_multiplier=1).then_inc(S["pool_const"], 1)
            nc.gpsimd.memset(q_op[:], 0.0).then_inc(S["pool_const"], 1)
            link.link(pool, nc.gpsimd.memset(k_op[:], 0.0))
            k_sel = k_op[96:128].rearrange("p (g h) n -> p g h n", h=GH)
            nc.gpsimd.affine_select(out=k_sel, in_=k_sel, compare_op=ALU.not_equal, fill=-SHIFT_UNIT, base=0,
                                    pattern=[[0, NG], [-1, GH], [0, T]],
                                    channel_multiplier=1).then_inc(S["pool_const"], 1)
            pool.wait_ge(S["pool_const"], 5)
            pool.wait_ge(S["attn_w"], 1)
            nc.gpsimd.partition_all_reduce(qk_top[:], qk_max[:], P, RMAX).then_inc(S["qk_topped"], 1)

            def normalise(n, par, t):
                if t == 0:
                    pool.wait_ge(S["var_done"], n + 1)
                    pool.sem_inc(S["pool_passed"], 1)
                    nc.gpsimd.tensor_tensor(rstd[:], mv[:, :, 1], neghalf[:], ALU.pow).then_inc(S["rstd_done"], 1)
                    pool.wait_ge(S["rstd_done"], n + 1)
                    pool.sem_inc(S["pool_passed"], 1)
                    if some(2 * n):
                        pool.wait_ge(S["xnT_in"], 2 * n)
                        pool.sem_inc(S["pool_passed"], 1)
                last = nc.gpsimd.tensor_scalar(xn[:, t], x_in[:, par, t], mv[:, t, 0:1], rstd[:, t:t + 1],
                                               ALU.subtract, ALU.mult)
                if t == NT - 1:
                    last.then_inc(S["xn_done"], 1)

            for t in range(NT):
                normalise(0, 0, t)
            for t in range(NT):
                normalise(1, 1, t)

            def residual_rstd(bp, j):
                pool.wait_ge(S["varb_done"], 2 * bp + j + 1)
                pool.sem_inc(S["pool_passed"], 1)
                nc.gpsimd.tensor_tensor(rstdb[:], mvb[:, :, 1], neghalf[:, 0:2],
                                        ALU.pow).then_inc(S["rstdb_done"], 1)

            def select(G, u, half):
                pool.wait_ge(S["exp_done"], UN * G + u + 1)
                pool.sem_inc(S["pool_passed"], 1)
                bankv = prob[:, half, u, :]
                if u < 4:
                    v, pat = bankv[:, 0:P], [[1, P]]
                elif u < 8:
                    v, pat = bankv.rearrange("p (s n) -> p s n", n=P)[:, 0:4:3, :], [[0, 2], [1, P]]
                else:
                    v, pat = bankv.rearrange("p (s n) -> p s n", n=P)[:, 0:4:2, :], [[0, 2], [1, P]]
                nc.gpsimd.affine_select(out=v, in_=v, compare_op=ALU.is_ge, fill=0.0, base=0, pattern=pat,
                                        channel_multiplier=-1).then_inc(S["sel_done"], 1)

            def body(b, par, cur, prev, prev2, nxt, nxt2):
                for g in range(NG):
                    G = 4 * b + g
                    has1 = (cur or g < 1) and (prev or g >= 1)
                    has2 = (cur or g < 2) and (prev or g >= 2)
                    for s in range(UN):
                        if s >= LAG - UN and has1:
                            select(G - 1, s + UN - LAG, (g - 1) % 2)
                        elif s < LAG - UN and has2:
                            select(G - 2, s + 2 * UN - LAG, g % 2)
                        if prev:
                            for t in range(NT):
                                if (g, s) == X_BIAS[t]:
                                    if t == 0:
                                        pool.wait_ge(S["const_in"], 48)
                                        pool.wait_ge(S["res_in"], 16 * b)
                                        pool.sem_inc(S["pool_passed"], 1)
                                    last = nc.gpsimd.tensor_tensor(xres[:, t], xres[:, t], bpb[:], ALU.add)
                                    if t == NT - 1:
                                        last.then_inc(S["xb_done"], 1)
                        if nxt2:
                            for t in range(NT):
                                if (g, s) == NORMALISE[t]:
                                    normalise(b + 2, par, t)
                        for j, bp, there in layernorm_of(b, prev, prev2):
                            if there and (g, s) == RSTD_B[j]:
                                residual_rstd(bp, j)
                if not cur:
                    residual_rstd(b - 1, 1)

            batches(pool, body)

            pool.wait_ge(S["lo_done"], 2 * NB)
            for stored in (*x1_stored, *xhl_stored):
                pool.wait_ge(stored, 16 * NB)
            nc.gpsimd.memset(zero_h[:], 0.0)
            nc.gpsimd.memset(no_tok[:, :, 1], 0)
            nc.gpsimd.iota(no_tok[:, :, 0], [[0, BLOCKS]], base=NTOK, channel_multiplier=1).then_inc(S["bconst"], 1)
            nc.gpsimd.memset(ones_f[:], 1.0)
            nc.gpsimd.memset(ones_b[:], 1.0)
            nc.gpsimd.memset(zeros[:], 0.0)
            nc.gpsimd.memset(rhalf[:], -0.5)
            nc.gpsimd.iota(iota_e[:], [[1, E]], base=0, channel_multiplier=0, allow_small_or_imprecise_dtypes=True)
            nc.gpsimd.iota(iota_j[:], [[P, TILES]], base=0, channel_multiplier=0,
                           allow_small_or_imprecise_dtypes=True)
            for k in range(2):
                nc.gpsimd.iota(tok_w[:, :, k, 0], [[P, TILES]], base=0, channel_multiplier=1)
            link.link(pool, nc.gpsimd.memset(before_b[:], 1.0))
            link.link(pool, nc.gpsimd.affine_select(out=before_b[:], in_=before_b[:], compare_op=ALU.is_gt,
                                                    fill=0.0, base=0, pattern=[[1, P]], channel_multiplier=-1))
            nc.gpsimd.iota(iota_b[:], [[1, BLOCKS]], base=0, channel_multiplier=0,
                           allow_small_or_imprecise_dtypes=True).then_inc(S["bconst"], 1)
            pool.wait_ge(S["bconst"], 2)
            pool.wait_ge(S["gprep"], 1)
            nc.gpsimd.partition_all_reduce(top[:, 1:3, :], top[:, 1:3, :], P, RMAX).then_inc(S["topped"], 1)
            pool.wait_ge(S["route_var"], 1)
            nc.gpsimd.tensor_tensor(rvar[:, 1], rvar[:, 0], rhalf[:], ALU.pow).then_inc(S["route_rstd"], 1)
            pool.wait_ge(S["zero_st"], 16)
            pool.wait_ge(S["slots_done"], 1)
            pool.wait_ge(S["weights_done"], 1)

            def scatter(t, par, i):
                if some(32 * i):
                    pool.wait_ge(scattered[par], 32 * i)
                    pool.sem_inc(S["pool_passed"], 1)
                nc.gpsimd.tensor_copy(to_col[:, par], dest_i[:, bass.ds(t, 1), :].rearrange("p o k -> p (o k)"))
                nc.gpsimd.tensor_copy(tw_col[:, par], tok_w[:, bass.ds(t, 1)].rearrange("p o k w -> p (o k w)")
                                      ).then_inc(S["scol"], 1)
                pool.wait_ge(S["scol"], t + 1)
                pool.sem_inc(S["pool_passed"], 1)
                for k in range(2):
                    pool.indirect_dma_start(
                        out=tok_d, out_offset=bass.IndirectOffsetOnAxis(ap=to_col[:, par, k:k + 1], axis=0),
                        in_=tw_col[:, par, 2 * k:2 * k + 2], in_offset=None).then_inc(scattered[par], 16)

            for par in range(2):
                scatter(par, par, 0)
            with pool.Fori(1, BEFORE_MAX // 2) as i:
                for par in range(2):
                    scatter(2 * i + par, par, i)
            pool.wait_ge(S["wmax_done"], E)
            nc.gpsimd.partition_all_reduce(top[:, 0, 0:3], run3[:], P, RMAX).then_inc(S["topped"], 1)
            with pool.Fori(BEFORE_MAX // 2, TILES // 2) as i:
                for par in range(2):
                    scatter(2 * i + par, par, i)
            pool.wait_ge(S["rows_in"], 16)
            pool.wait_ge(S["spare_st"], 32)

            def gather(n, par):
                pool.wait_ge(S["xT_in"], n - 1)
                pool.sem_inc(S["pool_passed"], 1)
                nc.gpsimd.tensor_copy(ga_col[:, par, :], tok_rows[:, bass.ds(n - N_SH, 1), 0]
                                      ).then_inc(S["gcol"], 1)
                pool.wait_ge(S["gcol"], n - (N_SH - 1))
                pool.sem_inc(S["pool_passed"], 1)
                pool.indirect_dma_start(
                    out=xrow[:, par], out_offset=None, in_=xhl_d,
                    in_offset=bass.IndirectOffsetOnAxis(ap=ga_col[:, par, :], axis=0),
                ).then_inc(row_gathered[par], 16)

            def add(n, par):
                nc.gpsimd.tensor_copy(ad_col[:, par, :], tok_rows[:, bass.ds(n - N_SH, 1), 0]
                                      ).then_inc(S["acol"], 1)
                pool.wait_ge(S["acol"], n - (N_SH - 1))
                pool.sem_inc(S["pool_passed"], 1)
                if some(n - N_SH):
                    pool.wait_ge(S["y_added"], 16 * (n - N_SH))
                    pool.sem_inc(S["pool_passed"], 1)
                pool.wait_ge(S["y_out"], n + 1)
                pool.sem_inc(S["pool_passed"], 1)
                pool.indirect_dma_start(
                    out=out, out_offset=bass.IndirectOffsetOnAxis(ap=ad_col[:, par, :], axis=0),
                    in_=ysb[:, par], in_offset=None, compute_op=ALU.add).then_inc(S["y_added"], 16)

            for n in range(N_SH, N_SH + 4):
                gather(n, n % 2)
            for par in range(2):
                pool.wait_ge(y_stored[par], 16 * (TILES // 2))
            for n in range(N_SH, N_SH + 2):
                gather(n + 4, n % 2)
                add(n, n % 2)
            with pool.Fori(0, BLOCKS // 2 - 3) as i:
                for par in range(2):
                    gather(2 * i + (N_SH + 6 + par), par)
                    add(2 * i + (N_SH + 2 + par), par)
            for n in range(N_ALL - 4, N_ALL):
                add(n, n % 2)
            pool.wait_ge(S["y_added"], 16 * BLOCKS)

        @block.scalar
        def _(act):
            def xn_high(n, c):
                act.wait_ge(S["xnT_in"], 2 * n + c + 1)
                if some(4 * n):
                    act.wait_ge(S["qk_in"], 4 * n)
                nc.scalar.copy(xh[:, c, :], ps_q[:]).then_inc(S["xh_done"], 1)

            def qk_high(n, i):
                act.wait_ge(S["qk_in"], 4 * n + i + 1)
                for g in (0, 1) if i < 2 else (2, 3):
                    if some(LOADS * n):
                        act.wait_ge(ops_in[g], LOADS * n)
                nc.scalar.activation(qkh[:, i, :], ps_q[:], ACT.Identity,
                                     bias=bcol[:, i:i + 1]).then_inc(S["qkh_done"], 1)

            def prologue():
                act.wait_ge(S["pool_const"], 5)
                act.wait_ge(S["scales_done"], 1)
                for c in range(2):
                    xn_high(0, c)
                for i in range(4):
                    qk_high(0, i)

            prologue()

            def exponentials(G, u, half):
                if u == 0 and some(G - 1):
                    act.wait_ge(S["pv_in"], G - 1)
                act.wait_ge(S["t_in"], UN * G + u + 1)
                nc.scalar.activation(prob[:, half, u, :], ps_t[u % 2][:], ACT.Exp,
                                     scale=exp_scale[:]).then_inc(S["exp_done"], 1)

            def residual_high(bp, j):
                act.wait_ge(S["xf_done"], 2 * bp + j + 1)
                if some(16 * bp):
                    act.wait_ge(xhl_stored[j], 16 * bp)
                nc.scalar.activation(xhl[:, j, :, 0, :], xf[:], ACT.Copy, scale=X_SCALE
                                     ).then_inc(S["hi_done"], 1)

            def body(b, par, cur, prev, prev2, nxt, nxt2):
                for g in range(NG):
                    G = 4 * b + g
                    has1 = (cur or g < 1) and (prev or g >= 1)
                    has2 = (cur or g < 2) and (prev or g >= 2)
                    for s in range(UN):
                        if s == M_ROWS and has1:
                            act.wait_ge(S["m_in"], G)
                            pair = 2 * ((g - 1) % 4)
                            nc.scalar.activation(
                                q_op[96:96 + GH, pair:pair + 2, :],
                                ps_m[0:GH, :].unsqueeze(1).broadcast_to([GH, 2, T]),
                                ACT.Copy, scale=1.0 / SHIFT_UNIT).then_inc(S["m_done"], 1)
                        if s >= LAG - UN and has1:
                            exponentials(G - 1, s + UN - LAG, (g - 1) % 2)
                        elif s < LAG - UN and has2:
                            exponentials(G - 2, s + 2 * UN - LAG, g % 2)
                        if s == O_OUT and has2:
                            opar = par if g >= 2 else 1 - par
                            nb = b if g >= 2 else b - 1
                            act.wait_ge(S["pv_in"], G - 1)
                            if some(4 * (nb - 1)):
                                act.wait_ge(S["ot_in"], 4 * (nb - 1))
                            nc.scalar.copy(o_t[:, opar, (g - 2) % 4, :], ps_o[:]).then_inc(S["o_done"], 1)
                        if nxt:
                            for c in range(2):
                                if (g, s) == XN_HIGH[c]:
                                    xn_high(b + 1, c)
                            for i in range(4):
                                if (g, s) == QK_HIGH[i]:
                                    qk_high(b + 1, i)
                        if prev:
                            for j in range(2):
                                if (g, s) == Y_OUT[j]:
                                    k = 2 * (b - 1) + j
                                    act.wait_ge(S["yT_in"], k + 1)
                                    if some(k):
                                        act.wait_ge(S["pr_in"], k)
                                    nc.scalar.copy(y_t[:].rearrange("p t c n -> p (t c n)"),
                                                   ps_y[:]).then_inc(S["yT_done"], 1)
                        for j, bp, there in layernorm_of(b, prev, prev2):
                            if there and (g, s) == HIGH[j]:
                                residual_high(bp, j)
                if not cur:
                    residual_high(b - 1, 1)

            batches(act, body)

            act.wait_ge(S["top_in"], 1)
            for m, (off, n) in enumerate(MATS):
                nc.scalar.activation(wsh[:, off:off + n], shared_raw[:, off // 2:off // 2 + n], ACT.Copy,
                                     scale=wsc[:, 1, m:m + 1]).then_inc(S["shsplit_done"], 1)

            def take_pair(r):
                act.wait_ge(S["lxT_in"], r + 1)
                if some(r - 1):
                    act.wait_ge(S["lg_in"], r - 1)
                nc.scalar.copy(xtl[:, 1].rearrange("p t c n -> p (t c n)"), ps_lx[1]).then_inc(S["lxt_done1"], 1)

            take_pair(1)
            with act.Fori(1, LQ) as q:
                take_pair(2 * q + 1)

            def silu(n, par, r):
                act.wait_ge(S["g_in"], n + 1)
                if some(n - 1):
                    act.wait_ge(S["h_done"], n - 1)
                nc.scalar.activation(sg[:, par], ps_g[:], ACT.Silu, scale=silu_s[:, r:r + 1]
                                     ).then_inc(S["sg_done"], 1)

            def high(n):
                act.wait_ge(S["hT_in"], n + 1)
                if some(n):
                    act.wait_ge(S["yp_in"], n)
                nc.scalar.copy(hth[:].rearrange("p c n -> p (c n)"), ps_h[:]).then_inc(S["hh_done"], 1)

            def shared(n, par, half, prev, nxt):
                if prev:
                    high(n - 1)
                silu(n, par, 1)

            def second(e, k):
                if k == len(MATS):
                    return
                off, n = MATS[k]
                act.wait_ge(S["wlo_done"], 3 * e + 1)
                nc.scalar.activation(wbuf[:, bass.ds(e * SLOT + off, n)],
                                     wraw[:, bass.ds(e + 1, 1), off // 2:off // 2 + n],
                                     ACT.Copy, scale=wsc[:, 0, k:k + 1]).then_inc(S["whi_done"], 1)

            def beside(n):
                if n == EXP_AT:
                    act.wait_ge(S["exp_in"], 1)
                    nc.scalar.activation(tmp[:], tmp[:], ACT.Exp)
                    nc.scalar.activation(m12[:, 3], m12[:, 2], ACT.Exp).then_inc(S["exp_out"], 1)

            shared_blocks(act, shared, beside, second=second)
            high(N_SH - 1)
            act.wait_ge(S["row_w_done"], 1)
            for par in range(2):
                act.wait_ge(y_stored[par], 16 * (TILES // 2))

            def result(n, par):
                act.wait_ge(S["yp_in"], n + 1)
                if some(n - N_SH - 1):
                    act.wait_ge(S["y_added"], 16 * (n - (N_SH + 1)))
                nc.scalar.activation(ysb[:, par], ps_z[:, 0:C], ACT.Copy, scale=row_w[:, bass.ds(n - N_SH, 1)]
                                     ).then_inc(S["y_out"], 1)

            def routed(n, par, half, prev, nxt):
                if prev:
                    high(n - 1)
                silu(n, par, 0)
                if prev:
                    result(n - 1, 1 - par)

            routed_blocks(act, routed)
            high(N_ALL - 1)
            result(N_ALL - 1, (N_ALL - 1) % 2)

        @block.vector
        def _(dve):
            link = Count(S["dve_link"])

            def stats(n, par, j):
                if j == 0:
                    dve.wait_ge(x_loaded[par], 8 * n + 16 - 8 * par)
                    if some(n):
                        dve.wait_ge(S["xn_done"], n)
                for t in (2 * j, 2 * j + 1):
                    last = nc.vector.bn_stats(st6[:, t], x_in[:, par, t])
                if j == 1:
                    last.then_inc(S["stats_taken"], 1)

            def variance(n):
                dve.wait_ge(S["stats_taken"], n + 1)
                dve.sem_inc(S["dve_passed"], 1)
                for t in range(NT):
                    last = nc.vector.bn_aggr(mv[:, t], st6[:, t])
                link.link(dve, last)
                nc.vector.tensor_scalar(mv[:, :, 1], mv[:, :, 1], EPS, None,
                                        ALU.add).then_inc(S["var_done"], 1)

            def xn_low(n, c):
                dve.wait_ge(S["xh_done"], 2 * n + c + 1)
                nc.vector.tensor_tensor(xl[:, c, :], ps_q[:], xh[:, c, :].bitcast(F32),
                                        ALU.subtract).then_inc(S["xl_done"], 1)

            def qk_low(n, i):
                dve.wait_ge(S["qkh_done"], 4 * n + i + 1)
                nc.vector.scalar_tensor_tensor(out=qkl[:, i, :], in0=ps_q[:], scalar=bcol[:, i:i + 1],
                                               in1=qkh[:, i, :], op0=ALU.add,
                                               op1=ALU.subtract).then_inc(S["qkl_done"], 1)

            def values(n, par, j):
                dve.wait_ge(S["v_in"], 2 * n + j + 1)
                if some(4 * (n - 1)):
                    dve.wait_ge(S["pv_in"], 4 * (n - 1))
                for t in range(2):
                    last = nc.vector.tensor_tensor(
                        v_op[:, par, 2 * j + t, :, 0:HD],
                        ps_q[:, 256 * t:256 * t + 256].rearrange("p (h d) -> p h d", d=HD),
                        bvb[:].rearrange("p (h d) -> p h d", d=HD), ALU.add)
                last.then_inc(S["v_done"], 1)

            def prologue():
                for par in range(2):
                    nc.vector.memset(v_op[:, par, :, :, HD:], 0.0)
                link.link(dve, nc.vector.memset(mx[:], 0.0))
                link.link(dve, nc.vector.memset(v_op[:, :, :, :, HD:HD + 1].rearrange(
                    "p a t h d -> p (a t h) d"), 1.0))
                stats(0, 0, 0)
                stats(0, 0, 1)
                variance(0)
                dve.wait_ge(S["w_in"], 48)
                ev = wa[:, :, 0:512].rearrange("p k (i e) -> p k i e", e=2)[:, :, :, 0]
                od = wa[:, :, 0:512].rearrange("p k (i e) -> p k i e", e=2)[:, :, :, 1]
                cosv = cs[:, 0:1, :].broadcast_to([P, 3, 256])
                sinv = cs[:, 1:2, :].broadcast_to([P, 3, 256])
                nc.vector.tensor_tensor(rope_t[:, 0], ev, sinv, ALU.mult)
                link.link(dve, nc.vector.tensor_tensor(rope_t[:, 1], od, sinv, ALU.mult))
                nc.vector.tensor_tensor(ev, ev, cosv, ALU.mult)
                link.link(dve, nc.vector.tensor_tensor(od, od, cosv, ALU.mult))
                nc.vector.tensor_tensor(ev, ev, rope_t[:, 1], ALU.subtract)
                link.link(dve, nc.vector.tensor_tensor(od, od, rope_t[:, 0], ALU.add))
                for s in range(2):
                    last = nc.vector.tensor_reduce(qk_max[:, s:s + 1], wa[:, :, 256 * s:256 * s + 256],
                                                   mybir.AxisListType.XY, ALU.max, apply_absolute_value=True)
                last.then_inc(S["attn_w"], 1)
                dve.wait_ge(S["qk_topped"], 1)
                link.link(dve, nc.vector.tensor_scalar(qk_top[:], qk_top[:], 1e-30, None, ALU.max))
                link.link(dve, nc.vector.tensor_scalar(qk_top[:].bitcast(I32), qk_top[:].bitcast(I32),
                                                       0x7F800000, None, ALU.bitwise_and))
                link.link(dve, nc.vector.reciprocal(qk_inv[:], qk_top[:]))
                link.link(dve, nc.vector.tensor_scalar(qk_scale[:], qk_inv[:], 16.0, None, ALU.mult))
                nc.vector.scalar_tensor_tensor(out=exp_scale[:], in0=qk_top[:, 0:1], scalar=1.0 / 256,
                                               in1=qk_top[:, 1:2], op0=ALU.mult, op1=ALU.mult)
                for s in range(2):
                    w_s = wa[:, :, 256 * s:256 * s + 256]
                    last = nc.vector.tensor_scalar(w_s, w_s, qk_scale[:, s:s + 1], None, ALU.mult)
                last.then_inc(S["attn_w"], 1)
                dve.wait_ge(S["biascols"], 1)
                nc.vector.tensor_copy(bcol[:], ps_m[:, 0:4])
                link.link(dve, nc.vector.tensor_copy(wah[:], wa[:, 0:2, :]))
                nc.vector.tensor_tensor(wal[:], wa[:, 0:2, :], wah[:].bitcast(F32),
                                        ALU.subtract).then_inc(S["scales_done"], 1)
                stats(1, 1, 0)
                stats(1, 1, 1)
                variance(1)

            def prologue_qkv():
                dve.wait_ge(S["const_in"], 48)
                for c in range(2):
                    xn_low(0, c)
                for i in range(2):
                    qk_low(0, i)
                for j in range(2):
                    values(0, 0, j)
                for i in range(2, 4):
                    qk_low(0, i)

            prologue()
            prologue_qkv()

            def row_max(G, g, u):
                dve.wait_ge(S["s_in"], UN * G + u + 1)
                if u == 0:
                    if some(G - 1):
                        dve.wait_ge(S["m_in"], G - 1)
                src, dst = ps_s[u % 2], mx[:, g % 2]

                def top(lo, n, out):
                    return nc.vector.tensor_reduce(out, src[:, lo:lo + n], AX_X, ALU.max)

                if u < 4:
                    last = top(0, 512, dst[:, 3, u:u + 1])
                elif u < 8:
                    top(0, 384, dst[:, 2, u - 4:u - 3])
                    last = top(384, 128, dst[:, 0, u - 4:u - 3])
                else:
                    c = 2 * (u - 8)
                    last = nc.vector.tensor_reduce(dst[:, 1, c:c + 2],
                                                   src[:].rearrange("p (h n) -> p h n", h=2), AX_X, ALU.max)
                last.then_inc(S["max_done"], 1)

            def divide(bp, q):
                k = 4 * bp + q
                dve.wait_ge(S["ot_in"], k + 1)
                ov = ps_y[:].rearrange("p (h d) -> p h d", d=32)
                link.link(dve, nc.vector.reciprocal(rec[:, q % 2], ov[:, :, HD]))
                if some(2 * bp + q // 2):
                    dve.wait_ge(S["yT_in"], 2 * bp + q // 2)
                nc.vector.tensor_tensor(y[:, q % 2].rearrange("p (h d) -> p h d", d=HD), ov[:, :, 0:HD],
                                        rec[:, q % 2].unsqueeze(2).broadcast_to([P, H, HD]),
                                        ALU.mult).then_inc(S["y_done"], 1)

            def residual(bp, j):
                k = 2 * bp + j
                dve.wait_ge(S["pr_in"], k + 1)
                dve.wait_ge(S["xb_done"], bp + 1)
                if some(16 * bp):
                    dve.wait_ge(x1_stored[j], 16 * bp)
                nc.vector.tensor_tensor(x1[:, j].rearrange("p t c -> p (t c)"), ps_m[:],
                                        xres[:, 2 * j:2 * j + 2].rearrange("p t c -> p (t c)"), ALU.add
                                        ).then_inc(S["x1_done"], 1)

            def residual_stats(bp, j):
                dve.wait_ge(S["x1_done"], 2 * bp + j + 1)
                for t in range(2):
                    last = nc.vector.bn_stats(st6b[:, t], x1[:, j, t])
                last.then_inc(S["x1_taken"], 1)

            def residual_variance(bp, j):
                dve.wait_ge(S["x1_taken"], 2 * bp + j + 1)
                dve.sem_inc(S["dve_passed"], 1)
                for t in range(2):
                    last = nc.vector.bn_aggr(mvb[:, t], st6b[:, t])
                link.link(dve, last)
                link.link(dve, nc.vector.tensor_copy(var_all[:, bass.ds(NT * bp + 2 * j, 2)], mvb[:, :, 1]))
                nc.vector.tensor_scalar(mvb[:, :, 1], mvb[:, :, 1], EPS, None,
                                        ALU.add).then_inc(S["varb_done"], 1)

            def rows(bp, j):
                k = 2 * bp + j
                dve.wait_ge(S["rstdb_done"], k + 1)
                if some(k):
                    dve.wait_ge(S["lo_done"], k)
                for t in range(2):
                    last = nc.vector.tensor_scalar(xf[:, t], x1[:, j, t], mvb[:, t, 0:1], rstdb[:, t:t + 1],
                                                   ALU.subtract, ALU.mult)
                last.then_inc(S["xf_done"], 1)

            def low(bp, j):
                k = 2 * bp + j
                dve.wait_ge(S["hi_done"], k + 1)
                nc.vector.scalar_tensor_tensor(out=xhl[:, j, :, 1, :], in0=xf[:], scalar=X_SCALE,
                                               in1=xhl[:, j, :, 0, :], op0=ALU.mult,
                                               op1=ALU.subtract).then_inc(S["lo_done"], 1)

            def body(b, par, cur, prev, prev2, nxt, nxt2):
                for g in range(NG):
                    G = 4 * b + g
                    for s in range(UN):
                        if cur:
                            row_max(G, g, s)
                        if nxt:
                            for c in range(2):
                                if (g, s) == XN_LOW[c]:
                                    xn_low(b + 1, c)
                            for i in range(4):
                                if (g, s) == QK_LOW[i]:
                                    qk_low(b + 1, i)
                            for j in range(2):
                                if (g, s) == VALUES[j]:
                                    values(b + 1, 1 - par, j)
                        if nxt2:
                            for j in range(2):
                                if (g, s) == STATS[j]:
                                    stats(b + 2, par, j)
                            if (g, s) == VARIANCE:
                                variance(b + 2)
                        if prev:
                            for q in range(NT):
                                if (g, s) == DIVIDE[q]:
                                    divide(b - 1, q)
                            for j in range(2):
                                if (g, s) == X1[j]:
                                    residual(b - 1, j)
                                if (g, s) == X1_STATS[j]:
                                    residual_stats(b - 1, j)
                        for j, bp, there in layernorm_of(b, prev, prev2):
                            if there and (g, s) == X1_VARIANCE[j]:
                                residual_variance(bp, j)
                            if there and (g, s) == ROWS[j]:
                                rows(bp, j)
                            if there and (g, s) == LOW[j]:
                                low(bp, j)
                if not cur:
                    residual_variance(b - 1, 1)
                    rows(b - 1, 1)
                    low(b - 1, 1)

            batches(dve, body, link, DVE_LINKS)

            V = nc.vector
            ranks = ps_r[0][:].rearrange("p (t e) -> p t e", e=E)
            inclt = incl[:].rearrange("p e t -> p t e")

            def per_tile(v):
                return v.unsqueeze(2).broadcast_to([P, TILES, E])

            def per_expert(v):
                return v.unsqueeze(1).broadcast_to([P, TILES, E])

            def step(instruction):
                link.link(dve, instruction)

            def route_logits():
                step(V.tensor_scalar(rvar[:, 0], var_all[:], EPS, None, ALU.add))
                step(V.reciprocal(rvar[:, 1], rvar[:, 0]))
                step(V.tensor_tensor(rvar[:, 0], rvar[:, 1], var_all[:], ALU.mult))
                V.tensor_scalar(rvar[:, 0], rvar[:, 0], EPS, None, ALU.add).then_inc(S["route_var"], 1)
                dve.wait_ge(S["route_rstd"], 1)
                dve.wait_ge(S["lg_in"], TILES // 2)
                pl = ps_l[:].rearrange("p (t e) -> p t e", e=E)
                step(V.scalar_tensor_tensor(out=lg[:], in0=pl, scalar=lg_s[:], in1=per_tile(rvar[:, 1]),
                                            op0=ALU.mult, op1=ALU.mult))
                step(V.tensor_tensor(lg[:], lg[:], per_expert(sgb[:, 1]), ALU.add))

            def choose_expert(k, src):
                step(V.tensor_reduce(m12[:, k], src[:], AX_X, ALU.max))
                step(V.tensor_tensor(tmp[:], src[:], per_tile(m12[:, k]), ALU.is_equal))
                step(V.scalar_tensor_tensor(out=tmp[:], in0=tmp[:], scalar=-float(E), in1=per_expert(iota_e[:]),
                                            op0=ALU.mult, op1=ALU.add))
                step(V.tensor_reduce(rw[:, 0], tmp[:], AX_X, ALU.min))
                step(V.tensor_scalar(rw[:, 0], rw[:, 0], float(E), None, ALU.add))
                step(V.tensor_tensor(oh[:, k], per_expert(iota_e[:]), per_tile(rw[:, 0]), ALU.is_equal))

            def choose_first():
                choose_expert(0, lg)
                step(V.scalar_tensor_tensor(out=lg2[:], in0=oh[:, 0], scalar=MASKED, in1=lg[:], op0=ALU.mult,
                                            op1=ALU.add))

            def choose_second():
                choose_expert(1, lg2)

            def choose():
                V.tensor_tensor(sel[:], oh[:, 0], oh[:, 1], ALU.add).then_inc(S["sel_ready"], 1)
                step(V.tensor_tensor(tmp[:], lg[:], per_tile(m12[:, 0]), ALU.subtract))
                V.tensor_tensor(m12[:, 2], m12[:, 1], m12[:, 0], ALU.subtract).then_inc(S["exp_in"], 1)

            def weigh():
                dve.wait_ge(S["exp_out"], 1)
                step(V.tensor_reduce(rw[:, 0], tmp[:], AX_X, ALU.add))
                step(V.reciprocal(rw[:, 1], rw[:, 0]))
                step(V.tensor_tensor(rw[:, 2], m12[:, 3], rw[:, 1], ALU.mult))
                step(V.scalar_tensor_tensor(out=rw[:, 3], in0=rw[:, 1], scalar=EPS, in1=rw[:, 2], op0=ALU.add,
                                            op1=ALU.add))
                step(V.reciprocal(rw[:, 0], rw[:, 3]))
                V.tensor_tensor(tok_w[:, :, 0, 1].bitcast(F32), rw[:, 1], rw[:, 0], ALU.mult)
                V.tensor_tensor(tok_w[:, :, 1, 1].bitcast(F32), rw[:, 2], rw[:, 0], ALU.mult
                                ).then_inc(S["weights_done"], 1)

            def count():
                dve.wait_ge(S["ranks_in"], 1)
                totals = ps_r[1][:].rearrange("p (t e) -> p e t", e=E)
                for e in range(E):
                    last = V.tensor_tensor_scan(out=incl[:, e], data0=totals[:, e], data1=zeros[:], initial=0.0,
                                                op0=ALU.add, op1=ALU.add)
                step(last)
                cmp = lg2[:].rearrange("p t e -> p (t e)").rearrange("p (e t) -> p e t", e=E)
                step(V.tensor_tensor(cmp, incl[:, :, TILES - 1:TILES].broadcast_to([P, E, TILES]),
                                     iota_j[:].unsqueeze(1).broadcast_to([P, E, TILES]), ALU.is_gt))
                step(V.tensor_reduce(nblk[:, 0], cmp, AX_X, ALU.add))
                step(V.tensor_tensor_scan(out=nblk[:, 1], data0=nblk[:, 0], data1=zeros[:, 0:E], initial=0.0,
                                          op0=ALU.add, op1=ALU.add))
                step(V.tensor_tensor(nblk[:, 2], nblk[:, 1], nblk[:, 0], ALU.subtract))
                step(V.tensor_scalar(nblk[:, 3], nblk[:, 2], float(P), None, ALU.mult))

            def place():
                step(V.tensor_tensor(lg[:], inclt, ps_r[1][:].rearrange("p (t e) -> p t e", e=E), ALU.subtract))
                step(V.tensor_tensor(lg[:], lg[:], ranks, ALU.add))
                step(V.tensor_tensor(lg[:], lg[:], per_expert(nblk[:, 3]), ALU.add))
                for k in range(2):
                    step(V.tensor_tensor(lg2[:], oh[:, k], lg[:], ALU.mult))
                    step(V.tensor_reduce(slot_f[:, k], lg2[:], AX_X, ALU.add))
                step(V.tensor_copy(slot_i[:], slot_f[:]))
                V.tensor_scalar(row_i[:, 0], slot_i[:], P - 1, None, ALU.bitwise_and)
                step(V.tensor_scalar(row_i[:, 1], slot_i[:], 7, None, ALU.logical_shift_right))
                V.scalar_tensor_tensor(out=dest_i[:].rearrange("p t k -> p k t"), in0=row_i[:, 0],
                                       scalar=float(BLOCKS), in1=row_i[:, 1],
                                       op0=ALU.mult, op1=ALU.add).then_inc(S["slots_done"], 1)

            def experts_of_blocks():
                step(V.tensor_tensor(blk_cmp[:], iota_b[:].unsqueeze(2).broadcast_to([1, BLOCKS, E - 1]),
                                     nblk[0:1, 1, 0:E - 1].unsqueeze(1).broadcast_to([1, BLOCKS, E - 1]),
                                     ALU.is_ge))
                step(V.tensor_reduce(blk_f[:], blk_cmp[:], AX_X, ALU.add))
                V.tensor_scalar(blk_off[:], blk_f[:], float(SLOT), None, ALU.mult).then_inc(S["blk_done"], 1)

            dve.wait_ge(S["lo_done"], 2 * NB)
            for stored in (*x1_stored, *xhl_stored):
                dve.wait_ge(stored, 16 * NB)
            dve.wait_ge(S["shw_in"], 48)
            dve.wait_ge(S["misc_in"], 48)
            dve.wait_ge(S["bconst"], 2)
            link.link(dve, nc.vector.memset(top[:], 0.0))
            nc.vector.memset(run3[:], 0.0)
            nc.vector.tensor_reduce(top[:, 1, 0:3], shared_raw.rearrange("p (m n) -> p m n", m=3), AX_X, ALU.max,
                                    apply_absolute_value=True)
            for k in range(2):
                for c in range(CC):
                    last = nc.vector.tensor_scalar(gs_t[:, CC * k + c], gate_t[:, c], lns[:, k, c:c + 1], None,
                                                   ALU.mult)
            link.link(dve, last)
            nc.vector.tensor_reduce(top[:, 2, 0:1], gs_t[:, 0:CC], mybir.AxisListType.XY, ALU.max,
                                    apply_absolute_value=True).then_inc(S["gprep"], 1)
            dve.wait_ge(S["topped"], 1)
            scale_columns(dve, link, 1)
            power_scale(dve, link, 2)
            nc.vector.tensor_scalar(lg_s[:], top[:, 2, 0:1], 2.0 ** -25, None, ALU.mult)
            link.link(dve, nc.vector.tensor_scalar(gate_hl[:, 0], gs_t[:, 0:CC], wsc[:, 2, 0:1], None, ALU.mult))
            nc.vector.scalar_tensor_tensor(out=gate_hl[:, 1], in0=gs_t[:, 0:CC], scalar=wsc[:, 2, 0:1],
                                           in1=gate_hl[:, 0], op0=ALU.mult, op1=ALU.subtract
                                           ).then_inc(S["top_in"], 1)
            for m, (off, n) in enumerate(MATS):
                dve.wait_ge(S["shsplit_done"], m + 1)
                nc.vector.scalar_tensor_tensor(out=wsh[:, off + n:off + 2 * n],
                                               in0=shared_raw[:, off // 2:off // 2 + n],
                                               scalar=wsc[:, 1, m:m + 1], in1=wsh[:, off:off + n],
                                               op0=ALU.mult, op1=ALU.subtract).then_inc(S["gprep"], 1)
            dve.wait_ge(S["gsum"], 1)
            link.link(dve, nc.vector.tensor_copy(sgb[:], bank[6][:, 0:2 * E].rearrange("p (k e) -> p k e", k=2)))

            def take_pair(r):
                dve.wait_ge(S["lxT_in"], r + 1)
                if some(r - 1):
                    dve.wait_ge(S["lg_in"], r - 1)
                nc.vector.tensor_copy(xtl[:, 0].rearrange("p t c n -> p (t c n)"), ps_lx[0]
                                      ).then_inc(S["lxt_done0"], 1)

            take_pair(0)
            with dve.Fori(1, LQ) as q:
                take_pair(2 * q)

            def take_rows(n, par):
                dve.wait_ge(S["xT_in"], n + 1)
                if some(n - 1):
                    dve.wait_ge(S["u_in"], n - 1)
                nc.vector.tensor_copy(xt[:, par].rearrange("p c n -> p (c n)"), ps_x16[:, 0:2 * C]
                                      ).then_inc(S["xt_done"], 1)

            def low(n):
                dve.wait_ge(S["hh_done"], n + 1)
                nc.vector.tensor_tensor(htl[:].rearrange("p c n -> p (c n)"), ps_h[:],
                                        hth[:].rearrange("p c n -> p (c n)"),
                                        ALU.subtract).then_inc(S["hl_done"], 1)

            def hidden(n, par, r):
                dve.wait_ge(S["u_in"], n + 1)
                dve.wait_ge(S["sg_done"], n + 1)
                if some(n):
                    dve.wait_ge(S["hT_in"], n)
                nc.vector.scalar_tensor_tensor(out=hb[:], in0=ps_u[:], scalar=h_s[:, r:r + 1], in1=sg[:, par],
                                               op0=ALU.mult, op1=ALU.mult).then_inc(S["h_done"], 1)

            def result(n, par, half):
                dve.wait_ge(S["yp_in"], n + 1)
                if some(16 * half):
                    dve.wait_ge(y_stored[par], 16 * half)
                dve.wait_ge(x1_loaded[par], 16 * half + 16)
                nc.vector.scalar_tensor_tensor(out=ysb[:, par], in0=ps_z[:, 0:C], scalar=y_s[:, 1:2],
                                               in1=x1t[:, par], op0=ALU.mult, op1=ALU.add
                                               ).then_inc(S["y_out"], 1)

            def shared(n, par, half, prev, nxt):
                if prev:
                    low(n - 1)
                hidden(n, par, 1)
                if nxt:
                    take_rows(n + 1, 1 - par)
                if prev:
                    result(n - 1, 1 - par, half - 1 if par == 0 else half)

            def first(e):
                dve.wait_ge(S["w_exp"], 48 * (e + 1))
                link.link(dve, nc.vector.tensor_reduce(
                    top[:, 0, 0:3], wraw[:, bass.ds(e + 1, 1), :].rearrange("p o (m n) -> p (o m) n", m=3),
                    AX_X, ALU.max, apply_absolute_value=True))
                nc.vector.tensor_tensor(run3[:], run3[:], top[:, 0, 0:3], ALU.max).then_inc(S["wmax_done"], 1)
                dve.wait_ge(S["wmax_done"], e + 1)

            def second(e, k):
                if k == len(MATS):
                    return
                off, n = MATS[k]
                dve.wait_ge(S["whi_done"], 3 * e + k + 1)
                nc.vector.scalar_tensor_tensor(
                    out=wbuf[:, bass.ds(e * SLOT + (off + n), n)],
                    in0=wraw[:, bass.ds(e + 1, 1), off // 2:off // 2 + n].rearrange("p o n -> p (o n)"),
                    scalar=wsc[:, 0, k:k + 1], in1=wbuf[:, bass.ds(e * SLOT + off, n)],
                    op0=ALU.mult, op1=ALU.subtract).then_inc(S["wlo_done"], 1)

            take_rows(0, 0)
            def middle():
                dve.wait_ge(S["topped"], 2)
                scale_columns(dve, link, 0)

            AFTER = {0: route_logits, 2: choose_first, 4: choose_second, 6: choose, EXP_AT: weigh,
                     9: count, 10: place, 11: experts_of_blocks}

            def beside(n):
                if n in AFTER:
                    AFTER[n]()

            shared_blocks(dve, shared, beside, first, second, middle, link, (1, 0))
            low(N_SH - 1)
            result(N_SH - 1, (N_SH - 1) % 2, (N_SH - 1) // 2)
            dve.wait_ge(S["rows_in"], 16)
            nc.vector.tensor_scalar(row_w[:], tok_rows[:, :, 1].bitcast(F32), y_s[:, 0:1], None, ALU.mult
                                    ).then_inc(S["row_w_done"], 1)

            def routed(n, par, half, prev, nxt):
                if prev:
                    low(n - 1)
                hidden(n, par, 0)
                if nxt:
                    take_rows(n + 1, 1 - par)

            take_rows(N_SH, 0)
            routed_blocks(dve, routed)
            low(N_ALL - 1)
        @block.tensor
        def _(pe):
            def transpose_xn(n, c):
                pe.wait_ge(S["xn_done"], n + 1)
                if c:
                    pe.wait_ge(S["xl_done"], 2 * n + c)
                elif some(4 * n):
                    pe.wait_ge(S["qkl_done"], 4 * n)
                for t in range(NT):
                    last = nc.tensor.transpose(ps_q[:, P * t:P * (t + 1)], xn[:, t, P * c:P * (c + 1)], ident[:])
                last.then_inc(S["xnT_in"], 1)

            def products(out, pairs):
                n = 3 * len(pairs)
                i = 0
                for (lh, ll), (rh, rl) in pairs:
                    for a, m in ((lh, rh), (lh, rl), (ll, rh)):
                        last = nc.tensor.matmul(out, a, m, start=(i == 0), stop=(i == n - 1))
                        i += 1
                return last

            def project_qk(n, i):
                if i == 0:
                    pe.wait_ge(S["xl_done"], 2 * n + 2)
                elif i == 2:
                    pe.wait_ge(S["v_done"], 2 * n + 2)
                else:
                    pe.wait_ge(S["qkl_done"], 4 * n + i)
                col = 256 * (i % 2) + P * (i // 2)
                products(ps_q[:], [((wah[:, c, col:col + P], wal[:, c, col:col + P]),
                                    (xh[:, c, :], xl[:, c, :])) for c in range(2)]).then_inc(S["qk_in"], 1)

            def project_v(n, j):
                if j == 0:
                    pe.wait_ge(S["qkl_done"], 4 * n + 2)
                else:
                    pe.wait_ge(S["v_done"], 2 * n + 1)
                for t in range(2):
                    tok = slice(P * (2 * j + t), P * (2 * j + t + 1))
                    last = products(ps_q[:, 256 * t:256 * t + 256],
                                    [((xh[:, c, tok], xl[:, c, tok]),
                                      (wah[:, c, 2 * C:], wal[:, c, 2 * C:])) for c in range(2)])
                last.then_inc(S["v_in"], 1)

            def prologue():
                pe.wait_ge(S["attn_w"], 2)
                pe.wait_ge(S["pool_const"], 3)
                for i in range(4):
                    col = 256 * (i % 2) + P * (i // 2)
                    last = nc.tensor.matmul(ps_m[:, i:i + 1], wa[0:1, 2, col:col + P], one[0:1, :],
                                            start=True, stop=True)
                last.then_inc(S["biascols"], 1)
                transpose_xn(0, 0)
                transpose_xn(0, 1)
                pe.wait_ge(S["scales_done"], 1)
                for i in range(2):
                    project_qk(0, i)
                project_v(0, 0)
                project_v(0, 1)
                for i in range(2, 4):
                    project_qk(0, i)

            prologue()

            def scores(b, G, g, u):
                if u == 0:
                    pe.wait_ge(ops_in[g], LOADS * (b + 1))
                if some(UN * G + u - 1):
                    pe.wait_ge(S["max_done"], UN * G + u - 1)
                out = ps_s[u % 2]

                def mm(h, q, lo, start):
                    nc.tensor.matmul(out[:, lo:lo + P * (q + 1)],
                                     q_op[0:96, 2 * g + h // 2, P * q:P * (q + 1)],
                                     k_op[0:96, GH * g + h, 0:P * (q + 1)], start=start, stop=False)

                cols = out[:].rearrange("p (s n) -> p s n", n=P)
                if u < 4:
                    mm(u, 3, 0, True)
                    sel, n = cols[:, 3:4, :], 1
                elif u < 8:
                    mm(u - 4, 2, 0, True)
                    mm(u - 4, 0, 384, False)
                    sel, n = cols[:, 2:4, :], 2
                else:
                    mm(2 * (u - 8), 1, 0, True)
                    mm(2 * (u - 8) + 1, 1, 256, False)
                    sel, n = cols[:, 1:4:2, :], 2
                nc.tensor.matmul(sel, ident_b[:], mask[:].unsqueeze(1).broadcast_to([P, n, P]),
                                 start=False, stop=True).then_inc(S["s_in"], 1)

            def maxima(b, G, g):
                pe.wait_ge(S["max_done"], UN * G)
                if some(G - 1):
                    pe.wait_ge(S["m_done"], G - 1)
                if g == 0:
                    if some(2 * (b - 1)):
                        pe.wait_ge(S["x1_done"], 2 * (b - 1))
                if g == 3:
                    if some(2 * (b - 1) + 1):
                        pe.wait_ge(S["x1_done"], 2 * (b - 1) + 1)
                for q in range(NT):
                    last = nc.tensor.matmul(ps_m[0:GH, P * q:P * (q + 1)], mx[:, (g - 1) % 2, q, :], ident[:],
                                            start=True, stop=True)
                last.then_inc(S["m_in"], 1)

            def shifted(G, gg, u):
                if u == 0:
                    pe.wait_ge(S["m_done"], G + 1)
                if some(UN * G + u - 1):
                    pe.wait_ge(S["exp_done"], UN * G + u - 1)
                out = ps_t[u % 2]

                def mm(h, k, lo, start, stop):
                    n = T - P * k
                    return nc.tensor.matmul(out[:, lo:lo + n], k_op[:, GH * gg + h, P * k:P * (k + 1)],
                                            q_op[:, 2 * gg + h // 2, P * k:], start=start, stop=stop)

                if u < 4:
                    last = mm(u, 0, 0, True, True)
                elif u < 8:
                    mm(u - 4, 1, 0, True, False)
                    last = mm(u - 4, 3, 384, False, True)
                else:
                    mm(2 * (u - 8), 2, 0, True, False)
                    last = mm(2 * (u - 8) + 1, 2, 256, False, True)
                last.then_inc(S["t_in"], 1)

            def mix(G, gg, vpar, nb, piece):
                if piece == 0:
                    if some(G):
                        pe.wait_ge(S["o_done"], G)
                    pe.wait_ge(S["v_done"], 2 * (nb + 1))
                k = (0, 1, 3, 2)[piece]
                pe.wait_ge(S["sel_done"], UN * G + (4, 8, 8, 10)[piece])
                pr = prob[:, gg % 2]
                for h in range(GH):
                    unit, lo = ((h, 0), (4 + h, 0), (8 + h // 2, 256 * (h % 2)), (4 + h, 384))[k]
                    n = T - P * k
                    last = nc.tensor.matmul(ps_o[32 * h:32 * h + 32, P * k:], v_op[:, vpar, k, GH * gg + h, :],
                                            pr[:, unit, lo:lo + n], start=(piece == 0), stop=(piece == 3))
                if piece == 3:
                    last.then_inc(S["pv_in"], 1)

            def transpose_o(bp, opar, q):
                k = 4 * bp + q
                pe.wait_ge(S["o_done"], 4 * bp + 4)
                if q == 0:
                    if some(2 * bp):
                        pe.wait_ge(S["yT_done"], 2 * bp)
                elif q == 2:
                    pe.wait_ge(S["yT_done"], 2 * bp + 1)
                else:
                    pe.wait_ge(S["y_done"], k)
                for g in range(NG):
                    last = nc.tensor.transpose(ps_y[:, P * g:P * (g + 1)], o_t[:, opar, g, P * q:P * (q + 1)],
                                               ident[:])
                last.then_inc(S["ot_in"], 1)

            def transpose_y(bp, j):
                pe.wait_ge(S["y_done"], 4 * bp + 2 * j + 2)
                for t in range(2):
                    for c in range(2):
                        last = nc.tensor.transpose(ps_y[:, P * (2 * t + c):P * (2 * t + c + 1)],
                                                   y[:, t, P * c:P * (c + 1)], ident[:])
                last.then_inc(S["yT_in"], 1)

            def project_out(b, bp, j, tail):
                pe.wait_ge(S["yT_done"], 2 * bp + j + 1)
                if tail:
                    pe.wait_ge(S["x1_done"], 2 * bp + j)
                else:
                    pe.wait_ge(S["m_done"], 4 * b + 2 + j)
                for t in range(2):
                    for c in range(2):
                        last = nc.tensor.matmul(ps_m[:, 256 * t:256 * t + 256], y_t[:, t, c, :], wp[:, c, :],
                                                start=(c == 0), stop=(c == 1))
                last.then_inc(S["pr_in"], 1)

            def body(b, par, cur, prev, prev2, nxt, nxt2):
                for g in range(NG):
                    G = 4 * b + g
                    has1 = (cur or g < 1) and (prev or g >= 1)
                    has2 = (cur or g < 2) and (prev or g >= 2)
                    for s in range(UN):
                        if cur:
                            scores(b, G, g, s)
                        if s == MAXIMA and has1:
                            maxima(b, G, g)
                        if s >= LAG - UN and has1:
                            shifted(G - 1, (g - 1) % 4, s + UN - LAG)
                        elif s < LAG - UN and has2:
                            shifted(G - 2, (g - 2) % 4, s + 2 * UN - LAG)
                        if has2 and s in MIX:
                            mix(G - 2, (g - 2) % 4, par if g >= 2 else 1 - par, b if g >= 2 else b - 1,
                                MIX.index(s))
                        if nxt:
                            for c in range(2):
                                if (g, s) == XN_T[c]:
                                    transpose_xn(b + 1, c)
                            for i in range(4):
                                if (g, s) == QK[i]:
                                    project_qk(b + 1, i)
                            for j in range(2):
                                if (g, s) == V_PROJ[j]:
                                    project_v(b + 1, j)
                        if prev:
                            for q in range(NT):
                                if (g, s) == O_T[q]:
                                    transpose_o(b - 1, 1 - par, q)
                            for j in range(2):
                                if (g, s) == Y_T[j]:
                                    transpose_y(b - 1, j)
                                if (g, s) == PROJ[j]:
                                    project_out(b, b - 1, j, not cur)

            batches(pe, body)

            pe.wait_ge(S["lo_done"], 2 * NB)
            for stored in (*x1_stored, *xhl_stored):
                pe.wait_ge(stored, 16 * NB)
            pe.wait_ge(S["top_in"], 2)
            pe.wait_ge(S["bconst"], 2)
            for k in range(2):
                for c in range(CC):
                    last = nc.tensor.matmul(bank[6][:, E * k:E * (k + 1)], ones_f[:], gs_t[:, CC * k + c],
                                            start=(c == 0), stop=(c == CC - 1))
            last.then_inc(S["gsum"], 1)

            def transpose_pair(q, par, h, i):
                if h == 0:
                    pe.wait_ge(lrow_loaded[par], 16 * i + 16)
                if some(q):
                    pe.wait_ge(S[f"lxt_done{h}"], q)
                for t in range(2):
                    for c in range(2 * CC):
                        at = P * (2 * CC * t + c)
                        last = nc.tensor.transpose(ps_lx[h][:, at:at + P],
                                                   lrow[:, par, 2 * h + t, P * c:P * (c + 1)], ident_h[:])
                last.then_inc(S["lxT_in"], 1)

            def logits(q, h):
                pe.wait_ge(S[f"lxt_done{h}"], q + 1)
                for t in range(2):
                    last = products(ps_l[:, bass.ds((4 * q + (2 * h + t)) * E, E)],
                                    [((xtl[:, h, t, c, :], xtl[:, h, t, CC + c, :]),
                                      (gate_hl[:, 0, c, :], gate_hl[:, 1, c, :])) for c in range(CC)])
                last.then_inc(S["lg_in"], 1)

            transpose_pair(0, 0, 0, 0)
            transpose_pair(0, 0, 1, 0)
            logits(0, 0)
            transpose_pair(1, 1, 0, 0)
            logits(0, 1)
            transpose_pair(1, 1, 1, 0)
            logits(1, 0)
            with pe.Fori(1, LQ // 2) as i:
                for par in range(2):
                    transpose_pair(2 * i + par, par, 0, i)
                    logits(2 * i + (par - 1), 1)
                    transpose_pair(2 * i + par, par, 1, i)
                    logits(2 * i + par, 0)
            logits(LQ - 1, 1)

            def weights(w, off, k, n, size):
                if w is None:
                    return wsh[:, off + k * n:off + (k + 1) * n], wsh[:, off + size + k * n:off + size + (k + 1) * n]
                return (wbuf[:, bass.ds(w + (off + k * n), n)], wbuf[:, bass.ds(w + (off + size + k * n), n)])

            def transpose_rows(n, par, arrived, count):
                pe.wait_ge(arrived[par], 16 * count + 16)
                if some(n):
                    pe.wait_ge(S["xt_done"], n)
                for c in range(2 * CC):
                    last = nc.tensor.transpose(ps_x16[:, P * c:P * (c + 1)], xrow[:, par, P * c:P * (c + 1)],
                                               ident_h[:])
                last.then_inc(S["xT_in"], 1)

            def x_pair(par, c):
                return xt[:, par, c, :], xt[:, par, CC + c, :]

            def gate(n, par, w):
                pe.wait_ge(S["xt_done"], n + 1)
                if some(n):
                    pe.wait_ge(S["sg_done"], n)
                products(ps_g[:], [(x_pair(par, c), weights(w, WG, c, HID, CC * HID)) for c in range(CC)]
                         ).then_inc(S["g_in"], 1)

            def up(n, par, w):
                if some(n):
                    pe.wait_ge(S["h_done"], n)
                products(ps_u[:], [(x_pair(par, c), weights(w, WU, c, HID, CC * HID)) for c in range(CC)]
                         ).then_inc(S["u_in"], 1)

            def transpose_hidden(n):
                pe.wait_ge(S["h_done"], n + 1)
                if some(n):
                    pe.wait_ge(S["hl_done"], n)
                for k in range(HC):
                    last = nc.tensor.transpose(ps_h[:, P * k:P * (k + 1)], hb[:, P * k:P * (k + 1)], ident[:])
                last.then_inc(S["hT_in"], 1)

            def down(n, w):
                pe.wait_ge(S["hl_done"], n + 1)
                if some(n):
                    pe.wait_ge(S["y_out"], n)
                products(ps_z[:, 0:C], [((hth[:, k, :], htl[:, k, :]), weights(w, WD, k, C, HC * C))
                                        for k in range(HC)]).then_inc(S["yp_in"], 1)

            def shared(n, par, half, prev, nxt):
                if prev:
                    transpose_hidden(n - 1)
                gate(n, par, None)
                up(n, par, None)
                if nxt:
                    transpose_rows(n + 1, 1 - par, row_loaded, half + par)
                if prev:
                    down(n - 1, None)

            transpose_rows(0, 0, row_loaded, 0)
            pe.wait_ge(S["gprep"], 4)

            def beside(n):
                if n == RANKS_AT:
                    pe.wait_ge(S["sel_ready"], 1)
                    flat = sel[:].rearrange("p t e -> p (t e)")
                    nc.tensor.matmul(ps_r[0][:], before_b[:], flat, start=True, stop=True)
                    nc.tensor.matmul(ps_r[1][:], ones_b[:], flat, start=True, stop=True
                                     ).then_inc(S["ranks_in"], 1)

            shared_blocks(pe, shared, beside)
            transpose_hidden(N_SH - 1)
            down(N_SH - 1, None)
            pe.wait_ge(S["wlo_done"], 3 * E + 1)
            pe.wait_ge(S["blk_done"], 1)
            offset = [pe.alloc_register("offset_even"), pe.alloc_register("offset_odd")]
            offset_down = pe.alloc_register("offset_down")

            def at(register):
                return pe.snap(register, min_val=0, max_val=(E - 1) * SLOT)

            def routed(n, par, half, prev, nxt):
                if prev:
                    transpose_hidden(n - 1)
                begin = at(offset[par])
                gate(n, par, begin)
                up(n, par, begin)
                if prev:
                    pe.reg_mov(offset_down, offset[1 - par])
                if nxt:
                    pe.reg_load(offset[1 - par], blk_off[0:1, bass.ds(n - (N_SH - 1), 1)])
                    transpose_rows(n + 1, 1 - par, row_gathered, half + (par - N_SH // 2))
                if prev:
                    down(n - 1, at(offset_down))

            pe.reg_load(offset[0], blk_off[0:1, 0:1])
            transpose_rows(N_SH, 0, row_gathered, 0)
            routed_blocks(pe, routed)
            transpose_hidden(N_ALL - 1)
            down(N_ALL - 1, at(offset[(N_ALL - 1) % 2]))


def rope_table(heads, hd):
    theta = (1.0 / 10000.0 ** (np.arange(0, hd, 2, dtype=np.float32) / np.float32(hd))).astype(np.float32)
    ang = (np.arange(heads, dtype=np.float32)[:, None] * theta[None, :]).reshape(-1)
    k = np.stack([np.cos(ang), np.sin(ang)]).astype(np.float32)
    return np.concatenate([k * np.float32(hd ** -0.5), k], axis=1)


INPUTS = ["L0_attn_x", "L0_attn_W_attn", "L0_attn_b_attn", "L0_attn_W_proj", "L0_attn_b_proj",
          "L0_ffn_ln_scale", "L0_ffn_ln_bias", "L0_ffn_gate_w", "L0_ffn_Wg", "L0_ffn_Wu", "L0_ffn_Wd",
          "L0_ffn_sWg", "L0_ffn_sWu", "L0_ffn_sWd"]


def kernel(**inputs):
    import concourse.bacc as bacc
    from concourse.bass_utils import run_bass_kernel_spmd

    nc = bacc.Bacc("TRN2", target_bir_lowering=False, num_devices=1)
    shape = inputs["L0_attn_x"].shape
    arrays = {f"in_{name}": np.ascontiguousarray(inputs[name]) for name in INPUTS}
    arrays["in_L0_attn_x"] = arrays["in_L0_attn_x"].reshape(-1, shape[-1])
    gate = arrays["in_L0_ffn_gate_w"]
    arrays["in_L0_ffn_gate_w"] = np.ascontiguousarray(gate.reshape(gate.shape[0], -1, P).transpose(2, 1, 0))
    for name in ("in_L0_ffn_ln_scale", "in_L0_ffn_ln_bias"):
        arrays[name] = np.ascontiguousarray(arrays[name].reshape(-1, P).T)
    arrays["in_rope"] = rope_table(16, shape[-1] // 16)
    args = [nc.dram_tensor(n, a.shape, mybir.dt.from_np(a.dtype), kind="ExternalInput").ap()
            for n, a in arrays.items()]
    rows = arrays["in_L0_attn_x"].shape[0]
    out = nc.dram_tensor("out_x", (rows + P, shape[-1]), F32, kind="ExternalOutput").ap()
    build(nc, *args, out)
    r = run_bass_kernel_spmd(nc, [arrays], core_ids=[0])
    return r.results[0]["out_x"][:rows].reshape(shape)
```

```python
from contextlib import ExitStack

import numpy as np
import concourse.bass as bass
from concourse import mybir

F32 = mybir.dt.float32
F32R = mybir.dt.float32r
F16 = mybir.dt.float16
BF16 = mybir.dt.bfloat16
I32 = mybir.dt.int32
ALU = mybir.AluOpType
ACT = mybir.ActivationFunctionType
AX_X = mybir.AxisListType.X
RMAX = bass.bass_isa.ReduceOp.max

P = 128
BEFORE_MAX = 38
EPS = 1e-5
X_SCALE = 2048.0
SHIFT_UNIT = 32768.0
MASKED = -1e30
DVE_LINKS = 18


class Count:

    def __init__(self, sem):
        self.sem, self.base, self.n = sem, 0, 0

    def link(self, engine, instruction):
        instruction.then_inc(self.sem, 1)
        self.n += 1
        engine.wait_ge(self.sem, self.base + self.n)


def some(value):
    return not isinstance(value, int) or value > 0


def build(nc, x, w_attn, b_attn, w_proj, b_proj, ln_scale, ln_bias, gate_w, Wg, Wu, Wd, sWg, sWu, sWd, rope, out):
    NTOK, C = x.shape
    T = 512
    NB = NTOK // T
    NT = T // P
    H = 16
    HD = C // H
    GH = 4
    NG = H // GH
    UN = 10
    LOADS = 18 * 16

    E = Wg.shape[0]
    HID = Wg.shape[2]
    TILES = NTOK // P
    BLOCKS = (2 * NTOK + E * (P - 1)) // P
    BLOCKS += BLOCKS % 2
    CC, HC = C // P, HID // P
    WG, WU, WD = 0, 2 * CC * HID, 4 * CC * HID
    SLOT = 4 * CC * HID + 2 * HC * C

    def scratch(name, shape, dt):
        return nc.dram_tensor(name, shape, dt, kind="Internal").ap()

    x1_d = scratch("x1_d", (NTOK, C), F32)
    xhl_d = scratch("xhl_d", (NTOK + P, 2 * C), F16)
    tok_d = scratch("tok_d", (P * BLOCKS, 2), I32)

    xv = x.rearrange("(b t p) c -> b p t c", t=NT, p=P)
    x1v = x1_d.rearrange("(b j t p) c -> b j p t c", j=2, t=2, p=P)
    xhlv = xhl_d[0:NTOK].rearrange("(b j t p) c -> b j p t c", j=2, t=2, p=P)

    with ExitStack() as ctx:
        def sb(name, shape, dt):
            return ctx.enter_context(nc.sbuf_tensor(name, shape, dt))

        ctx_a = ctx.enter_context(ExitStack())

        def sb_a(name, shape, dt):
            return ctx_a.enter_context(nc.sbuf_tensor(name, shape, dt))

        def sem(name):
            return ctx.enter_context(nc.semaphore(name))

        bank = [ctx.enter_context(nc.psum_tensor(f"bank{i}", [P, 512], F32)) for i in range(8)]
        ps_s, ps_t, ps_o, ps_q, ps_m, ps_y = bank[0:2], bank[2:4], bank[4], bank[5], bank[6], bank[7]

        ident_h = sb("ident_h", [P, P], F16)
        wsh = sb("wsh", [P, SLOT], F16)
        var_all = sb("var_all", [P, TILES], F32)
        early = sb("early", [P, SLOT // 2 + 3 * 256], F32)
        ident = sb("ident", [P, P], F32)
        ident_b = sb("ident_b", [P, P], BF16)
        mask = sb("mask", [P, P], BF16)
        one = sb("one", [P, 1], F32)
        neghalf = sb("neghalf", [P, 4], F32)
        top = sb("top", [P, 3, 4], F32)
        inv = sb("inv", [P, 3, 4], F32)
        wsc = sb("wsc", [P, 3, 4], F32)
        run3 = sb("run3", [P, 3], F32)
        silu_s = sb("silu_s", [P, 2], F32)
        h_s = sb("h_s", [P, 2], F32)
        y_s = sb("y_s", [P, 2], F32)
        lg_s = sb("lg_s", [P, 1], F32)
        gate_t = sb("gate_t", [P, CC, E], F32)
        gs_t = sb("gs_t", [P, 2 * CC, E], F32)
        gate_hl = sb("gate_hl", [P, 2, CC, E], F16)
        lns = sb("lns", [P, 2, CC], F32)
        ones_f = sb("ones_f", [P, P], F32)
        sgb = sb("sgb", [P, 2, E], F32)
        cs = sb_a("cs", [P, 2, 256], F32)
        bvb = sb_a("bvb", [P, C], F32)
        bpb = sb_a("bpb", [P, C], F32)
        wa = early[:, 0:9 * C].rearrange("p (k n) -> p k n", k=3)
        shared_raw = early[:, 0:SLOT // 2]
        wah = sb_a("wah", [P, 2, 3 * C], F32R)
        wal = sb_a("wal", [P, 2, 3 * C], F32R)
        wp = sb_a("wp", [P, 2, C], F32)
        bcol = sb_a("bcol", [P, 4], F32)
        qk_max = sb_a("qk_max", [P, 2], F32)
        qk_top = sb_a("qk_top", [P, 2], F32)
        qk_inv = sb_a("qk_inv", [P, 2], F32)
        qk_scale = sb_a("qk_scale", [P, 2], F32)
        exp_scale = sb_a("exp_scale", [P, 1], F32)
        rope_t = early[:, 9 * C:15 * C].rearrange("p (a k n) -> p a k n", a=2, k=3)
        x_in = sb_a("x_in", [P, 2, NT, C], F32)
        xn = sb_a("xn", [P, NT, C], F32)
        st6 = sb_a("st6", [P, NT, 6], F32)
        mv = sb_a("mv", [P, NT, 2], F32)
        rstd = sb_a("rstd", [P, NT], F32)
        shift = sb_a("shift", [P, NT], F32)
        xh = sb_a("xh", [P, 2, T], F32R)
        xl = sb_a("xl", [P, 2, T], F32R)
        qkh = sb_a("qkh", [P, 4, T], F16)
        qkl = sb_a("qkl", [P, 4, T], F16)
        q_op = sb_a("q_op", [P, H // 2, T], F16)
        k_op = sb_a("k_op", [P, H, T], F16)
        v_op = sb_a("v_op", [P, 2, NT, H, 32], F32)
        mx = sb_a("mx", [P, 2, NT, GH], F32)
        prob = sb_a("prob", [P, 2, UN, 512], F32)
        o_t = sb_a("o_t", [P, 2, NG, T], F32)
        rec = sb_a("rec", [P, 2, H], F32)
        y = sb_a("y", [P, 2, C], F32)
        y_t = sb_a("y_t", [P, 2, 2, P], F32)
        xres = sb_a("xres", [P, NT, C], F32)
        x1 = sb_a("x1", [P, 2, 2, C], F32)
        st6b = sb_a("st6b", [P, 2, 6], F32)
        mvb = sb_a("mvb", [P, 2, 2], F32)
        rstdb = sb_a("rstdb", [P, 2], F32)
        xf = sb_a("xf", [P, 2, C], F32)
        xhl = sb_a("xhl", [P, 2, 2, 2, C], F16)

        ctx_a.close()
        wbuf = sb("wbuf", [P, (E + 1) * SLOT], F16)
        wraw = wbuf[:].bitcast(F32).rearrange("p (s n) -> p s n", s=E + 1)
        xrow = sb("xrow", [P, 2, 2 * C], F16)
        xt = sb("xt", [P, 2, 2 * CC, P], F16)
        sg = sb("sg", [P, 2, HID], F32)
        hb = sb("hb", [P, HID], F32)
        hth = sb("hth", [P, HC, P], F16)
        htl = sb("htl", [P, HC, P], F16)
        ysb = sb("ysb", [P, 2, C], F32)
        x1t = sb("x1t", [P, 2, C], F32)
        spare = wbuf[:, (E - 1) * SLOT:]
        lrow = spare[:, 0:4 * 4 * 2 * C].rearrange("p (a t n) -> p a t n", a=4, t=4)
        xtl = spare[:, 4 * 4 * 2 * C:4 * 4 * 2 * C + 2 * 2 * 2 * CC * P].rearrange(
            "p (a t c n) -> p a t c n", a=2, t=2, c=2 * CC)
        zero_h = sb("zero_h", [P, 2 * C], F16)
        ones_b = sb("ones_b", [P, P], BF16)
        before_b = sb("before_b", [P, P], BF16)
        rvar = sb("rvar", [P, 2, TILES], F32)
        rhalf = sb("rhalf", [P, TILES], F32)
        lg = sb("lg", [P, TILES, E], F32)
        lg2 = sb("lg2", [P, TILES, E], F32)
        tmp = sb("tmp", [P, TILES, E], F32)
        oh = sb("oh", [P, 2, TILES, E], F32)
        sel = sb("sel", [P, TILES, E], BF16)
        m12 = sb("m12", [P, 4, TILES], F32)
        rw = sb("rw", [P, 6, TILES], F32)
        iota_e = sb("iota_e", [P, E], F32)
        iota_j = sb("iota_j", [P, TILES], F32)
        iota_b = sb("iota_b", [1, BLOCKS], F32)
        incl = sb("incl", [P, E, TILES], F32)
        zeros = sb("zeros", [P, TILES], F32)
        nblk = sb("nblk", [P, 4, E], F32)
        slot_f = sb("slot_f", [P, 2, TILES], F32)
        slot_i = sb("slot_i", [P, 2, TILES], I32)
        row_i = sb("row_i", [P, 3, 2, TILES], I32)
        dest_i = sb("dest_i", [P, TILES, 2], I32)
        tok_w = sb("tok_w", [P, TILES, 2, 2], I32)
        tok_rows = sb("tok_rows", [P, BLOCKS, 2], I32)
        no_tok = sb("no_tok", [P, BLOCKS, 2], I32)
        row_w = sb("row_w", [P, BLOCKS], F32)
        blk_cmp = sb("blk_cmp", [1, BLOCKS, E - 1], F32)
        blk_f = sb("blk_f", [1, BLOCKS], F32)
        blk_off = sb("blk_off", [1, BLOCKS], I32)
        to_col = sb("to_col", [P, 2, 2], I32)
        tw_col = sb("tw_col", [P, 2, 4], I32)
        ga_col = sb("ga_col", [P, 2, 1], I32)
        ad_col = sb("ad_col", [P, 2, 1], I32)
        ps_g, ps_u, ps_h, ps_x, ps_z, ps_l = bank[0], bank[1], bank[2], bank[3], bank[4], bank[5]
        ps_x16 = ps_x[:].bitcast(F16)
        ps_lx = [bank[k][:].bitcast(F16) for k in (6, 7)]
        ps_r = bank[6:8]

        names = ("k_zeroed const_in w_in x_in0 x_in1 res_in ops0 ops1 ops2 ops3 "
                 "pool_const attn_w qk_topped biascols scales_done "
                 "xn_done shift_done xnT_in xh_done xl_done qk_in qkh_done qkl_done v_in v_done "
                 "s_in max_done m_in m_done t_in exp_done sel_done pv_in o_done "
                 "ot_in y_done yT_in yT_done pr_in x1_done xb_done "
                 "var_done rstd_done varb_done rstdb_done xf_done hi_done lo_done "
                 "x1_out0 x1_out1 xhl_out0 xhl_out1 dve_link pool_link "
                 "shw_in shsplit_done misc_in bconst row_in0 row_in1 rowg0 rowg1 x1t_in0 x1t_in1 w_exp "
                 "xT_in xt_done g_in sg_done u_in h_done hT_in hh_done hl_done yp_in y_out "
                 "y_st0 y_st1 lg_in top_in topped wmax_done whi_done wlo_done gprep gsum "
                 "stats_taken x1_taken scol route_var route_rstd exp_in exp_out sel_ready ranks_in slots_done "
                 "zero_st scat0 scat1 rows_in blk_done gcol acol y_added spare_st "
                 "lrow_in0 lrow_in1 lrow_in2 lrow_in3 lxT_in lxt_done0 lxt_done1 row_w_done "
                 "weights_done pool_passed sp_passed dve_passed").split()
        S = {n: sem(n) for n in names}
        ops_in = [S[f"ops{g}"] for g in range(4)]
        x_loaded = [S["x_in0"], S["x_in1"]]
        x1_stored = [S["x1_out0"], S["x1_out1"]]
        xhl_stored = [S["xhl_out0"], S["xhl_out1"]]

        XN_BANK, QK_BANK, V_BANK = (ps_q, ps_y), (ps_s[0], ps_s[1], ps_o, ps_q), ps_t

        LOOPS = (NB - 6) // 2
        EXP_AT, RANKS_AT = 15, 16

        LAG = 13
        MAXIMA, M_ROWS = 2, 2
        MIX, O_OUT = (2, 4, 5, 6), 7
        XN_T, XN_HIGH, XN_LOW = ((0, 0), (0, 3)), ((0, 0), (0, 4)), ((0, 2), (0, 5))
        QK = ((0, 8), (1, 0), (2, 3), (2, 7))
        QK_HIGH = ((0, 7), (1, 0), (2, 3), (2, 7))
        QK_LOW = ((0, 9), (1, 2), (2, 5), (2, 9))
        V_PROJ, VALUES = ((1, 7), (1, 9)), ((1, 8), (2, 0))
        STATS, VARIANCE, RSTD, SHIFT = ((1, 4), (1, 6)), (2, 4), (2, 2), (2, 5)
        NORMALISE = ((2, 9), (3, 0), (3, 3), (3, 8))
        O_T = ((1, 8), (2, 0), (2, 9), (3, 2))
        DIVIDE = ((1, 9), (2, 1), (3, 1), (3, 3))
        Y_T, Y_OUT, PROJ = ((2, 5), (3, 4)), ((2, 6), (3, 5)), ((3, 0), (3, 7))
        X_BIAS = ((0, 4), (0, 9), (1, 0), (1, 3))
        X1, X1_STATS, X1_VARIANCE = ((3, 0), (3, 7)), ((3, 2), (3, 9)), ((3, 4), (0, 0))
        RSTD_B, ROWS, HIGH, LOW = ((3, 4), (0, 1)), ((3, 5), (0, 3)), ((3, 6), (0, 5)), ((3, 8), (0, 8))
        PREP_MAX, PREP_TOP, PREP_SCALE, PREP_SUM = (0, 8), (1, 0), (1, 1), (1, 1)
        PREP_HIGH, PREP_LOW = ((1, 4), (1, 5), (1, 6)), ((1, 5), (1, 6), (1, 7))

        def layernorm_of(b, prev, prev2):
            return (0, b - 1, prev), (1, b - 2, prev2)

        def batches(engine, body, link=None, links=0):
            full = dict(cur=True, prev=True, prev2=True, nxt=True, nxt2=True)
            body(0, 0, **{**full, "prev": False, "prev2": False})
            body(1, 1, **{**full, "prev2": False})
            body(2, 0, **full)
            before = link.n if link else 0
            with engine.Fori(0, LOOPS) as i:
                if link:
                    link.base = i * links
                body(2 * i + 3, 1, **full)
                body(2 * i + 4, 0, **full)
            if link:
                assert link.n - before == links, link.n - before
                link.base, link.n = 0, before + LOOPS * links
            body(NB - 3, 1, **full)
            body(NB - 2, 0, **{**full, "nxt2": False})
            body(NB - 1, 1, **{**full, "nxt2": False, "nxt": False})
            body(NB, 0, cur=False, prev=True, prev2=True, nxt=False, nxt2=False)

        row_loaded = [S["row_in0"], S["row_in1"]]
        row_gathered = [S["rowg0"], S["rowg1"]]
        y_stored = [S["y_st0"], S["y_st1"]]
        x1_loaded = [S["x1t_in0"], S["x1t_in1"]]
        scattered = [S["scat0"], S["scat1"]]
        lrow_loaded = [S[f"lrow_in{k}"] for k in range(4)]
        LQ = TILES // 4
        LOGITS_END = LQ // 2
        ROUTE_END = 22
        MAX_END = ROUTE_END + 3 * E
        SPLIT_AT = TILES - 2 * E
        LOADS_AT = ROUTE_END - 3 * (E // 2)
        N_SH = TILES
        N_ALL = TILES + BLOCKS

        def shared_blocks(engine, body, beside=None, first=None, second=None, middle=None, link=None, links=0):
            for n in range(4):
                body(n, n % 2, n // 2, n > 0, True)
            with engine.Fori(2, LOGITS_END // 2) as i:
                for k in range(2):
                    body(2 * i + k, k, i, True, True)
            for n in range(LOGITS_END, ROUTE_END):
                body(n, n % 2, n // 2, True, False)
                if beside:
                    beside(n)
            before = link.n if link else 0
            with engine.Fori(0, E // 2) as i:
                if link:
                    link.base = i * links
                for k in range(6):
                    body(6 * i + (ROUTE_END + k), k % 2, 3 * i + (ROUTE_END + k) // 2, True, False)
                    if first:
                        first(2 * i + k // 3, k % 3)
            if link:
                assert link.n - before == links, link.n - before
                link.base, link.n = 0, before + E // 2 * links
            for n in range(MAX_END, SPLIT_AT):
                body(n, n % 2, n // 2, True, False)
            if middle:
                middle()
            pieces = ((0, 1), (2,), (3, 4), (5,))
            with engine.Fori(0, E // 2 - 1) as i:
                for k in range(4):
                    body(4 * i + (SPLIT_AT + k), k % 2, 2 * i + (SPLIT_AT + k) // 2, True, False)
                    if second:
                        for m in pieces[k]:
                            second(2 * i + m // 3, m % 3)
            for k in range(4):
                n = TILES - 4 + k
                body(n, n % 2, n // 2, True, False)
                if second:
                    for m in pieces[k]:
                        second(E - 2 + m // 3, m % 3)

        def routed_blocks(engine, body):
            for k in range(4):
                body(N_SH + k, k % 2, (N_SH + k) // 2, k > 0, True)
            with engine.Fori(0, BLOCKS // 2 - 3) as i:
                for k in range(2):
                    body(2 * i + (N_SH + 4 + k), k, i + (N_SH // 2 + 2), True, True)
            for k in range(2):
                body(N_ALL - 2 + k, k, N_ALL // 2 - 1, True, k == 0)

        def power_scale(dve, link, r):
            link.link(dve, nc.vector.tensor_scalar(top[:, r], top[:, r], 1e-9, None, ALU.max))
            link.link(dve, nc.vector.tensor_scalar(top[:, r].bitcast(I32), top[:, r].bitcast(I32), 0x7F800000,
                                                   None, ALU.bitwise_and))
            link.link(dve, nc.vector.reciprocal(inv[:, r], top[:, r]))
            link.link(dve, nc.vector.tensor_scalar(wsc[:, r], inv[:, r], 2.0 ** 14, None, ALU.mult))

        def scale_columns(dve, link, r):
            power_scale(dve, link, r)
            nc.vector.tensor_scalar(silu_s[:, r:r + 1], top[:, r, 0:1], 2.0 ** -25, None, ALU.mult)
            nc.vector.tensor_scalar(h_s[:, r:r + 1], inv[:, r, 0:1], 2.0 ** -28, None, ALU.mult)
            link.link(dve, nc.vector.scalar_tensor_tensor(out=y_s[:, r:r + 1], in0=top[:, r, 0:1],
                                                          scalar=2.0 ** -11, in1=top[:, r, 1:2],
                                                          op0=ALU.mult, op1=ALU.mult))
            link.link(dve, nc.vector.tensor_tensor(y_s[:, r:r + 1], y_s[:, r:r + 1], top[:, r, 2:3], ALU.mult))
            nc.vector.tensor_copy(wsc[:, r, 3:4], wsc[:, r, 0:1]).then_inc(S["wlo_done" if r == 0 else "top_in"], 1)

        MATS = ((WG, CC * HID), (WU, CC * HID), (WD, HC * C))

        block = ctx.enter_context(nc.Block())

        @block.sync
        def _(sp):
            def load_x(b, par):
                sp.dma_start(x_in[:, par], xv[b]).then_inc(x_loaded[par], 16)

            def load_group(n, g):
                j = g // 2
                sp.wait_ge(S["qkl_done"], 4 * n + 2 * j + 2)
                sp.sem_inc(S["sp_passed"], 1)
                if some(4 * UN * n + UN * (g + 1) - 4 * UN):
                    sp.wait_ge(S["t_in"], 4 * UN * n + UN * (g + 1) - 4 * UN)
                    sp.sem_inc(S["sp_passed"], 1)
                r0 = 64 * (g % 2)
                for quad, (qs, ks) in enumerate(((qkh, qkh), (qkh, qkl), (qkl, qkh))):
                    for t in range(2):
                        sp.dma_start(q_op[32 * quad:32 * quad + 32, 2 * g + t, :],
                                     qs[r0 + 32 * t:r0 + 32 * t + 32, 2 * j, :]).then_inc(ops_in[g], 16)
                    for h in range(GH):
                        row = 32 * quad + HD * (h % 2)
                        sp.dma_start(k_op[row:row + HD, GH * g + h, :],
                                     ks[r0 + HD * h:r0 + HD * (h + 1), 2 * j + 1, :]).then_inc(ops_in[g], 16)

            sp.dma_start(wa[:, 0:2, :], w_attn.rearrange("(k p) n -> p k n", p=P)).then_inc(S["w_in"], 16)
            sp.wait_ge(S["pool_const"], 1)
            sp.dma_start(wa[0:1, 2, :], b_attn.unsqueeze(0)).then_inc(S["w_in"], 16)
            sp.dma_start(cs[:], rope.unsqueeze(0).broadcast_to([P, 2, 256])).then_inc(S["w_in"], 16)
            load_x(0, 0)
            load_x(1, 1)
            sp.dma_start(bvb[:], b_attn[2 * C:].unsqueeze(0).broadcast_to([P, C])).then_inc(S["const_in"], 16)
            sp.dma_start(bpb[:], b_proj.unsqueeze(0).broadcast_to([P, C])).then_inc(S["const_in"], 16)
            sp.dma_start(wp[:], w_proj.rearrange("(k p) n -> p k n", p=P)).then_inc(S["const_in"], 16)
            sp.wait_ge(S["pool_const"], 5)
            for g in range(2):
                load_group(0, g)
            sp.dma_start(gate_t[:], gate_w).then_inc(S["misc_in"], 16)
            sp.dma_start(lns[:, 0], ln_scale).then_inc(S["misc_in"], 16)
            sp.dma_start(lns[:, 1], ln_bias).then_inc(S["misc_in"], 16)
            sp.wait_ge(S["scales_done"], 1)
            for k, (src, n) in enumerate(((sWg, HID), (sWu, HID), (sWd, C))):
                sp.dma_start(shared_raw[:, k * CC * HID:(k + 1) * CC * HID].rearrange("p (c n) -> p c n", n=n),
                             src.rearrange("(c p) n -> p c n", p=P)).then_inc(S["shw_in"], 16)

            def store_half(b, j):
                sp.wait_ge(S["lo_done"], 2 * b + j + 1)
                sp.sem_inc(S["sp_passed"], 1)
                sp.dma_start(x1v[b, j], x1[:, j]).then_inc(x1_stored[j], 16)
                sp.dma_start(xhlv[b, j], xhl[:, j].rearrange("p t s c -> p t (s c)")
                             ).then_inc(xhl_stored[j], 16)

            def body(b, par, cur, prev, prev2, nxt, nxt2):
                if nxt2:
                    sp.wait_ge(S["xn_done"], b + 1)
                    sp.sem_inc(S["sp_passed"], 1)
                    load_x(b + 2, par)
                if prev:
                    if some(2 * (b - 1)):
                        sp.wait_ge(S["x1_done"], 2 * (b - 1))
                        sp.sem_inc(S["sp_passed"], 1)
                    sp.dma_start(xres[:], xv[b - 1]).then_inc(S["res_in"], 16)
                if cur:
                    load_group(b, 2)
                if prev2:
                    store_half(b - 2, 1)
                if cur:
                    load_group(b, 3)
                if nxt:
                    load_group(b + 1, 0)
                    load_group(b + 1, 1)
                if prev:
                    store_half(b - 1, 0)
                if not cur:
                    store_half(b - 1, 1)

            batches(sp, body)

            sp.wait_ge(S["lo_done"], 2 * NB)
            for stored in (*x1_stored, *xhl_stored):
                sp.wait_ge(stored, 16 * NB)
            def rows(n, par):
                if some(n - 1):
                    sp.wait_ge(S["xT_in"], n - 1)
                    sp.sem_inc(S["sp_passed"], 1)
                sp.dma_start(xrow[:, par], xhl_d[bass.ds(n * P, P), :]).then_inc(row_loaded[par], 16)

            def residual_rows(n, par):
                if some(n - 1):
                    sp.wait_ge(S["y_out"], n - 1)
                    sp.sem_inc(S["sp_passed"], 1)
                sp.dma_start(x1t[:, par], x1_d[bass.ds(n * P, P), :]).then_inc(x1_loaded[par], 16)

            def logit_rows(q, buf):
                if some(2 * q - 6):
                    sp.wait_ge(S["lxT_in"], 2 * q - 6)
                    sp.sem_inc(S["sp_passed"], 1)
                sp.dma_start(lrow[:, buf], xhl_d[bass.ds(q * 4 * P, 4 * P), :].rearrange("(t p) n -> p t n", p=P)
                             ).then_inc(lrow_loaded[buf], 16)

            rows(0, 0)
            logit_rows(0, 0)
            rows(1, 1)
            logit_rows(1, 1)
            residual_rows(0, 0)
            logit_rows(2, 2)
            logit_rows(3, 3)
            sp.wait_ge(S["bconst"], 1)
            sp.dma_start(tok_d.rearrange("(p n) o -> p (n o)", p=P), no_tok[:].rearrange("p n o -> p (n o)")
                         ).then_inc(S["zero_st"], 16)
            sp.dma_start(xhl_d[NTOK:, :], zero_h[:]).then_inc(S["spare_st"], 16)
            sp.dma_start(out[NTOK:, :], zero_h[:].bitcast(F32)).then_inc(S["spare_st"], 16)

            def body(n, par, half, prev, with_logits):
                if not isinstance(n, int) or n < TILES - 2:
                    rows(n + 2, par)
                if not isinstance(n, int) or n < TILES - 1:
                    residual_rows(n + 1, 1 - par)
                if prev:
                    sp.wait_ge(S["y_out"], n)
                    sp.sem_inc(S["sp_passed"], 1)
                    sp.dma_start(out[bass.ds((n - 1) * P, P), :], ysb[:, 1 - par]).then_inc(y_stored[1 - par], 16)
                if with_logits:
                    logit_rows(2 * n + 4, 2 * par)
                    logit_rows(2 * n + 5, 2 * par + 1)

            def load_matrix(e, k):
                if some(48 * e + 16 * k):
                    sp.wait_ge(S["w_exp"], 48 * e + 16 * k)
                    sp.sem_inc(S["sp_passed"], 1)
                (off, n), src = MATS[k], (Wg, Wu, Wd)[k]
                dst = wraw[:, bass.ds(e + 1, 1), off // 2:off // 2 + n]
                w = src[bass.ds(e, 1)].rearrange("o (c p) n -> p (o c) n", p=P)
                sp.dma_start(dst.rearrange("p o (c n) -> p (o c) n", n=w.shape[2]), w).then_inc(S["w_exp"], 16)

            for n in range(2):
                body(n, n, 0, n > 0, True)
            with sp.Fori(1, LOGITS_END // 2 - 1) as i:
                for k in range(2):
                    body(2 * i + k, k, i, True, True)
            for n in range(LOGITS_END - 2, ROUTE_END):
                body(n, n % 2, n // 2, True, False)
                if 0 <= n - LOADS_AT < 3 * (E // 2):
                    load_matrix((n - LOADS_AT) // 3, (n - LOADS_AT) % 3)
            with sp.Fori(0, E // 4) as i:
                for k in range(6):
                    body(6 * i + (ROUTE_END + k), k % 2, 0, True, False)
                    load_matrix(2 * i + (E // 2 + k // 3), k % 3)
            with sp.Fori(E // 4, E // 2) as i:
                for k in range(6):
                    body(6 * i + (ROUTE_END + k), k % 2, 0, True, False)
            for n in range(MAX_END, SPLIT_AT):
                body(n, n % 2, 0, True, False)
            with sp.Fori(0, E // 2 - 1) as i:
                for k in range(4):
                    body(4 * i + (SPLIT_AT + k), k % 2, 0, True, False)
            for n in range(TILES - 4, TILES):
                if n == TILES - 1:
                    sp.wait_ge(scattered[0], 16 * TILES)
                    sp.wait_ge(scattered[1], 16 * TILES)
                    sp.dma_start(tok_rows[:].rearrange("p n o -> p (n o)"), tok_d.rearrange("(p n) o -> p (n o)", p=P)
                                 ).then_inc(S["rows_in"], 16)
                body(n, n % 2, 0, True, False)
            n = TILES - 1
            sp.wait_ge(S["y_out"], n + 1)
            sp.dma_start(out[n * P:(n + 1) * P, :], ysb[:, n % 2]).then_inc(y_stored[n % 2], 16)

        @block.gpsimd
        def _(pool):
            link = Count(S["pool_link"])
            nc.gpsimd.memset(wa[:, 2, :], 0.0).then_inc(S["pool_const"], 1)
            link.link(pool, nc.gpsimd.memset(ident[:], 0.0))
            link.link(pool, nc.gpsimd.affine_select(
                out=ident[:], in_=ident[:], compare_op=ALU.not_equal, fill=1.0, base=0,
                pattern=[[-1, P]], channel_multiplier=1))
            nc.gpsimd.tensor_copy(ident_b[:], ident[:])
            nc.gpsimd.tensor_copy(ident_h[:], ident[:])
            nc.gpsimd.memset(one[:], 1.0)
            nc.gpsimd.memset(ones_f[:], 1.0)
            nc.gpsimd.memset(neghalf[:], -0.5).then_inc(S["pool_const"], 1)
            link.link(pool, nc.gpsimd.memset(mask[:], 0.0))
            nc.gpsimd.affine_select(out=mask[:], in_=mask[:], compare_op=ALU.is_ge, fill=MASKED, base=0,
                                    pattern=[[-1, P]], channel_multiplier=1).then_inc(S["pool_const"], 1)
            nc.gpsimd.memset(q_op[:], 0.0).then_inc(S["pool_const"], 1)
            pool.wait_ge(S["k_zeroed"], 1)
            pool.wait_ge(S["pool_const"], 4)
            k_sel = k_op[96:128].rearrange("p (g h) n -> p g h n", h=GH)
            nc.gpsimd.affine_select(out=k_sel, in_=k_sel, compare_op=ALU.not_equal, fill=-SHIFT_UNIT, base=0,
                                    pattern=[[0, NG], [-1, GH], [0, T]],
                                    channel_multiplier=1).then_inc(S["pool_const"], 1)
            pool.wait_ge(S["pool_const"], 5)
            def input_rstd(n):
                pool.wait_ge(S["var_done"], n + 1)
                pool.sem_inc(S["pool_passed"], 1)
                nc.gpsimd.tensor_tensor(rstd[:], mv[:, :, 1], neghalf[:], ALU.pow).then_inc(S["rstd_done"], 1)

            input_rstd(0)
            pool.wait_ge(S["attn_w"], 1)
            nc.gpsimd.partition_all_reduce(qk_top[:], qk_max[:], P, RMAX).then_inc(S["qk_topped"], 1)

            input_rstd(1)

            def residual_rstd(bp, j):
                pool.wait_ge(S["varb_done"], 2 * bp + j + 1)
                pool.sem_inc(S["pool_passed"], 1)
                nc.gpsimd.tensor_tensor(rstdb[:], mvb[:, :, 1], neghalf[:, 0:2],
                                        ALU.pow).then_inc(S["rstdb_done"], 1)

            def select(G, u, half):
                pool.wait_ge(S["exp_done"], UN * G + u + 1)
                pool.sem_inc(S["pool_passed"], 1)
                bankv = prob[:, half, u, :]
                if u < 4:
                    v, pat = bankv[:, 0:P], [[1, P]]
                elif u < 8:
                    v, pat = bankv.rearrange("p (s n) -> p s n", n=P)[:, 0:4:3, :], [[0, 2], [1, P]]
                else:
                    v, pat = bankv.rearrange("p (s n) -> p s n", n=P)[:, 0:4:2, :], [[0, 2], [1, P]]
                nc.gpsimd.affine_select(out=v, in_=v, compare_op=ALU.is_ge, fill=0.0, base=0, pattern=pat,
                                        channel_multiplier=-1).then_inc(S["sel_done"], 1)

            def body(b, par, cur, prev, prev2, nxt, nxt2):
                for g in range(NG):
                    G = 4 * b + g
                    has1 = (cur or g < 1) and (prev or g >= 1)
                    has2 = (cur or g < 2) and (prev or g >= 2)
                    for s in range(UN):
                        if s >= LAG - UN and has1:
                            select(G - 1, s + UN - LAG, (g - 1) % 2)
                        elif s < LAG - UN and has2:
                            select(G - 2, s + 2 * UN - LAG, g % 2)
                        if prev:
                            for t in range(NT):
                                if (g, s) == X_BIAS[t]:
                                    if t == 0:
                                        pool.wait_ge(S["const_in"], 48)
                                        pool.wait_ge(S["res_in"], 16 * b)
                                        pool.sem_inc(S["pool_passed"], 1)
                                    last = nc.gpsimd.tensor_tensor(xres[:, t], xres[:, t], bpb[:], ALU.add)
                                    if t == NT - 1:
                                        last.then_inc(S["xb_done"], 1)
                        if nxt2:
                            if (g, s) == RSTD:
                                input_rstd(b + 2)
                        for j, bp, there in layernorm_of(b, prev, prev2):
                            if there and (g, s) == RSTD_B[j]:
                                residual_rstd(bp, j)
                        if not cur and (g, s) == PREP_TOP:
                            pool.wait_ge(S["gprep"], 1)
                            nc.gpsimd.partition_all_reduce(top[:, 1:3, :], top[:, 1:3, :], P, RMAX
                                                           ).then_inc(S["topped"], 1)
                if not cur:
                    residual_rstd(b - 1, 1)

            batches(pool, body)

            pool.wait_ge(S["lo_done"], 2 * NB)
            for stored in (*x1_stored, *xhl_stored):
                pool.wait_ge(stored, 16 * NB)
            nc.gpsimd.memset(rhalf[:], -0.5)
            nc.gpsimd.memset(zero_h[:], 0.0)
            nc.gpsimd.memset(no_tok[:, :, 1], 0)
            nc.gpsimd.iota(no_tok[:, :, 0], [[0, BLOCKS]], base=NTOK, channel_multiplier=1).then_inc(S["bconst"], 1)
            nc.gpsimd.memset(ones_b[:], 1.0)
            nc.gpsimd.memset(zeros[:], 0.0)
            nc.gpsimd.iota(iota_e[:], [[1, E]], base=0, channel_multiplier=0, allow_small_or_imprecise_dtypes=True)
            nc.gpsimd.iota(iota_j[:], [[P, TILES]], base=0, channel_multiplier=0,
                           allow_small_or_imprecise_dtypes=True)
            for k in range(2):
                nc.gpsimd.iota(tok_w[:, :, k, 0], [[P, TILES]], base=0, channel_multiplier=1)
            link.link(pool, nc.gpsimd.memset(before_b[:], 1.0))
            link.link(pool, nc.gpsimd.affine_select(out=before_b[:], in_=before_b[:], compare_op=ALU.is_gt,
                                                    fill=0.0, base=0, pattern=[[1, P]], channel_multiplier=-1))
            nc.gpsimd.iota(iota_b[:], [[1, BLOCKS]], base=0, channel_multiplier=0,
                           allow_small_or_imprecise_dtypes=True).then_inc(S["bconst"], 1)
            pool.wait_ge(S["bconst"], 2)
            pool.wait_ge(S["route_var"], 1)
            nc.gpsimd.tensor_tensor(rvar[:, 1], rvar[:, 0], rhalf[:], ALU.pow).then_inc(S["route_rstd"], 1)
            pool.wait_ge(S["zero_st"], 16)
            pool.wait_ge(S["slots_done"], 1)
            pool.wait_ge(S["weights_done"], 1)

            def scatter(t, par, i):
                if some(32 * i):
                    pool.wait_ge(scattered[par], 32 * i)
                    pool.sem_inc(S["pool_passed"], 1)
                nc.gpsimd.tensor_copy(to_col[:, par], dest_i[:, bass.ds(t, 1), :].rearrange("p o k -> p (o k)"))
                nc.gpsimd.tensor_copy(tw_col[:, par], tok_w[:, bass.ds(t, 1)].rearrange("p o k w -> p (o k w)")
                                      ).then_inc(S["scol"], 1)
                pool.wait_ge(S["scol"], t + 1)
                pool.sem_inc(S["pool_passed"], 1)
                for k in range(2):
                    pool.indirect_dma_start(
                        out=tok_d, out_offset=bass.IndirectOffsetOnAxis(ap=to_col[:, par, k:k + 1], axis=0),
                        in_=tw_col[:, par, 2 * k:2 * k + 2], in_offset=None).then_inc(scattered[par], 16)

            for par in range(2):
                scatter(par, par, 0)
            with pool.Fori(1, BEFORE_MAX // 2) as i:
                for par in range(2):
                    scatter(2 * i + par, par, i)
            pool.wait_ge(S["wmax_done"], 3 * E)
            nc.gpsimd.partition_all_reduce(top[:, 0, 0:3], run3[:], P, RMAX).then_inc(S["topped"], 1)
            with pool.Fori(BEFORE_MAX // 2, TILES // 2) as i:
                for par in range(2):
                    scatter(2 * i + par, par, i)
            pool.wait_ge(S["rows_in"], 16)
            pool.wait_ge(S["spare_st"], 32)

            def gather(n, par):
                pool.wait_ge(S["xT_in"], n - 1)
                pool.sem_inc(S["pool_passed"], 1)
                nc.gpsimd.tensor_copy(ga_col[:, par, :], tok_rows[:, bass.ds(n - N_SH, 1), 0]
                                      ).then_inc(S["gcol"], 1)
                pool.wait_ge(S["gcol"], n - (N_SH - 1))
                pool.sem_inc(S["pool_passed"], 1)
                pool.indirect_dma_start(
                    out=xrow[:, par], out_offset=None, in_=xhl_d,
                    in_offset=bass.IndirectOffsetOnAxis(ap=ga_col[:, par, :], axis=0),
                ).then_inc(row_gathered[par], 16)

            def add(n, par):
                nc.gpsimd.tensor_copy(ad_col[:, par, :], tok_rows[:, bass.ds(n - N_SH, 1), 0]
                                      ).then_inc(S["acol"], 1)
                pool.wait_ge(S["acol"], n - (N_SH - 1))
                pool.sem_inc(S["pool_passed"], 1)
                if some(n - N_SH):
                    pool.wait_ge(S["y_added"], 16 * (n - N_SH))
                    pool.sem_inc(S["pool_passed"], 1)
                pool.wait_ge(S["y_out"], n + 1)
                pool.sem_inc(S["pool_passed"], 1)
                pool.indirect_dma_start(
                    out=out, out_offset=bass.IndirectOffsetOnAxis(ap=ad_col[:, par, :], axis=0),
                    in_=ysb[:, par], in_offset=None, compute_op=ALU.add).then_inc(S["y_added"], 16)

            for n in range(N_SH, N_SH + 4):
                gather(n, n % 2)
            for par in range(2):
                pool.wait_ge(y_stored[par], 16 * (TILES // 2))
            for n in range(N_SH, N_SH + 2):
                gather(n + 4, n % 2)
                add(n, n % 2)
            with pool.Fori(0, BLOCKS // 2 - 3) as i:
                for par in range(2):
                    gather(2 * i + (N_SH + 6 + par), par)
                    add(2 * i + (N_SH + 2 + par), par)
            for n in range(N_ALL - 4, N_ALL):
                add(n, n % 2)
            pool.wait_ge(S["y_added"], 16 * BLOCKS)

        @block.scalar
        def _(act):
            def normalise(n, par, t):
                if t == 0:
                    act.wait_ge(S["shift_done"], n + 1)
                    if some(2 * n):
                        act.wait_ge(S["xnT_in"], 2 * n)
                last = nc.scalar.activation(xn[:, t], x_in[:, par, t], ACT.Identity, bias=shift[:, t:t + 1],
                                            scale=rstd[:, t:t + 1])
                if t == NT - 1:
                    last.then_inc(S["xn_done"], 1)

            def xn_high(n, c, src=ps_q):
                act.wait_ge(S["xnT_in"], 2 * n + c + 1)
                if some(4 * n):
                    act.wait_ge(S["qk_in"], 4 * n)
                nc.scalar.copy(xh[:, c, :], src[:]).then_inc(S["xh_done"], 1)

            def qk_high(n, i, src=ps_q):
                act.wait_ge(S["qk_in"], 4 * n + i + 1)
                for g in (0, 1) if i < 2 else (2, 3):
                    if some(LOADS * n):
                        act.wait_ge(ops_in[g], LOADS * n)
                nc.scalar.activation(qkh[:, i, :], src[:], ACT.Identity,
                                     bias=bcol[:, i:i + 1]).then_inc(S["qkh_done"], 1)

            def prologue():
                act.wait_ge(S["pool_const"], 4)
                for t in range(NT):
                    normalise(0, 0, t)
                for c in range(2):
                    xn_high(0, c, XN_BANK[c])
                act.wait_ge(S["scales_done"], 1)
                for i in range(4):
                    qk_high(0, i, QK_BANK[i])
                for t in range(NT):
                    normalise(1, 1, t)

            prologue()

            def exponentials(G, u, half):
                if u == 0 and some(G - 1):
                    act.wait_ge(S["pv_in"], G - 1)
                act.wait_ge(S["t_in"], UN * G + u + 1)
                nc.scalar.activation(prob[:, half, u, :], ps_t[u % 2][:], ACT.Exp,
                                     scale=exp_scale[:]).then_inc(S["exp_done"], 1)

            def residual_high(bp, j):
                act.wait_ge(S["xf_done"], 2 * bp + j + 1)
                if some(16 * bp):
                    act.wait_ge(xhl_stored[j], 16 * bp)
                nc.scalar.activation(xhl[:, j, :, 0, :], xf[:], ACT.Copy, scale=X_SCALE
                                     ).then_inc(S["hi_done"], 1)

            def body(b, par, cur, prev, prev2, nxt, nxt2):
                for g in range(NG):
                    G = 4 * b + g
                    has1 = (cur or g < 1) and (prev or g >= 1)
                    has2 = (cur or g < 2) and (prev or g >= 2)
                    for s in range(UN):
                        if s == M_ROWS and has1:
                            act.wait_ge(S["m_in"], G)
                            pair = 2 * ((g - 1) % 4)
                            nc.scalar.activation(
                                q_op[96:96 + GH, pair:pair + 2, :],
                                ps_m[0:GH, :].unsqueeze(1).broadcast_to([GH, 2, T]),
                                ACT.Copy, scale=1.0 / SHIFT_UNIT).then_inc(S["m_done"], 1)
                        if s >= LAG - UN and has1:
                            exponentials(G - 1, s + UN - LAG, (g - 1) % 2)
                        elif s < LAG - UN and has2:
                            exponentials(G - 2, s + 2 * UN - LAG, g % 2)
                        if s == O_OUT and has2:
                            opar = par if g >= 2 else 1 - par
                            nb = b if g >= 2 else b - 1
                            act.wait_ge(S["pv_in"], G - 1)
                            if some(4 * (nb - 1)):
                                act.wait_ge(S["ot_in"], 4 * (nb - 1))
                            nc.scalar.copy(o_t[:, opar, (g - 2) % 4, :], ps_o[:]).then_inc(S["o_done"], 1)
                        if nxt2:
                            for t in range(NT):
                                if (g, s) == NORMALISE[t]:
                                    normalise(b + 2, par, t)
                        if nxt:
                            for c in range(2):
                                if (g, s) == XN_HIGH[c]:
                                    xn_high(b + 1, c)
                            for i in range(4):
                                if (g, s) == QK_HIGH[i]:
                                    qk_high(b + 1, i)
                        if prev:
                            for j in range(2):
                                if (g, s) == Y_OUT[j]:
                                    k = 2 * (b - 1) + j
                                    act.wait_ge(S["yT_in"], k + 1)
                                    if some(k):
                                        act.wait_ge(S["pr_in"], k)
                                    nc.scalar.copy(y_t[:].rearrange("p t c n -> p (t c n)"),
                                                   ps_y[:]).then_inc(S["yT_done"], 1)
                        for j, bp, there in layernorm_of(b, prev, prev2):
                            if there and (g, s) == HIGH[j]:
                                residual_high(bp, j)
                        if not cur and (g, s) in PREP_HIGH:
                            m = PREP_HIGH.index((g, s))
                            off, n = MATS[m]
                            act.wait_ge(S["top_in"], 1)
                            nc.scalar.activation(wsh[:, off:off + n], shared_raw[:, off // 2:off // 2 + n], ACT.Copy,
                                                 scale=wsc[:, 1, m:m + 1]).then_inc(S["shsplit_done"], 1)
                if not cur:
                    residual_high(b - 1, 1)

            batches(act, body)

            def take_pair(r):
                act.wait_ge(S["lxT_in"], r + 1)
                if some(r - 1):
                    act.wait_ge(S["lg_in"], r - 1)
                nc.scalar.copy(xtl[:, 1].rearrange("p t c n -> p (t c n)"), ps_lx[1]).then_inc(S["lxt_done1"], 1)

            def silu(n, par, r):
                act.wait_ge(S["g_in"], n + 1)
                if some(n - 1):
                    act.wait_ge(S["h_done"], n - 1)
                nc.scalar.activation(sg[:, par], ps_g[:], ACT.Silu, scale=silu_s[:, r:r + 1]
                                     ).then_inc(S["sg_done"], 1)

            def high(n):
                act.wait_ge(S["hT_in"], n + 1)
                if some(n):
                    act.wait_ge(S["yp_in"], n)
                nc.scalar.copy(hth[:].rearrange("p c n -> p (c n)"), ps_h[:]).then_inc(S["hh_done"], 1)

            def shared(n, par, half, prev, with_logits):
                if prev:
                    high(n - 1)
                silu(n, par, 1)
                if with_logits:
                    take_pair(4 * n + 1)
                    take_pair(4 * n + 3)

            def second(e, k):
                off, n = MATS[k]
                act.wait_ge(S["wlo_done"], 3 * e + 1)
                nc.scalar.activation(wbuf[:, bass.ds(e * SLOT + off, n)],
                                     wraw[:, bass.ds(e + 1, 1), off // 2:off // 2 + n],
                                     ACT.Copy, scale=wsc[:, 0, k:k + 1]).then_inc(S["whi_done"], 1)

            def beside(n):
                if n == EXP_AT:
                    act.wait_ge(S["exp_in"], 1)
                    nc.scalar.activation(tmp[:], tmp[:], ACT.Exp)
                    nc.scalar.activation(m12[:, 3], m12[:, 2], ACT.Exp).then_inc(S["exp_out"], 1)

            shared_blocks(act, shared, beside, second=second)
            high(N_SH - 1)
            act.wait_ge(S["row_w_done"], 1)
            for par in range(2):
                act.wait_ge(y_stored[par], 16 * (TILES // 2))

            def result(n, par):
                act.wait_ge(S["yp_in"], n + 1)
                if some(n - N_SH - 1):
                    act.wait_ge(S["y_added"], 16 * (n - (N_SH + 1)))
                nc.scalar.activation(ysb[:, par], ps_z[:, 0:C], ACT.Copy, scale=row_w[:, bass.ds(n - N_SH, 1)]
                                     ).then_inc(S["y_out"], 1)

            def routed(n, par, half, prev, nxt):
                if prev:
                    high(n - 1)
                silu(n, par, 0)
                if prev:
                    result(n - 1, 1 - par)

            routed_blocks(act, routed)
            high(N_ALL - 1)
            result(N_ALL - 1, (N_ALL - 1) % 2)

        @block.vector
        def _(dve):
            link = Count(S["dve_link"])

            def stats(n, par, j):
                if j == 0:
                    dve.wait_ge(x_loaded[par], 8 * n + 16 - 8 * par)
                    if some(n):
                        dve.wait_ge(S["xn_done"], n)
                for t in (2 * j, 2 * j + 1):
                    last = nc.vector.bn_stats(st6[:, t], x_in[:, par, t])
                if j == 1:
                    last.then_inc(S["stats_taken"], 1)

            def variance(n):
                dve.wait_ge(S["stats_taken"], n + 1)
                dve.sem_inc(S["dve_passed"], 1)
                for t in range(NT):
                    last = nc.vector.bn_aggr(mv[:, t], st6[:, t])
                link.link(dve, last)
                nc.vector.tensor_scalar(mv[:, :, 1], mv[:, :, 1], EPS, None,
                                        ALU.add).then_inc(S["var_done"], 1)

            def input_shift(n):
                dve.wait_ge(S["rstd_done"], n + 1)
                nc.vector.scalar_tensor_tensor(out=shift[:], in0=mv[:, :, 0], scalar=-1.0, in1=rstd[:],
                                               op0=ALU.mult, op1=ALU.mult).then_inc(S["shift_done"], 1)

            def xn_low(n, c, src=ps_q):
                dve.wait_ge(S["xh_done"], 2 * n + c + 1)
                nc.vector.tensor_tensor(xl[:, c, :], src[:], xh[:, c, :].bitcast(F32),
                                        ALU.subtract).then_inc(S["xl_done"], 1)

            def qk_low(n, i, src=ps_q):
                dve.wait_ge(S["qkh_done"], 4 * n + i + 1)
                nc.vector.scalar_tensor_tensor(out=qkl[:, i, :], in0=src[:], scalar=bcol[:, i:i + 1],
                                               in1=qkh[:, i, :], op0=ALU.add,
                                               op1=ALU.subtract).then_inc(S["qkl_done"], 1)

            def values(n, par, j, src=ps_q):
                dve.wait_ge(S["v_in"], 2 * n + j + 1)
                if some(4 * (n - 1)):
                    dve.wait_ge(S["pv_in"], 4 * (n - 1))
                for t in range(2):
                    last = nc.vector.tensor_tensor(
                        v_op[:, par, 2 * j + t, :, 0:HD],
                        src[:, 256 * t:256 * t + 256].rearrange("p (h d) -> p h d", d=HD),
                        bvb[:].rearrange("p (h d) -> p h d", d=HD), ALU.add)
                last.then_inc(S["v_done"], 1)

            def prologue():
                nc.vector.memset(k_op[:], 0.0).then_inc(S["k_zeroed"], 1)
                for par in range(2):
                    nc.vector.memset(v_op[:, par, :, :, HD:], 0.0)
                link.link(dve, nc.vector.memset(mx[:], 0.0))
                link.link(dve, nc.vector.memset(v_op[:, :, :, :, HD:HD + 1].rearrange(
                    "p a t h d -> p (a t h) d"), 1.0))
                stats(0, 0, 0)
                stats(0, 0, 1)
                variance(0)
                input_shift(0)
                dve.wait_ge(S["w_in"], 48)
                ev = wa[:, :, 0:512].rearrange("p k (i e) -> p k i e", e=2)[:, :, :, 0]
                od = wa[:, :, 0:512].rearrange("p k (i e) -> p k i e", e=2)[:, :, :, 1]
                cosv = cs[:, 0:1, :].broadcast_to([P, 3, 256])
                sinv = cs[:, 1:2, :].broadcast_to([P, 3, 256])
                nc.vector.tensor_tensor(rope_t[:, 0], ev, sinv, ALU.mult)
                link.link(dve, nc.vector.tensor_tensor(rope_t[:, 1], od, sinv, ALU.mult))
                nc.vector.tensor_tensor(ev, ev, cosv, ALU.mult)
                link.link(dve, nc.vector.tensor_tensor(od, od, cosv, ALU.mult))
                nc.vector.tensor_tensor(ev, ev, rope_t[:, 1], ALU.subtract)
                link.link(dve, nc.vector.tensor_tensor(od, od, rope_t[:, 0], ALU.add))
                for s in range(2):
                    last = nc.vector.tensor_reduce(qk_max[:, s:s + 1], wa[:, :, 256 * s:256 * s + 256],
                                                   mybir.AxisListType.XY, ALU.max, apply_absolute_value=True)
                last.then_inc(S["attn_w"], 1)
                dve.wait_ge(S["qk_topped"], 1)
                link.link(dve, nc.vector.tensor_scalar(qk_top[:], qk_top[:], 1e-30, None, ALU.max))
                link.link(dve, nc.vector.tensor_scalar(qk_top[:].bitcast(I32), qk_top[:].bitcast(I32),
                                                       0x7F800000, None, ALU.bitwise_and))
                link.link(dve, nc.vector.reciprocal(qk_inv[:], qk_top[:]))
                link.link(dve, nc.vector.tensor_scalar(qk_scale[:], qk_inv[:], 16.0, None, ALU.mult))
                nc.vector.scalar_tensor_tensor(out=exp_scale[:], in0=qk_top[:, 0:1], scalar=1.0 / 256,
                                               in1=qk_top[:, 1:2], op0=ALU.mult, op1=ALU.mult)
                for s in range(2):
                    w_s = wa[:, :, 256 * s:256 * s + 256]
                    last = nc.vector.tensor_scalar(w_s, w_s, qk_scale[:, s:s + 1], None, ALU.mult)
                last.then_inc(S["attn_w"], 1)
                dve.wait_ge(S["biascols"], 1)
                nc.vector.tensor_copy(bcol[:], ps_m[:, 0:4])
                link.link(dve, nc.vector.tensor_copy(wah[:], wa[:, 0:2, :]))
                nc.vector.tensor_tensor(wal[:], wa[:, 0:2, :], wah[:].bitcast(F32),
                                        ALU.subtract).then_inc(S["scales_done"], 1)

            def prologue_qkv():
                dve.wait_ge(S["const_in"], 48)
                for c in range(2):
                    xn_low(0, c, XN_BANK[c])
                for i in range(2):
                    qk_low(0, i, QK_BANK[i])
                for j in range(2):
                    values(0, 0, j, V_BANK[j])
                for i in range(2, 4):
                    qk_low(0, i, QK_BANK[i])
                stats(1, 1, 0)
                stats(1, 1, 1)
                variance(1)
                input_shift(1)

            prologue()
            prologue_qkv()

            def row_max(G, g, u):
                dve.wait_ge(S["s_in"], UN * G + u + 1)
                if u == 0:
                    if some(G - 1):
                        dve.wait_ge(S["m_in"], G - 1)
                src, dst = ps_s[u % 2], mx[:, g % 2]

                def top(lo, n, out):
                    return nc.vector.tensor_reduce(out, src[:, lo:lo + n], AX_X, ALU.max)

                if u < 4:
                    last = top(0, 512, dst[:, 3, u:u + 1])
                elif u < 8:
                    top(0, 384, dst[:, 2, u - 4:u - 3])
                    last = top(384, 128, dst[:, 0, u - 4:u - 3])
                else:
                    c = 2 * (u - 8)
                    last = nc.vector.tensor_reduce(dst[:, 1, c:c + 2],
                                                   src[:].rearrange("p (h n) -> p h n", h=2), AX_X, ALU.max)
                last.then_inc(S["max_done"], 1)

            def divide(bp, q):
                k = 4 * bp + q
                dve.wait_ge(S["ot_in"], k + 1)
                ov = ps_y[:].rearrange("p (h d) -> p h d", d=32)
                link.link(dve, nc.vector.reciprocal(rec[:, q % 2], ov[:, :, HD]))
                if some(2 * bp + q // 2):
                    dve.wait_ge(S["yT_in"], 2 * bp + q // 2)
                nc.vector.tensor_tensor(y[:, q % 2].rearrange("p (h d) -> p h d", d=HD), ov[:, :, 0:HD],
                                        rec[:, q % 2].unsqueeze(2).broadcast_to([P, H, HD]),
                                        ALU.mult).then_inc(S["y_done"], 1)

            def residual(bp, j):
                k = 2 * bp + j
                dve.wait_ge(S["pr_in"], k + 1)
                dve.wait_ge(S["xb_done"], bp + 1)
                if some(16 * bp):
                    dve.wait_ge(x1_stored[j], 16 * bp)
                nc.vector.tensor_tensor(x1[:, j].rearrange("p t c -> p (t c)"), ps_m[:],
                                        xres[:, 2 * j:2 * j + 2].rearrange("p t c -> p (t c)"), ALU.add
                                        ).then_inc(S["x1_done"], 1)

            def residual_stats(bp, j):
                dve.wait_ge(S["x1_done"], 2 * bp + j + 1)
                for t in range(2):
                    last = nc.vector.bn_stats(st6b[:, t], x1[:, j, t])
                last.then_inc(S["x1_taken"], 1)

            def residual_variance(bp, j):
                dve.wait_ge(S["x1_taken"], 2 * bp + j + 1)
                dve.sem_inc(S["dve_passed"], 1)
                for t in range(2):
                    last = nc.vector.bn_aggr(mvb[:, t], st6b[:, t])
                link.link(dve, last)
                link.link(dve, nc.vector.tensor_copy(var_all[:, bass.ds(NT * bp + 2 * j, 2)], mvb[:, :, 1]))
                nc.vector.tensor_scalar(mvb[:, :, 1], mvb[:, :, 1], EPS, None,
                                        ALU.add).then_inc(S["varb_done"], 1)

            def rows(bp, j):
                k = 2 * bp + j
                dve.wait_ge(S["rstdb_done"], k + 1)
                if some(k):
                    dve.wait_ge(S["lo_done"], k)
                for t in range(2):
                    last = nc.vector.tensor_scalar(xf[:, t], x1[:, j, t], mvb[:, t, 0:1], rstdb[:, t:t + 1],
                                                   ALU.subtract, ALU.mult)
                last.then_inc(S["xf_done"], 1)

            def low(bp, j):
                k = 2 * bp + j
                dve.wait_ge(S["hi_done"], k + 1)
                nc.vector.scalar_tensor_tensor(out=xhl[:, j, :, 1, :], in0=xf[:], scalar=X_SCALE,
                                               in1=xhl[:, j, :, 0, :], op0=ALU.mult,
                                               op1=ALU.subtract).then_inc(S["lo_done"], 1)

            def prepare_maxima():
                dve.wait_ge(S["shw_in"], 48)
                dve.wait_ge(S["misc_in"], 48)
                link.link(dve, nc.vector.memset(top[:], 0.0))
                nc.vector.memset(run3[:], 0.0)
                nc.vector.tensor_reduce(top[:, 1, 0:3], shared_raw.rearrange("p (m n) -> p m n", m=3), AX_X,
                                        ALU.max, apply_absolute_value=True)
                for k in range(2):
                    for c in range(CC):
                        last = nc.vector.tensor_scalar(gs_t[:, CC * k + c], gate_t[:, c], lns[:, k, c:c + 1], None,
                                                       ALU.mult)
                link.link(dve, last)
                nc.vector.tensor_reduce(top[:, 2, 0:1], gs_t[:, 0:CC], mybir.AxisListType.XY, ALU.max,
                                        apply_absolute_value=True).then_inc(S["gprep"], 1)

            def prepare_scales():
                dve.wait_ge(S["topped"], 1)
                scale_columns(dve, link, 1)
                power_scale(dve, link, 2)
                nc.vector.tensor_scalar(lg_s[:], top[:, 2, 0:1], 2.0 ** -25, None, ALU.mult)
                link.link(dve, nc.vector.tensor_scalar(gate_hl[:, 0], gs_t[:, 0:CC], wsc[:, 2, 0:1], None,
                                                       ALU.mult))
                nc.vector.scalar_tensor_tensor(out=gate_hl[:, 1], in0=gs_t[:, 0:CC], scalar=wsc[:, 2, 0:1],
                                               in1=gate_hl[:, 0], op0=ALU.mult, op1=ALU.subtract
                                               ).then_inc(S["top_in"], 1)
                dve.wait_ge(S["gsum"], 1)
                link.link(dve, nc.vector.tensor_copy(sgb[:], bank[0][:, 0:2 * E].rearrange("p (k e) -> p k e",
                                                                                           k=2)))

            def prepare_low(m):
                off, n = MATS[m]
                dve.wait_ge(S["shsplit_done"], m + 1)
                nc.vector.scalar_tensor_tensor(out=wsh[:, off + n:off + 2 * n],
                                               in0=shared_raw[:, off // 2:off // 2 + n],
                                               scalar=wsc[:, 1, m:m + 1], in1=wsh[:, off:off + n],
                                               op0=ALU.mult, op1=ALU.subtract).then_inc(S["gprep"], 1)

            def body(b, par, cur, prev, prev2, nxt, nxt2):
                for g in range(NG):
                    G = 4 * b + g
                    for s in range(UN):
                        if cur:
                            row_max(G, g, s)
                        if nxt:
                            for c in range(2):
                                if (g, s) == XN_LOW[c]:
                                    xn_low(b + 1, c)
                            for i in range(4):
                                if (g, s) == QK_LOW[i]:
                                    qk_low(b + 1, i)
                            for j in range(2):
                                if (g, s) == VALUES[j]:
                                    values(b + 1, 1 - par, j)
                        if nxt2:
                            for j in range(2):
                                if (g, s) == STATS[j]:
                                    stats(b + 2, par, j)
                            if (g, s) == VARIANCE:
                                variance(b + 2)
                            if (g, s) == SHIFT:
                                input_shift(b + 2)
                        if prev:
                            for q in range(NT):
                                if (g, s) == DIVIDE[q]:
                                    divide(b - 1, q)
                            for j in range(2):
                                if (g, s) == X1[j]:
                                    residual(b - 1, j)
                                if (g, s) == X1_STATS[j]:
                                    residual_stats(b - 1, j)
                        for j, bp, there in layernorm_of(b, prev, prev2):
                            if there and (g, s) == X1_VARIANCE[j]:
                                residual_variance(bp, j)
                            if there and (g, s) == ROWS[j]:
                                rows(bp, j)
                            if there and (g, s) == LOW[j]:
                                low(bp, j)
                        if not cur and (g, s) == PREP_MAX:
                            prepare_maxima()
                        if not cur and (g, s) == PREP_SCALE:
                            prepare_scales()
                        if not cur and (g, s) in PREP_LOW:
                            prepare_low(PREP_LOW.index((g, s)))
                if not cur:
                    residual_variance(b - 1, 1)
                    rows(b - 1, 1)
                    low(b - 1, 1)

            batches(dve, body, link, DVE_LINKS)

            V = nc.vector
            ranks = ps_r[0][:].rearrange("p (t e) -> p t e", e=E)
            inclt = incl[:].rearrange("p e t -> p t e")

            def per_tile(v):
                return v.unsqueeze(2).broadcast_to([P, TILES, E])

            def per_expert(v):
                return v.unsqueeze(1).broadcast_to([P, TILES, E])

            def step(instruction):
                link.link(dve, instruction)

            def route_logits():
                dve.wait_ge(S["route_rstd"], 1)
                dve.wait_ge(S["lg_in"], TILES // 2)
                pl = ps_l[:].rearrange("p (t e) -> p t e", e=E)
                step(V.scalar_tensor_tensor(out=lg[:], in0=pl, scalar=lg_s[:], in1=per_tile(rvar[:, 1]),
                                            op0=ALU.mult, op1=ALU.mult))
                step(V.tensor_tensor(lg[:], lg[:], per_expert(sgb[:, 1]), ALU.add))

            def largest(k, src):
                step(V.tensor_reduce(m12[:, k], src[:], AX_X, ALU.max))
                step(V.tensor_tensor(tmp[:], src[:], per_tile(m12[:, k]), ALU.is_equal))
                step(V.scalar_tensor_tensor(out=tmp[:], in0=tmp[:], scalar=-float(E), in1=per_expert(iota_e[:]),
                                            op0=ALU.mult, op1=ALU.add))

            def one_hot(k):
                step(V.tensor_reduce(rw[:, 0], tmp[:], AX_X, ALU.min))
                step(V.tensor_scalar(rw[:, 0], rw[:, 0], float(E), None, ALU.add))
                step(V.tensor_tensor(oh[:, k], per_expert(iota_e[:]), per_tile(rw[:, 0]), ALU.is_equal))
                if k == 0:
                    step(V.scalar_tensor_tensor(out=lg2[:], in0=oh[:, 0], scalar=MASKED, in1=lg[:], op0=ALU.mult,
                                                op1=ALU.add))

            def choose():
                V.tensor_tensor(sel[:], oh[:, 0], oh[:, 1], ALU.add).then_inc(S["sel_ready"], 1)
                step(V.tensor_tensor(tmp[:], lg[:], per_tile(m12[:, 0]), ALU.subtract))
                V.tensor_tensor(m12[:, 2], m12[:, 1], m12[:, 0], ALU.subtract).then_inc(S["exp_in"], 1)

            def weigh():
                dve.wait_ge(S["exp_out"], 1)
                step(V.tensor_reduce(rw[:, 0], tmp[:], AX_X, ALU.add))
                step(V.reciprocal(rw[:, 1], rw[:, 0]))
                step(V.tensor_tensor(rw[:, 2], m12[:, 3], rw[:, 1], ALU.mult))
                step(V.scalar_tensor_tensor(out=rw[:, 3], in0=rw[:, 1], scalar=EPS, in1=rw[:, 2], op0=ALU.add,
                                            op1=ALU.add))
                step(V.reciprocal(rw[:, 0], rw[:, 3]))
                V.tensor_tensor(tok_w[:, :, 0, 1].bitcast(F32), rw[:, 1], rw[:, 0], ALU.mult)
                V.tensor_tensor(tok_w[:, :, 1, 1].bitcast(F32), rw[:, 2], rw[:, 0], ALU.mult
                                ).then_inc(S["weights_done"], 1)

            def count():
                dve.wait_ge(S["ranks_in"], 1)
                totals = ps_r[1][:].rearrange("p (t e) -> p e t", e=E)
                for e in range(E):
                    last = V.tensor_tensor_scan(out=incl[:, e], data0=totals[:, e], data1=zeros[:], initial=0.0,
                                                op0=ALU.add, op1=ALU.add)
                step(last)

            def count_blocks():
                cmp = lg2[:].rearrange("p t e -> p (t e)").rearrange("p (e t) -> p e t", e=E)
                step(V.tensor_tensor(cmp, incl[:, :, TILES - 1:TILES].broadcast_to([P, E, TILES]),
                                     iota_j[:].unsqueeze(1).broadcast_to([P, E, TILES]), ALU.is_gt))
                step(V.tensor_reduce(nblk[:, 0], cmp, AX_X, ALU.add))
                step(V.tensor_tensor_scan(out=nblk[:, 1], data0=nblk[:, 0], data1=zeros[:, 0:E], initial=0.0,
                                          op0=ALU.add, op1=ALU.add))
                step(V.tensor_tensor(nblk[:, 2], nblk[:, 1], nblk[:, 0], ALU.subtract))
                step(V.tensor_scalar(nblk[:, 3], nblk[:, 2], float(P), None, ALU.mult))

            def rows_in_order():
                step(V.tensor_tensor(lg[:], inclt, ps_r[1][:].rearrange("p (t e) -> p t e", e=E), ALU.subtract))
                step(V.tensor_tensor(lg[:], lg[:], ranks, ALU.add))
                step(V.tensor_tensor(lg[:], lg[:], per_expert(nblk[:, 3]), ALU.add))

            def place():
                for k in range(2):
                    step(V.tensor_tensor(lg2[:], oh[:, k], lg[:], ALU.mult))
                    step(V.tensor_reduce(slot_f[:, k], lg2[:], AX_X, ALU.add))
                step(V.tensor_copy(slot_i[:], slot_f[:]))
                V.tensor_scalar(row_i[:, 0], slot_i[:], P - 1, None, ALU.bitwise_and)
                step(V.tensor_scalar(row_i[:, 1], slot_i[:], 7, None, ALU.logical_shift_right))
                V.scalar_tensor_tensor(out=dest_i[:].rearrange("p t k -> p k t"), in0=row_i[:, 0],
                                       scalar=float(BLOCKS), in1=row_i[:, 1],
                                       op0=ALU.mult, op1=ALU.add).then_inc(S["slots_done"], 1)

            def experts_of_blocks():
                step(V.tensor_tensor(blk_cmp[:], iota_b[:].unsqueeze(2).broadcast_to([1, BLOCKS, E - 1]),
                                     nblk[0:1, 1, 0:E - 1].unsqueeze(1).broadcast_to([1, BLOCKS, E - 1]),
                                     ALU.is_ge))
                step(V.tensor_reduce(blk_f[:], blk_cmp[:], AX_X, ALU.add))
                V.tensor_scalar(blk_off[:], blk_f[:], float(SLOT), None, ALU.mult).then_inc(S["blk_done"], 1)

            dve.wait_ge(S["lo_done"], 2 * NB)
            for stored in (*x1_stored, *xhl_stored):
                dve.wait_ge(stored, 16 * NB)
            dve.wait_ge(S["bconst"], 2)
            step(V.tensor_scalar(rvar[:, 0], var_all[:], EPS, None, ALU.add))
            step(V.reciprocal(rvar[:, 1], rvar[:, 0]))
            step(V.tensor_tensor(rvar[:, 0], rvar[:, 1], var_all[:], ALU.mult))
            V.tensor_scalar(rvar[:, 0], rvar[:, 0], EPS, None, ALU.add).then_inc(S["route_var"], 1)

            def take_pair(r):
                dve.wait_ge(S["lxT_in"], r + 1)
                if some(r - 1):
                    dve.wait_ge(S["lg_in"], r - 1)
                nc.vector.tensor_copy(xtl[:, 0].rearrange("p t c n -> p (t c n)"), ps_lx[0]
                                      ).then_inc(S["lxt_done0"], 1)

            def take_rows(n, par):
                dve.wait_ge(S["xT_in"], n + 1)
                if some(n - 1):
                    dve.wait_ge(S["u_in"], n - 1)
                nc.vector.tensor_copy(xt[:, par].rearrange("p c n -> p (c n)"), ps_x16[:, 0:2 * C]
                                      ).then_inc(S["xt_done"], 1)

            def low(n):
                dve.wait_ge(S["hh_done"], n + 1)
                nc.vector.tensor_tensor(htl[:].rearrange("p c n -> p (c n)"), ps_h[:],
                                        hth[:].rearrange("p c n -> p (c n)"),
                                        ALU.subtract).then_inc(S["hl_done"], 1)

            def hidden(n, par, r):
                dve.wait_ge(S["u_in"], n + 1)
                dve.wait_ge(S["sg_done"], n + 1)
                if some(n):
                    dve.wait_ge(S["hT_in"], n)
                nc.vector.scalar_tensor_tensor(out=hb[:], in0=ps_u[:], scalar=h_s[:, r:r + 1], in1=sg[:, par],
                                               op0=ALU.mult, op1=ALU.mult).then_inc(S["h_done"], 1)

            def result(n, par, half):
                dve.wait_ge(S["yp_in"], n + 1)
                if some(16 * half):
                    dve.wait_ge(y_stored[par], 16 * half)
                dve.wait_ge(x1_loaded[par], 16 * half + 16)
                nc.vector.scalar_tensor_tensor(out=ysb[:, par], in0=ps_z[:, 0:C], scalar=y_s[:, 1:2],
                                               in1=x1t[:, par], op0=ALU.mult, op1=ALU.add
                                               ).then_inc(S["y_out"], 1)

            def shared(n, par, half, prev, with_logits):
                if with_logits:
                    take_pair(4 * n)
                if prev:
                    low(n - 1)
                hidden(n, par, 1)
                if with_logits:
                    take_pair(4 * n + 2)
                if not isinstance(n, int) or n < TILES - 1:
                    take_rows(n + 1, 1 - par)
                if prev:
                    result(n - 1, 1 - par, half - 1 if par == 0 else half)

            def first(e, k):
                dve.wait_ge(S["w_exp"], 48 * e + 48)
                off, n = MATS[k]
                link.link(dve, nc.vector.tensor_reduce(
                    top[:, 0, k:k + 1], wraw[:, bass.ds(e + 1, 1), off // 2:off // 2 + n].rearrange(
                        "p o n -> p (o n)"), AX_X, ALU.max, apply_absolute_value=True))
                link.link(dve, nc.vector.tensor_tensor(run3[:, k:k + 1], run3[:, k:k + 1], top[:, 0, k:k + 1],
                                                       ALU.max))
                nc.vector.sem_inc(S["wmax_done"], 1)

            def second(e, k):
                off, n = MATS[k]
                dve.wait_ge(S["whi_done"], 3 * e + k + 1)
                nc.vector.scalar_tensor_tensor(
                    out=wbuf[:, bass.ds(e * SLOT + (off + n), n)],
                    in0=wraw[:, bass.ds(e + 1, 1), off // 2:off // 2 + n].rearrange("p o n -> p (o n)"),
                    scalar=wsc[:, 0, k:k + 1], in1=wbuf[:, bass.ds(e * SLOT + off, n)],
                    op0=ALU.mult, op1=ALU.subtract).then_inc(S["wlo_done"], 1)

            take_rows(0, 0)
            def middle():
                dve.wait_ge(S["topped"], 2)
                scale_columns(dve, link, 0)

            AFTER = {8: route_logits, 9: lambda: largest(0, lg), 10: lambda: one_hot(0),
                     11: lambda: largest(1, lg2), 12: lambda: one_hot(1), 13: choose, 15: weigh, 16: count,
                     17: count_blocks, 18: rows_in_order, 19: place, 20: experts_of_blocks}

            def beside(n):
                if n in AFTER:
                    AFTER[n]()

            shared_blocks(dve, shared, beside, first, second, middle, link, 12)
            low(N_SH - 1)
            result(N_SH - 1, (N_SH - 1) % 2, (N_SH - 1) // 2)
            dve.wait_ge(S["rows_in"], 16)
            nc.vector.tensor_scalar(row_w[:], tok_rows[:, :, 1].bitcast(F32), y_s[:, 0:1], None, ALU.mult
                                    ).then_inc(S["row_w_done"], 1)

            def routed(n, par, half, prev, nxt):
                if prev:
                    low(n - 1)
                hidden(n, par, 0)
                if nxt:
                    take_rows(n + 1, 1 - par)

            take_rows(N_SH, 0)
            routed_blocks(dve, routed)
            low(N_ALL - 1)
        @block.tensor
        def _(pe):
            def transpose_xn(n, c, out=None):
                pe.wait_ge(S["xn_done"], n + 1)
                if out is None:
                    out = ps_q
                    if c:
                        pe.wait_ge(S["xl_done"], 2 * n + c)
                    else:
                        pe.wait_ge(S["qkl_done"], 4 * n)
                for t in range(NT):
                    last = nc.tensor.transpose(out[:, P * t:P * (t + 1)], xn[:, t, P * c:P * (c + 1)], ident[:])
                last.then_inc(S["xnT_in"], 1)

            def products(out, pairs):
                n = 3 * len(pairs)
                i = 0
                for (lh, ll), (rh, rl) in pairs:
                    for a, m in ((lh, rh), (lh, rl), (ll, rh)):
                        last = nc.tensor.matmul(out, a, m, start=(i == 0), stop=(i == n - 1))
                        i += 1
                return last

            def project_qk(n, i, out=None):
                if out is not None or i == 0:
                    pe.wait_ge(S["xl_done"], 2 * n + 2)
                elif i == 2:
                    pe.wait_ge(S["v_done"], 2 * n + 2)
                else:
                    pe.wait_ge(S["qkl_done"], 4 * n + i)
                col = 256 * (i % 2) + P * (i // 2)
                out = ps_q if out is None else out
                products(out[:], [((wah[:, c, col:col + P], wal[:, c, col:col + P]),
                                    (xh[:, c, :], xl[:, c, :])) for c in range(2)]).then_inc(S["qk_in"], 1)

            def project_v(n, j, out=None):
                if out is not None:
                    pe.wait_ge(S["xl_done"], 2 * n + 2)
                elif j == 0:
                    pe.wait_ge(S["qkl_done"], 4 * n + 2)
                else:
                    pe.wait_ge(S["v_done"], 2 * n + 1)
                out = ps_q if out is None else out
                for t in range(2):
                    tok = slice(P * (2 * j + t), P * (2 * j + t + 1))
                    last = products(out[:, 256 * t:256 * t + 256],
                                    [((xh[:, c, tok], xl[:, c, tok]),
                                      (wah[:, c, 2 * C:], wal[:, c, 2 * C:])) for c in range(2)])
                last.then_inc(S["v_in"], 1)

            def prologue():
                for c in range(2):
                    transpose_xn(0, c, XN_BANK[c])
                pe.wait_ge(S["attn_w"], 2)
                pe.wait_ge(S["pool_const"], 3)
                for i in range(4):
                    col = 256 * (i % 2) + P * (i // 2)
                    last = nc.tensor.matmul(ps_m[:, i:i + 1], wa[0:1, 2, col:col + P], one[0:1, :],
                                            start=True, stop=True)
                last.then_inc(S["biascols"], 1)
                pe.wait_ge(S["scales_done"], 1)
                for i in range(2):
                    project_qk(0, i, QK_BANK[i])
                for j in range(2):
                    project_v(0, j, V_BANK[j])
                for i in range(2, 4):
                    project_qk(0, i, QK_BANK[i])

            prologue()

            def scores(b, G, g, u):
                if u == 0:
                    pe.wait_ge(ops_in[g], LOADS * (b + 1))
                if some(UN * G + u - 1):
                    pe.wait_ge(S["max_done"], UN * G + u - 1)
                out = ps_s[u % 2]

                def mm(h, q, lo, start):
                    nc.tensor.matmul(out[:, lo:lo + P * (q + 1)],
                                     q_op[0:96, 2 * g + h // 2, P * q:P * (q + 1)],
                                     k_op[0:96, GH * g + h, 0:P * (q + 1)], start=start, stop=False)

                cols = out[:].rearrange("p (s n) -> p s n", n=P)
                if u < 4:
                    mm(u, 3, 0, True)
                    sel, n = cols[:, 3:4, :], 1
                elif u < 8:
                    mm(u - 4, 2, 0, True)
                    mm(u - 4, 0, 384, False)
                    sel, n = cols[:, 2:4, :], 2
                else:
                    mm(2 * (u - 8), 1, 0, True)
                    mm(2 * (u - 8) + 1, 1, 256, False)
                    sel, n = cols[:, 1:4:2, :], 2
                nc.tensor.matmul(sel, ident_b[:], mask[:].unsqueeze(1).broadcast_to([P, n, P]),
                                 start=False, stop=True).then_inc(S["s_in"], 1)

            def maxima(b, G, g):
                pe.wait_ge(S["max_done"], UN * G)
                if some(G - 1):
                    pe.wait_ge(S["m_done"], G - 1)
                if g == 0:
                    if some(2 * (b - 1)):
                        pe.wait_ge(S["x1_done"], 2 * (b - 1))
                if g == 3:
                    if some(2 * (b - 1) + 1):
                        pe.wait_ge(S["x1_done"], 2 * (b - 1) + 1)
                for q in range(NT):
                    last = nc.tensor.transpose(ps_m[0:GH, P * q:P * (q + 1)], mx[:, (g - 1) % 2, q, :], ident[:])
                last.then_inc(S["m_in"], 1)

            def shifted(G, gg, u):
                if u == 0:
                    pe.wait_ge(S["m_done"], G + 1)
                if some(UN * G + u - 1):
                    pe.wait_ge(S["exp_done"], UN * G + u - 1)
                out = ps_t[u % 2]

                def mm(h, k, lo, start, stop):
                    n = T - P * k
                    return nc.tensor.matmul(out[:, lo:lo + n], k_op[:, GH * gg + h, P * k:P * (k + 1)],
                                            q_op[:, 2 * gg + h // 2, P * k:], start=start, stop=stop)

                if u < 4:
                    last = mm(u, 0, 0, True, True)
                elif u < 8:
                    mm(u - 4, 1, 0, True, False)
                    last = mm(u - 4, 3, 384, False, True)
                else:
                    mm(2 * (u - 8), 2, 0, True, False)
                    last = mm(2 * (u - 8) + 1, 2, 256, False, True)
                last.then_inc(S["t_in"], 1)

            def mix(G, gg, vpar, nb, piece):
                if piece == 0:
                    if some(G):
                        pe.wait_ge(S["o_done"], G)
                    pe.wait_ge(S["v_done"], 2 * (nb + 1))
                k = (0, 1, 3, 2)[piece]
                pe.wait_ge(S["sel_done"], UN * G + (4, 8, 8, 10)[piece])
                pr = prob[:, gg % 2]
                for h in range(GH):
                    unit, lo = ((h, 0), (4 + h, 0), (8 + h // 2, 256 * (h % 2)), (4 + h, 384))[k]
                    n = T - P * k
                    last = nc.tensor.matmul(ps_o[32 * h:32 * h + 32, P * k:], v_op[:, vpar, k, GH * gg + h, :],
                                            pr[:, unit, lo:lo + n], start=(piece == 0), stop=(piece == 3))
                if piece == 3:
                    last.then_inc(S["pv_in"], 1)

            def transpose_o(bp, opar, q):
                k = 4 * bp + q
                pe.wait_ge(S["o_done"], 4 * bp + 4)
                if q == 0:
                    if some(2 * bp):
                        pe.wait_ge(S["yT_done"], 2 * bp)
                elif q == 2:
                    pe.wait_ge(S["yT_done"], 2 * bp + 1)
                else:
                    pe.wait_ge(S["y_done"], k)
                for g in range(NG):
                    last = nc.tensor.transpose(ps_y[:, P * g:P * (g + 1)], o_t[:, opar, g, P * q:P * (q + 1)],
                                               ident[:])
                last.then_inc(S["ot_in"], 1)

            def transpose_y(bp, j):
                pe.wait_ge(S["y_done"], 4 * bp + 2 * j + 2)
                for t in range(2):
                    for c in range(2):
                        last = nc.tensor.transpose(ps_y[:, P * (2 * t + c):P * (2 * t + c + 1)],
                                                   y[:, t, P * c:P * (c + 1)], ident[:])
                last.then_inc(S["yT_in"], 1)

            def project_out(b, bp, j, tail):
                pe.wait_ge(S["yT_done"], 2 * bp + j + 1)
                if tail:
                    pe.wait_ge(S["x1_done"], 2 * bp + j)
                else:
                    pe.wait_ge(S["m_done"], 4 * b + 2 + j)
                for t in range(2):
                    for c in range(2):
                        last = nc.tensor.matmul(ps_m[:, 256 * t:256 * t + 256], y_t[:, t, c, :], wp[:, c, :],
                                                start=(c == 0), stop=(c == 1))
                last.then_inc(S["pr_in"], 1)

            def body(b, par, cur, prev, prev2, nxt, nxt2):
                for g in range(NG):
                    G = 4 * b + g
                    has1 = (cur or g < 1) and (prev or g >= 1)
                    has2 = (cur or g < 2) and (prev or g >= 2)
                    for s in range(UN):
                        if cur:
                            scores(b, G, g, s)
                        if s == MAXIMA and has1:
                            maxima(b, G, g)
                        if s >= LAG - UN and has1:
                            shifted(G - 1, (g - 1) % 4, s + UN - LAG)
                        elif s < LAG - UN and has2:
                            shifted(G - 2, (g - 2) % 4, s + 2 * UN - LAG)
                        if has2 and s in MIX:
                            mix(G - 2, (g - 2) % 4, par if g >= 2 else 1 - par, b if g >= 2 else b - 1,
                                MIX.index(s))
                        if nxt:
                            for c in range(2):
                                if (g, s) == XN_T[c]:
                                    transpose_xn(b + 1, c)
                            for i in range(4):
                                if (g, s) == QK[i]:
                                    project_qk(b + 1, i)
                            for j in range(2):
                                if (g, s) == V_PROJ[j]:
                                    project_v(b + 1, j)
                        if prev:
                            for q in range(NT):
                                if (g, s) == O_T[q]:
                                    transpose_o(b - 1, 1 - par, q)
                            for j in range(2):
                                if (g, s) == Y_T[j]:
                                    transpose_y(b - 1, j)
                                if (g, s) == PROJ[j]:
                                    project_out(b, b - 1, j, not cur)
                        if not cur and (g, s) == PREP_SUM:
                            pe.wait_ge(S["top_in"], 2)
                            for k in range(2):
                                for c in range(CC):
                                    last = nc.tensor.matmul(bank[0][:, E * k:E * (k + 1)], ones_f[:],
                                                            gs_t[:, CC * k + c], start=(c == 0), stop=(c == CC - 1))
                            last.then_inc(S["gsum"], 1)

            batches(pe, body)

            pe.wait_ge(S["lo_done"], 2 * NB)
            for stored in (*x1_stored, *xhl_stored):
                pe.wait_ge(stored, 16 * NB)
            def transpose_pair(n, par, p):
                buf = 2 * par + p // 2
                if p % 2 == 0:
                    pe.wait_ge(lrow_loaded[buf], 8 * n + (16 - 8 * par))
                if some(2 * n + p // 2):
                    pe.wait_ge(S[f"lxt_done{p % 2}"], 2 * n + p // 2)
                for t in range(2):
                    for c in range(2 * CC):
                        at = P * (2 * CC * t + c)
                        last = nc.tensor.transpose(ps_lx[p % 2][:, at:at + P],
                                                   lrow[:, buf, 2 * (p % 2) + t, P * c:P * (c + 1)], ident_h[:])
                last.then_inc(S["lxT_in"], 1)

            def logits(n, p):
                h = p % 2
                pe.wait_ge(S[f"lxt_done{h}"], 2 * n + (p // 2 + 1))
                for t in range(2):
                    last = products(ps_l[:, bass.ds((8 * n + (2 * p + t)) * E, E)],
                                    [((xtl[:, h, t, c, :], xtl[:, h, t, CC + c, :]),
                                      (gate_hl[:, 0, c, :], gate_hl[:, 1, c, :])) for c in range(CC)])
                last.then_inc(S["lg_in"], 1)

            def weights(w, off, k, n, size):
                if w is None:
                    return wsh[:, off + k * n:off + (k + 1) * n], wsh[:, off + size + k * n:off + size + (k + 1) * n]
                return (wbuf[:, bass.ds(w + (off + k * n), n)], wbuf[:, bass.ds(w + (off + size + k * n), n)])

            def transpose_rows(n, par, arrived, count):
                pe.wait_ge(arrived[par], 16 * count + 16)
                if some(n):
                    pe.wait_ge(S["xt_done"], n)
                for c in range(2 * CC):
                    last = nc.tensor.transpose(ps_x16[:, P * c:P * (c + 1)], xrow[:, par, P * c:P * (c + 1)],
                                               ident_h[:])
                last.then_inc(S["xT_in"], 1)

            def x_pair(par, c):
                return xt[:, par, c, :], xt[:, par, CC + c, :]

            def gate(n, par, w):
                pe.wait_ge(S["xt_done"], n + 1)
                if some(n):
                    pe.wait_ge(S["sg_done"], n)
                products(ps_g[:], [(x_pair(par, c), weights(w, WG, c, HID, CC * HID)) for c in range(CC)]
                         ).then_inc(S["g_in"], 1)

            def up(n, par, w):
                if some(n):
                    pe.wait_ge(S["h_done"], n)
                products(ps_u[:], [(x_pair(par, c), weights(w, WU, c, HID, CC * HID)) for c in range(CC)]
                         ).then_inc(S["u_in"], 1)

            def transpose_hidden(n):
                pe.wait_ge(S["h_done"], n + 1)
                if some(n):
                    pe.wait_ge(S["hl_done"], n)
                for k in range(HC):
                    last = nc.tensor.transpose(ps_h[:, P * k:P * (k + 1)], hb[:, P * k:P * (k + 1)], ident[:])
                last.then_inc(S["hT_in"], 1)

            def down(n, w):
                pe.wait_ge(S["hl_done"], n + 1)
                if some(n):
                    pe.wait_ge(S["y_out"], n)
                products(ps_z[:, 0:C], [((hth[:, k, :], htl[:, k, :]), weights(w, WD, k, C, HC * C))
                                        for k in range(HC)]).then_inc(S["yp_in"], 1)

            def shared(n, par, half, prev, with_logits):
                if prev:
                    transpose_hidden(n - 1)
                    if with_logits:
                        logits(n - 1, 3)
                if with_logits:
                    transpose_pair(n, par, 0)
                gate(n, par, None)
                if with_logits:
                    transpose_pair(n, par, 1)
                    logits(n, 0)
                up(n, par, None)
                if with_logits:
                    transpose_pair(n, par, 2)
                    logits(n, 1)
                if not isinstance(n, int) or n < TILES - 1:
                    transpose_rows(n + 1, 1 - par, row_loaded, half + par)
                if prev:
                    down(n - 1, None)
                if with_logits:
                    transpose_pair(n, par, 3)
                    logits(n, 2)
                if isinstance(n, int) and n == LOGITS_END:
                    logits(n - 1, 3)

            transpose_rows(0, 0, row_loaded, 0)
            pe.wait_ge(S["gprep"], 4)

            def beside(n):
                if n == RANKS_AT:
                    pe.wait_ge(S["sel_ready"], 1)
                    flat = sel[:].rearrange("p t e -> p (t e)")
                    nc.tensor.matmul(ps_r[0][:], before_b[:], flat, start=True, stop=True)
                    nc.tensor.matmul(ps_r[1][:], ones_b[:], flat, start=True, stop=True
                                     ).then_inc(S["ranks_in"], 1)

            shared_blocks(pe, shared, beside)
            transpose_hidden(N_SH - 1)
            down(N_SH - 1, None)
            pe.wait_ge(S["wlo_done"], 3 * E + 1)
            pe.wait_ge(S["blk_done"], 1)
            offset = [pe.alloc_register("offset_even"), pe.alloc_register("offset_odd")]
            offset_down = pe.alloc_register("offset_down")

            def at(register):
                return pe.snap(register, min_val=0, max_val=(E - 1) * SLOT)

            def routed(n, par, half, prev, nxt):
                if prev:
                    transpose_hidden(n - 1)
                begin = at(offset[par])
                gate(n, par, begin)
                up(n, par, begin)
                if prev:
                    pe.reg_mov(offset_down, offset[1 - par])
                if nxt:
                    pe.reg_load(offset[1 - par], blk_off[0:1, bass.ds(n - (N_SH - 1), 1)])
                    transpose_rows(n + 1, 1 - par, row_gathered, half + (par - N_SH // 2))
                if prev:
                    down(n - 1, at(offset_down))

            pe.reg_load(offset[0], blk_off[0:1, 0:1])
            transpose_rows(N_SH, 0, row_gathered, 0)
            routed_blocks(pe, routed)
            transpose_hidden(N_ALL - 1)
            down(N_ALL - 1, at(offset[(N_ALL - 1) % 2]))


def rope_table(heads, hd):
    theta = (1.0 / 10000.0 ** (np.arange(0, hd, 2, dtype=np.float32) / np.float32(hd))).astype(np.float32)
    ang = (np.arange(heads, dtype=np.float32)[:, None] * theta[None, :]).reshape(-1)
    k = np.stack([np.cos(ang), np.sin(ang)]).astype(np.float32)
    return np.concatenate([k * np.float32(hd ** -0.5), k], axis=1)


INPUTS = ["L0_attn_x", "L0_attn_W_attn", "L0_attn_b_attn", "L0_attn_W_proj", "L0_attn_b_proj",
          "L0_ffn_ln_scale", "L0_ffn_ln_bias", "L0_ffn_gate_w", "L0_ffn_Wg", "L0_ffn_Wu", "L0_ffn_Wd",
          "L0_ffn_sWg", "L0_ffn_sWu", "L0_ffn_sWd"]


def kernel(**inputs):
    import concourse.bacc as bacc
    from concourse.bass_utils import run_bass_kernel_spmd

    nc = bacc.Bacc("TRN2", target_bir_lowering=False, num_devices=1)
    shape = inputs["L0_attn_x"].shape
    arrays = {f"in_{name}": np.ascontiguousarray(inputs[name]) for name in INPUTS}
    arrays["in_L0_attn_x"] = arrays["in_L0_attn_x"].reshape(-1, shape[-1])
    gate = arrays["in_L0_ffn_gate_w"]
    arrays["in_L0_ffn_gate_w"] = np.ascontiguousarray(gate.reshape(gate.shape[0], -1, P).transpose(2, 1, 0))
    for name in ("in_L0_ffn_ln_scale", "in_L0_ffn_ln_bias"):
        arrays[name] = np.ascontiguousarray(arrays[name].reshape(-1, P).T)
    arrays["in_rope"] = rope_table(16, shape[-1] // 16)
    args = [nc.dram_tensor(n, a.shape, mybir.dt.from_np(a.dtype), kind="ExternalInput").ap()
            for n, a in arrays.items()]
    rows = arrays["in_L0_attn_x"].shape[0]
    out = nc.dram_tensor("out_x", (rows + P, shape[-1]), F32, kind="ExternalOutput").ap()
    build(nc, *args, out)
    r = run_bass_kernel_spmd(nc, [arrays], core_ids=[0])
    return r.results[0]["out_x"][:rows].reshape(shape)
```
